# Optimizing a Trainium2 kernel written in Bass

```python
import numpy as np
import jax
import jax.numpy as jnp

def _softmax(x, axis=-1):
    return jax.nn.softmax(x, axis=axis)

def _gelu(x):
    return jax.nn.gelu(x, approximate=True)

def _silu(x):
    return jax.nn.silu(x)

def _sigmoid(x):
    return jax.nn.sigmoid(x)

def _layernorm(x, axis=-1, eps=1e-05):
    m = jnp.mean(x, axis=axis, keepdims=True)
    v = jnp.var(x, axis=axis, keepdims=True)
    return (x - m) / jnp.sqrt(v + eps)

def _scatter_add(tgt, idx, src, axis=0):
    return tgt.at[idx].add(src)

def _segment_sum(src, seg, n):
    return jax.ops.segment_sum(src, seg, n)
kernel_name = 'mk_lm_tower_d1_tok_ids2048_r4_0bc050'

def setup_inputs(seed: int=0):
    np.random.seed(seed)
    _w = jnp.asarray

    def _rec_inputs():
        import jax
        import jax.numpy as jnp
        _rk = jax.random.key(seed)
        x = jax.random.randint(jax.random.fold_in(_rk, 1), (4, 512), 0, 512, jnp.int32)
        return x
    x = _rec_inputs()

    def _L0_tok_setup():
        import jax, jax.numpy as jnp
        import numpy as np
        B, S, D, DQK, L = (4, 512, 512, 128, 4)

        def _sinusoidal_pe(seq_len, d_model):
            pos = jnp.arange(seq_len, dtype=jnp.float32)[:, None]
            half = jnp.arange(0, d_model, 2, dtype=jnp.float32)
            div = jnp.exp(-(jnp.log(jnp.float32(10000.0)) / d_model) * half)
            pe = jnp.zeros((seq_len, d_model), jnp.float32)
            pe = pe.at[:, 0::2].set(jnp.sin(pos * div))
            pe = pe.at[:, 1::2].set(jnp.cos(pos * div))
            return pe
        key = jax.random.key(seed)
        k1, k2, k3 = jax.random.split(key, 3)
        token_ids = jax.random.randint(k1, (B, S), 0, D)
        Wq = jax.random.normal(k2, (L, D, DQK), jnp.float32) * 0.02
        Wk = jax.random.normal(k3, (L, D, DQK), jnp.float32) * 0.02
        return {'token_ids': token_ids, 'Wq': Wq, 'Wk': Wk}
    _L0_tok_all = _L0_tok_setup()
    _L0_tok_in = {k: v for k, v in _L0_tok_all.items() if k in ('Wq', 'Wk')}
    del _L0_tok_all

    def _L0_attn_setup():
        import jax, jax.numpy as jnp
        import numpy as np
        B, L, E = (2, 512, 512)
        NUM_HEADS = 16
        NUM_KV_HEADS = 2
        HEAD_DIM = E // NUM_HEADS
        THETA = 10000.0

        def apply_rope(x, theta=THETA):
            D = x.shape[-1]
            half = D // 2
            inv_freq = theta ** (-jnp.arange(half, dtype=jnp.float32) / half)
            pos = jnp.arange(x.shape[1], dtype=jnp.float32)
            ang = pos[:, None] * inv_freq[None, :]
            cos = jnp.cos(ang)[None, :, None, :].astype(x.dtype)
            sin = jnp.sin(ang)[None, :, None, :].astype(x.dtype)
            x1, x2 = (x[..., :half], x[..., half:])
            return jnp.concatenate([x1 * cos - x2 * sin, x2 * cos + x1 * sin], axis=-1)
        key = jax.random.key(seed)
        ks = jax.random.split(key, 8)
        s = 0.02
        return {'x': jax.random.normal(ks[0], (B, L, E), dtype=jnp.float32), 'wq': jax.random.normal(ks[1], (NUM_HEADS * HEAD_DIM, E), dtype=jnp.float32) * s, 'wk': jax.random.normal(ks[2], (NUM_KV_HEADS * HEAD_DIM, E), dtype=jnp.float32) * s, 'wv': jax.random.normal(ks[3], (NUM_KV_HEADS * HEAD_DIM, E), dtype=jnp.float32) * s, 'wo': jax.random.normal(ks[4], (E, NUM_HEADS * HEAD_DIM), dtype=jnp.float32) * s, 'bq': jax.random.normal(ks[5], (NUM_HEADS * HEAD_DIM,), dtype=jnp.float32) * s, 'bk': jax.random.normal(ks[6], (NUM_KV_HEADS * HEAD_DIM,), dtype=jnp.float32) * s, 'bv': jax.random.normal(ks[7], (NUM_KV_HEADS * HEAD_DIM,), dtype=jnp.float32) * s}
    _L0_attn_all = _L0_attn_setup()
    _L0_attn_in = {k: v for k, v in _L0_attn_all.items() if k in ('wq', 'wk', 'wv', 'wo', 'bq', 'bk', 'bv')}
    del _L0_attn_all

    def _L0_ffn_setup():
        import jax, jax.numpy as jnp
        import numpy as np
        D = 512
        H = 16
        KV = 4
        DH = 128
        RD = 64
        E = 8
        TOPK = 2
        I = 256
        EPS = 1e-06
        THETA = 1000000.0

        def rmsnorm(h, w, eps=EPS):
            dt = h.dtype
            h32 = h.astype(jnp.float32)
            var = jnp.mean(h32 * h32, axis=-1, keepdims=True)
            return (w * (h32 * jax.lax.rsqrt(var + eps))).astype(dt)

        def rotate_half(t):
            half = t.shape[-1] // 2
            return jnp.concatenate([-t[..., half:], t[..., :half]], axis=-1)
        key = jax.random.key(seed)
        ks = jax.random.split(key, 16)
        s = lambda k, shape, sc: jax.random.normal(k, shape, dtype=jnp.float32) * sc
        B, S = (1, 512)
        return {'x': s(ks[0], (B, S, D), 1.0), 'ln1_w': jnp.ones((D,), jnp.float32), 'ln2_w': jnp.ones((D,), jnp.float32), 'wq': s(ks[1], (D, H * DH), 0.02), 'wk': s(ks[2], (D, KV * DH), 0.02), 'wv': s(ks[3], (D, KV * DH), 0.02), 'wo': s(ks[4], (H * DH, D), 0.02), 'qnorm_w': jnp.ones((H * DH,), jnp.float32), 'knorm_w': jnp.ones((KV * DH,), jnp.float32), 'router_w': s(ks[5], (D, E), 0.02), 'router_bias': s(ks[6], (E,), 0.1), 'wg': s(ks[7], (E, D, I), 0.02), 'wu': s(ks[8], (E, D, I), 0.02), 'wd': s(ks[9], (E, I, D), 0.02)}
    _L0_ffn_all = _L0_ffn_setup()
    _L0_ffn_in = {k: v for k, v in _L0_ffn_all.items() if k in ('ln1_w', 'ln2_w', 'wq', 'wk', 'wv', 'wo', 'qnorm_w', 'knorm_w', 'router_w', 'router_bias', 'wg', 'wu', 'wd')}
    del _L0_ffn_all
    return {'x': x, 'L0_tok_Wq': _L0_tok_in['Wq'], 'L0_tok_Wk': _L0_tok_in['Wk'], 'L0_attn_wq': _L0_attn_in['wq'], 'L0_attn_wk': _L0_attn_in['wk'], 'L0_attn_wv': _L0_attn_in['wv'], 'L0_attn_wo': _L0_attn_in['wo'], 'L0_attn_bq': _L0_attn_in['bq'], 'L0_attn_bk': _L0_attn_in['bk'], 'L0_attn_bv': _L0_attn_in['bv'], 'L0_ffn_ln1_w': _L0_ffn_in['ln1_w'], 'L0_ffn_ln2_w': _L0_ffn_in['ln2_w'], 'L0_ffn_wq': _L0_ffn_in['wq'], 'L0_ffn_wk': _L0_ffn_in['wk'], 'L0_ffn_wv': _L0_ffn_in['wv'], 'L0_ffn_wo': _L0_ffn_in['wo'], 'L0_ffn_qnorm_w': _L0_ffn_in['qnorm_w'], 'L0_ffn_knorm_w': _L0_ffn_in['knorm_w'], 'L0_ffn_router_w': _L0_ffn_in['router_w'], 'L0_ffn_router_bias': _L0_ffn_in['router_bias'], 'L0_ffn_wg': _L0_ffn_in['wg'], 'L0_ffn_wu': _L0_ffn_in['wu'], 'L0_ffn_wd': _L0_ffn_in['wd']}

def reference(x, L0_tok_Wq, L0_tok_Wk, L0_attn_wq, L0_attn_wk, L0_attn_wv, L0_attn_wo, L0_attn_bq, L0_attn_bk, L0_attn_bv, L0_ffn_ln1_w, L0_ffn_ln2_w, L0_ffn_wq, L0_ffn_wk, L0_ffn_wv, L0_ffn_wo, L0_ffn_qnorm_w, L0_ffn_knorm_w, L0_ffn_router_w, L0_ffn_router_bias, L0_ffn_wg, L0_ffn_wu, L0_ffn_wd):
    import jax
    import jax.numpy as jnp

    def _L0_tok_ref(token_ids, Wq, Wk):
        import jax, jax.numpy as jnp
        import numpy as np
        B, S, D, DQK, L = (4, 512, 512, 128, 4)

        def _sinusoidal_pe(seq_len, d_model):
            pos = jnp.arange(seq_len, dtype=jnp.float32)[:, None]
            half = jnp.arange(0, d_model, 2, dtype=jnp.float32)
            div = jnp.exp(-(jnp.log(jnp.float32(10000.0)) / d_model) * half)
            pe = jnp.zeros((seq_len, d_model), jnp.float32)
            pe = pe.at[:, 0::2].set(jnp.sin(pos * div))
            pe = pe.at[:, 1::2].set(jnp.cos(pos * div))
            return pe
        d_model = Wq.shape[1]
        d_qk = Wq.shape[2]
        seq_len = token_ids.shape[1]
        enc = jax.nn.one_hot(token_ids, d_model, dtype=jnp.float32)
        enc = enc + _sinusoidal_pe(seq_len, d_model)[None, :, :]
        causal_mask = jnp.triu(jnp.ones((seq_len, seq_len), bool), 1)
        scale = 1.0 / jnp.sqrt(jnp.float32(d_qk))

        def layer(enc, ws):
            wq, wk = ws
            q = enc @ wq
            k = enc @ wk
            sims = jnp.einsum('bqd,bkd->bqk', q, k) * scale
            sims = jnp.where(causal_mask[None, :, :], jnp.float32(-1000000000.0), sims)
            attn = jax.nn.softmax(sims, axis=-1)
            enc = jnp.einsum('bqk,bkd->bqd', attn, enc)
            return (enc, None)
        enc, _ = jax.lax.scan(layer, enc, (Wq, Wk))
        return enc

    def _L0_attn_ref(x, wq, wk, wv, wo, bq, bk, bv):
        import jax, jax.numpy as jnp
        import numpy as np
        B, L, E = (2, 512, 512)
        NUM_HEADS = 16
        NUM_KV_HEADS = 2
        HEAD_DIM = E // NUM_HEADS
        THETA = 10000.0

        def apply_rope(x, theta=THETA):
            D = x.shape[-1]
            half = D // 2
            inv_freq = theta ** (-jnp.arange(half, dtype=jnp.float32) / half)
            pos = jnp.arange(x.shape[1], dtype=jnp.float32)
            ang = pos[:, None] * inv_freq[None, :]
            cos = jnp.cos(ang)[None, :, None, :].astype(x.dtype)
            sin = jnp.sin(ang)[None, :, None, :].astype(x.dtype)
            x1, x2 = (x[..., :half], x[..., half:])
            return jnp.concatenate([x1 * cos - x2 * sin, x2 * cos + x1 * sin], axis=-1)
        b, l, _ = x.shape
        Hq, Hkv, Dh = (NUM_HEADS, NUM_KV_HEADS, HEAD_DIM)
        G = Hq // Hkv
        scale = 1.0 / Dh ** 0.5
        q = (x @ wq.T + bq).reshape(b, l, Hq, Dh)
        k = (x @ wk.T + bk).reshape(b, l, Hkv, Dh)
        v = (x @ wv.T + bv).reshape(b, l, Hkv, Dh)
        q = apply_rope(q)
        k = apply_rope(k)
        q = q.transpose(0, 2, 1, 3).reshape(b, Hkv, G, l, Dh).astype(jnp.float32)
        k = k.transpose(0, 2, 1, 3).astype(jnp.float32)
        v = v.transpose(0, 2, 1, 3).astype(jnp.float32)
        scores = jnp.einsum('bhgqd,bhkd->bhgqk', q, k) * scale
        causal = jnp.tril(jnp.ones((l, l), dtype=bool))
        scores = jnp.where(causal[None, None, None, :, :], scores, -jnp.inf)
        attn = jax.nn.softmax(scores, axis=-1)
        out = jnp.einsum('bhgqk,bhkd->bhgqd', attn, v)
        out = out.reshape(b, Hq, l, Dh).transpose(0, 2, 1, 3).reshape(b, l, Hq * Dh)
        out = out.astype(x.dtype)
        return out @ wo.T

    def _L0_ffn_ref(x, ln1_w, ln2_w, wq, wk, wv, wo, qnorm_w, knorm_w, router_w, router_bias, wg, wu, wd):
        import jax, jax.numpy as jnp
        import numpy as np
        D = 512
        H = 16
        KV = 4
        DH = 128
        RD = 64
        E = 8
        TOPK = 2
        I = 256
        EPS = 1e-06
        THETA = 1000000.0

        def rmsnorm(h, w, eps=EPS):
            dt = h.dtype
            h32 = h.astype(jnp.float32)
            var = jnp.mean(h32 * h32, axis=-1, keepdims=True)
            return (w * (h32 * jax.lax.rsqrt(var + eps))).astype(dt)

        def rotate_half(t):
            half = t.shape[-1] // 2
            return jnp.concatenate([-t[..., half:], t[..., :half]], axis=-1)
        B, S, _ = x.shape
        res = x
        h = rmsnorm(x, ln1_w)
        q = h @ wq
        k = h @ wk
        v = h @ wv
        q = rmsnorm(q, qnorm_w)
        k = rmsnorm(k, knorm_w)
        q = q.reshape(B, S, H, DH).transpose(0, 2, 1, 3)
        k = k.reshape(B, S, KV, DH).transpose(0, 2, 1, 3)
        v = v.reshape(B, S, KV, DH).transpose(0, 2, 1, 3)
        pos = jnp.arange(S, dtype=jnp.float32)
        inv_freq = 1.0 / THETA ** (jnp.arange(0, RD, 2, dtype=jnp.float32) / RD)
        ang = pos[:, None] * inv_freq[None, :]
        emb = jnp.concatenate([ang, ang], axis=-1)
        cos, sin = (jnp.cos(emb), jnp.sin(emb))

        def rope(t):
            rot, pas = (t[..., :RD], t[..., RD:])
            rot = rot * cos + rotate_half(rot) * sin
            return jnp.concatenate([rot, pas], axis=-1)
        q, k = (rope(q), rope(k))
        rep = H // KV
        k = jnp.repeat(k, rep, axis=1)
        v = jnp.repeat(v, rep, axis=1)
        scores = jnp.einsum('bhqd,bhkd->bhqk', q, k) / np.sqrt(DH)
        causal = jnp.tril(jnp.ones((S, S), dtype=bool))
        scores = jnp.where(causal, scores, jnp.finfo(jnp.float32).min)
        attn = jax.nn.softmax(scores.astype(jnp.float32), axis=-1).astype(q.dtype)
        o = jnp.einsum('bhqk,bhkd->bhqd', attn, v)
        o = o.transpose(0, 2, 1, 3).reshape(B, S, H * DH) @ wo
        x1 = res + o
        h2 = rmsnorm(x1, ln2_w)
        t = h2.reshape(-1, D)
        T = t.shape[0]
        logits = t.astype(jnp.float32) @ router_w
        sig = jax.nn.sigmoid(logits)
        _, topi = jax.lax.top_k(sig + router_bias, TOPK)
        aff = jnp.take_along_axis(sig, topi, axis=-1)
        aff = aff / jnp.sum(aff, axis=-1, keepdims=True)
        combine = jnp.zeros((T, E), jnp.float32).at[jnp.arange(T)[:, None], topi].set(aff)
        gate = jnp.einsum('td,edi->tei', t, wg)
        up = jnp.einsum('td,edi->tei', t, wu)
        act = jax.nn.silu(gate) * up
        moe = jnp.einsum('te,tei,eid->td', combine.astype(t.dtype), act, wd)
        return x1 + moe.reshape(B, S, D)
    h = _L0_tok_ref(x, L0_tok_Wq, L0_tok_Wk)
    h = h + _L0_attn_ref(_layernorm(h, axis=-1), L0_attn_wq, L0_attn_wk, L0_attn_wv, L0_attn_wo, L0_attn_bq, L0_attn_bk, L0_attn_bv)
    h = h + _L0_ffn_ref(_layernorm(h, axis=-1), L0_ffn_ln1_w, L0_ffn_ln2_w, L0_ffn_wq, L0_ffn_wk, L0_ffn_wv, L0_ffn_wo, L0_ffn_qnorm_w, L0_ffn_knorm_w, L0_ffn_router_w, L0_ffn_router_bias, L0_ffn_wg, L0_ffn_wu, L0_ffn_wd)
    return h

_drawn_inputs = setup_inputs


def setup_inputs(seed=0):
    import zlib

    import numpy as np

    out = dict(_drawn_inputs(seed))
    spreads = {'L0_ffn_ln1_w': (1.0, 0.2),
     'L0_ffn_ln2_w': (1.0, 0.6),
     'L0_ffn_qnorm_w': (1.0, 0.6),
     'L0_ffn_knorm_w': (1.0, 0.6)}
    factors = {'L0_tok_Wq': 8.0,
     'L0_tok_Wk': 7.999,
     'L0_attn_wq': 8.0,
     'L0_attn_wk': 8.0,
     'L0_attn_bq': 8.0,
     'L0_attn_bk': 8.0,
     'L0_attn_bv': 2.767,
     'L0_ffn_wq': 7.813,
     'L0_ffn_wk': 7.623,
     'L0_ffn_router_w': 4.891,
     'L0_ffn_router_bias': 6.107,
     'L0_ffn_wg': 3.406,
     'L0_ffn_wu': 3.682,
     'L0_ffn_wd': 3.827}
    for name, (base, spread) in spreads.items():
        noise = np.random.default_rng([zlib.crc32(name.encode()), seed]).standard_normal(out[name].shape)
        drawn = base * np.exp(spread * noise) if base else spread * noise
        out[name] = jnp.asarray(drawn.astype(out[name].dtype))
    for name, factor in factors.items():
        out[name] = (out[name] * factor).astype(out[name].dtype)
    return out
```

```python
from contextlib import ExitStack

import concourse.bass as bass
import numpy as np
from concourse import mybir

F32 = mybir.dt.float32
F32R = mybir.dt.float32r
I32 = mybir.dt.int32
ALU = mybir.AluOpType
ACT = mybir.ActivationFunctionType
AX_X = mybir.AxisListType.X

P = 128
BATCH, SEQ, D = 4, 512, 512
QT = SEQ // P
DT = D // P
TILES = BATCH * QT
MASKED = -1e30

TOK_LAYERS, TOK_DQK = 4, 128


class Stage:

    def __init__(self, nc, ctx, stage):
        self.nc, self.ctx, self.stage = nc, ctx, stage

    def sb(self, name, shape, dt=F32):
        return self.ctx.enter_context(self.nc.sbuf_tensor(f"{self.stage}_{name}", shape, dt))

    def bank(self, name):
        return self.ctx.enter_context(self.nc.psum_tensor(f"{self.stage}_{name}", [P, 512], F32))

    def sem(self, name):
        return self.ctx.enter_context(self.nc.semaphore(f"{self.stage}_{name}"))


def product(pe, out, a, b, start, stop):
    (a_h, a_l), (b_h, b_l) = a, b
    pe.matmul(out, a_l, b_h, start=start, stop=False)
    pe.matmul(out, a_h, b_l, start=False, stop=False)
    return pe.matmul(out, a_h, b_h, start=False, stop=stop)


def token_stage(nc, H, const, tok_w, ids_dram, pe_dram, iota_dram):
    SCALE = float(TOK_DQK) ** -0.5
    U = BATCH * QT
    X = BATCH * (DT + 2)
    ident, mask, const_ready = const

    def unit(u):
        return u // QT, QT - 1 - u % QT

    with ExitStack() as ctx:
        m = Stage(nc, ctx, "tok")
        E_h = m.sb("E_h", [P, TILES, D], F32R)
        E_l = m.sb("E_l", [P, TILES, D], F32R)
        ET_h = [m.sb(f"ET_h{i}", [P, DT, SEQ], F32R) for i in range(2)]
        ET_l = [m.sb(f"ET_l{i}", [P, DT, SEQ], F32R) for i in range(2)]
        QK_h = [m.sb(f"QK_h{i}", [P, 2, SEQ], F32R) for i in range(2)]
        QK_l = [m.sb(f"QK_l{i}", [P, 2, SEQ], F32R) for i in range(2)]
        W = m.sb("W", [P, TOK_LAYERS, DT, 2 * TOK_DQK])
        W_h = m.sb("W_h", [P, TOK_LAYERS, DT, 2 * TOK_DQK])
        W_l = W
        Wn_h = m.sb("Wn_h", [P, DT, 2 * TOK_DQK], F32R)
        Wn_l = m.sb("Wn_l", [P, DT, 2 * TOK_DQK], F32R)
        work = m.sb("work", [P, 4, SEQ])
        Sm = [work[:, 0], work[:, 1]]
        Pr = [work[:, 2], work[:, 3]]
        pos = work[:]
        PT_h = [m.sb(f"PT_h{i}", [P, SEQ], F32R) for i in range(2)]
        PT_l = [m.sb(f"PT_l{i}", [P, SEQ], F32R) for i in range(2)]
        least = m.sb("least", [P, 4])
        den = m.sb("den", [P, 4])
        rden = m.sb("rden", [P, 4])
        ids_i = m.sb("ids_i", [P, TILES], I32)
        ids_f = m.sb("ids_f", [P, TILES])
        iota = m.sb("iota", [P, D])

        S_bank = [m.bank(f"S_bank{i}") for i in range(2)]
        T_bank = [m.bank(f"T_bank{i}") for i in range(2)]
        O_bank = [m.bank(f"O_bank{i}") for i in range(2)]
        X_bank = [m.bank(f"X_bank{i}") for i in range(2)]

        in_ids, in_tabs = m.sem("in_ids"), m.sem("in_tabs")
        w_in, w_hi, w_lo, w_now = m.sem("w_in"), m.sem("w_hi"), m.sem("w_lo"), m.sem("w_now")
        ids_ok = m.sem("ids_ok")
        enc, enc_hi, enc_lo = m.sem("enc"), m.sem("enc_hi"), m.sem("enc_lo")
        x_done, x_hi, x_lo = m.sem("x_done"), m.sem("x_hi"), m.sem("x_lo")
        s_done, s_masked, p_done, rden_ok = m.sem("s_done"), m.sem("s_masked"), m.sem("p_done"), m.sem("rden_ok")
        pt_done, pt_hi, pt_lo, pv_done = m.sem("pt_done"), m.sem("pt_hi"), m.sem("pt_lo"), m.sem("pv_done")

        waited = m.sem("waited")
        block = ctx.enter_context(nc.Block())

        SLOTS = U + 3

        def older(n):
            return max(n - 1, 0)

        def turned_in(s):
            return s // QT + 1 if s % QT == 1 and s // QT + 1 < BATCH else None

        def projected_in(s):
            return s // QT + 1 if s % QT == 3 and s // QT + 1 < BATCH else None

        @block.sync
        def _(sp):
            sp.dma_start(ids_i[:], ids_dram).then_inc(in_ids, 16)
            sp.dma_start(iota[:], iota_dram).then_inc(in_tabs, 16)
            sp.dma_start(pos, pe_dram.rearrange("(j p) d -> p j d", p=P)).then_inc(in_tabs, 16)
            sp.dma_start(W[:], tok_w.rearrange("l (t p) n -> p l t n", p=P)).then_inc(w_in, 16)

        @block.gpsimd
        def _(pool):
            pool.wait_ge(w_in, 16)
            pool.tensor_copy(W_h[:].bitcast(F32R), W[:]).then_inc(w_hi, 1)
            pool.wait_ge(w_hi, 1)
            pool.tensor_tensor(W_l[:], W[:], W_h[:], ALU.subtract).then_inc(w_lo, 1)
            for t in range(TILES):
                pool.wait_ge(enc_hi, t + 1)
                pool.tensor_tensor(E_l[:, t], H[:, t], E_h[:, t].bitcast(F32), ALU.subtract).then_inc(enc_lo, 1)
            pool.wait_ge(w_lo, 1)
            with pool.Fori(0, TOK_LAYERS) as l:
                pool.wait_ge(x_done, l * X)
                pool.tensor_copy(Wn_h[:], W_h[:, bass.ds(l, 1)]).then_inc(w_now, 1)
                pool.tensor_copy(Wn_l[:], W_l[:, bass.ds(l, 1)]).then_inc(w_now, 1)
                for u in range(U):
                    b, q = unit(u)
                    t = b * QT + q
                    pool.wait_ge(enc_hi, l * U + TILES + u + 1)
                    pool.tensor_tensor(E_l[:, t], H[:, t], E_h[:, t].bitcast(F32), ALU.subtract).then_inc(enc_lo, 1)

        @block.tensor
        def _(pe):
            pe.wait_ge(const_ready, 32)

            def transposes(l, b):
                pe.wait_ge(enc, l * U + QT * (b + 1))
                for t in range(DT):
                    x = b * (DT + 2) + t
                    pe.wait_ge(x_lo, l * X + older(x))
                    for j in range(QT):
                        mm = pe.transpose(X_bank[x % 2][:, bass.ts(j, P)], H[:, b * QT + j, bass.ts(t, P)], ident[:])
                    mm.then_inc(x_done, 1)

            def projections(l, b):
                if b == 0:
                    pe.wait_ge(w_now, l * 2 + 2)
                for r in range(2):
                    x = b * (DT + 2) + DT + r
                    pe.wait_ge(x_lo, l * X + b * (DT + 2) + DT)
                    for t in range(DT):
                        c = bass.ts(r, TOK_DQK)
                        mm = product(pe, X_bank[x % 2][:], (Wn_h[:, t, c], Wn_l[:, t, c]),
                                     (ET_h[b % 2][:, t], ET_l[b % 2][:, t]), t == 0, t == DT - 1)
                    mm.then_inc(x_done, 1)

            def score(l, u):
                b, q = unit(u)
                n = P * (q + 1)
                pe.wait_ge(x_lo, l * X + (b + 1) * (DT + 2))
                pe.wait_ge(s_masked, l * U + older(u))
                product(pe, S_bank[u % 2][:, 0:n], (QK_h[b % 2][:, 0, bass.ts(q, P)], QK_l[b % 2][:, 0, bass.ts(q, P)]),
                        (QK_h[b % 2][:, 1, 0:n], QK_l[b % 2][:, 1, 0:n]), True, True).then_inc(s_done, 1)

            def turn(l, u):
                _, q = unit(u)
                pe.wait_ge(p_done, l * U + u + 1)
                pe.wait_ge(pt_lo, l * U + older(u))
                for k in range(q + 1):
                    mm = pe.transpose(T_bank[u % 2][:, bass.ts(k, P)], Pr[u % 2][:, bass.ts(k, P)], ident[:])
                mm.then_inc(pt_done, 1)

            def apply(l, u):
                b, q = unit(u)
                pe.wait_ge(pt_lo, l * U + u + 1)
                pe.wait_ge(enc_lo, l * U + QT * (b + 1))
                pe.wait_ge(enc, l * U + TILES + older(u))
                for k in range(q + 1):
                    mm = product(pe, O_bank[u % 2][:], (PT_h[u % 2][:, bass.ts(k, P)], PT_l[u % 2][:, bass.ts(k, P)]),
                                 (E_h[:, b * QT + k], E_l[:, b * QT + k]), k == 0, k == q)
                mm.then_inc(pv_done, 1)

            with pe.Fori(0, TOK_LAYERS) as l:
                transposes(l, 0)
                projections(l, 0)
                for s in range(SLOTS):
                    if s < U:
                        score(l, s)
                    if 0 <= s - 2 < U:
                        turn(l, s - 2)
                    if turned_in(s) is not None:
                        transposes(l, turned_in(s))
                    if 0 <= s - 3 < U:
                        apply(l, s - 3)
                    if projected_in(s) is not None:
                        projections(l, projected_in(s))

        @block.scalar
        def _(act):
            for t in range(TILES):
                act.wait_ge(enc, t + 1)
                act.copy(E_h[:, t], H[:, t]).then_inc(enc_hi, 1)

            def take(l, x):
                b, r = x // (DT + 2), x % (DT + 2)
                to = ET_h[b % 2][:, r] if r < DT else QK_h[b % 2][:, r - DT]
                act.wait_ge(x_done, l * X + x + 1)
                act.copy(to, X_bank[x % 2][:]).then_inc(x_hi, 1)

            def exps(l, u):
                _, q = unit(u)
                n = P * (q + 1)
                act.wait_ge(pt_done, l * U + older(u))
                act.wait_ge(s_masked, l * U + u + 1)
                act.activation(Pr[u % 2][:, 0:n], Sm[u % 2][:, 0:n], ACT.Exp, bias=least[:, u % 4:u % 4 + 1], scale=-1.0,
                               accum_out=den[:, u % 4:u % 4 + 1]).then_inc(p_done, 1)

            def turned(l, u):
                _, q = unit(u)
                n = P * (q + 1)
                act.wait_ge(pt_done, l * U + u + 1)
                act.wait_ge(pv_done, l * U + older(u))
                act.copy(PT_h[u % 2][:, 0:n], T_bank[u % 2][:, 0:n]).then_inc(pt_hi, 1)

            def encoded(l, u):
                b, q = unit(u)
                act.wait_ge(enc, l * U + TILES + u + 1)
                act.copy(E_h[:, b * QT + q], H[:, b * QT + q]).then_inc(enc_hi, 1)

            with act.Fori(0, TOK_LAYERS) as l:
                for x in range(DT + 2):
                    take(l, x)
                for s in range(SLOTS):
                    if s < U:
                        exps(l, s)
                    if 0 <= s - 2 < U:
                        turned(l, s - 2)
                    if turned_in(s) is not None:
                        for t in range(DT):
                            take(l, turned_in(s) * (DT + 2) + t)
                    if 0 <= s - 3 < U:
                        encoded(l, s - 3)
                    if projected_in(s) is not None:
                        for r in range(2):
                            take(l, projected_in(s) * (DT + 2) + DT + r)

        @block.vector
        def _(dve):
            dve.wait_ge(const_ready, 32)
            dve.wait_ge(in_ids, 16)
            dve.tensor_copy(ids_f[:], ids_i[:]).then_inc(ids_ok, 1)
            dve.wait_ge(ids_ok, 1)
            dve.wait_ge(in_tabs, 32)
            for t in range(TILES):
                dve.scalar_tensor_tensor(out=H[:, t], in0=iota[:], scalar=ids_f[:, t:t + 1], in1=pos[:, t % QT],
                                         op0=ALU.is_equal, op1=ALU.add).then_inc(enc, 1)

            def take(l, x):
                b, r = x // (DT + 2), x % (DT + 2)
                h, lo = ((ET_h[b % 2][:, r], ET_l[b % 2][:, r]) if r < DT
                         else (QK_h[b % 2][:, r - DT], QK_l[b % 2][:, r - DT]))
                dve.wait_ge(x_hi, l * X + x + 1)
                dve.tensor_tensor(lo, X_bank[x % 2][:], h.bitcast(F32), ALU.subtract).then_inc(x_lo, 1)

            def mask_scores(l, u):
                _, q = unit(u)
                n = P * (q + 1)
                dve.wait_ge(s_done, l * U + u + 1)
                dve.wait_ge(p_done, l * U + older(u))
                dve.sem_inc(waited, 1)
                dve.tensor_tensor_reduce(out=Sm[u % 2][:, 0:n], in0=S_bank[u % 2][:, 0:n], in1=mask[:, SEQ - n:SEQ],
                                         scale=-SCALE, scalar=-MASKED, op0=ALU.add, op1=ALU.min,
                                         accum_out=least[:, u % 4:u % 4 + 1]).then_inc(s_masked, 1)

            def turned(l, u):
                _, q = unit(u)
                n = P * (q + 1)
                dve.wait_ge(p_done, l * U + u + 1)
                dve.reciprocal(rden[:, u % 4:u % 4 + 1], den[:, u % 4:u % 4 + 1]).then_inc(rden_ok, 1)
                dve.wait_ge(pt_hi, l * U + u + 1)
                dve.tensor_tensor(PT_l[u % 2][:, 0:n], T_bank[u % 2][:, 0:n], PT_h[u % 2][:, 0:n].bitcast(F32),
                                  ALU.subtract).then_inc(pt_lo, 1)

            def encoded(l, u):
                b, q = unit(u)
                dve.wait_ge(rden_ok, l * U + u + 1)
                dve.wait_ge(pv_done, l * U + u + 1)
                dve.tensor_scalar(H[:, b * QT + q], O_bank[u % 2][:], rden[:, u % 4:u % 4 + 1], None,
                                  ALU.mult).then_inc(enc, 1)

            with dve.Fori(0, TOK_LAYERS) as l:
                for x in range(DT + 2):
                    take(l, x)
                for s in range(SLOTS):
                    if s < U:
                        mask_scores(l, s)
                    if 0 <= s - 2 < U:
                        turned(l, s - 2)
                    if turned_in(s) is not None:
                        for t in range(DT):
                            take(l, turned_in(s) * (DT + 2) + t)
                    if 0 <= s - 3 < U:
                        encoded(l, s - 3)
                    if projected_in(s) is not None:
                        for r in range(2):
                            take(l, projected_in(s) * (DT + 2) + DT + r)


def attn_project(nc, H, const, QKV, w_dram, b_dram, cos_dram, sin_dram):
    HQ, HKV, DH = 16, 2, 32
    ROT = (HQ + HKV) * DH
    N = ROT + HKV * DH
    NQ = HQ * DH
    EPS = 1e-5
    ident, _, const_ready = const

    with ExitStack() as ctx:
        m = Stage(nc, ctx, "ap")
        W = m.sb("W", [P, DT, N])
        W_h = m.sb("W_h", [P, DT, N], F32R)
        W_l = m.sb("W_l", [P, DT, N], F32R)
        bias = m.sb("bias", [P, N])
        cos = m.sb("cos", [P, QT, DH])
        sin = m.sb("sin", [P, QT, DH])
        XN = [m.sb(f"XN{i}", [P, D]) for i in range(2)]
        XT_h = [m.sb(f"XT_h{i}", [P, D], F32R) for i in range(2)]
        XT_l = [m.sb(f"XT_l{i}", [P, D], F32R) for i in range(2)]
        raw = [m.sb(f"raw{i}", [P, ROT]) for i in range(2)]
        rc = m.sb("rc", [P, ROT])
        rs = [m.sb(f"rs{i}", [P, ROT]) for i in range(2)]
        stat = m.sb("stat", [P, 6])
        mv = m.sb("mv", [P, 2])
        std = m.sb("std", [P, 1])
        rstd = m.sb("rstd", [P, 1])
        eps = m.sb("eps", [P, 1])
        X_bank = [m.bank(f"X_bank{i}") for i in range(2)]
        Q_bank = [m.bank(f"Q_bank{i}") for i in range(2)]
        KV_bank = [m.bank(f"KV_bank{i}") for i in range(2)]

        w_in, tabs_in, w_hi, w_lo = m.sem("w_in"), m.sem("tabs_in"), m.sem("w_hi"), m.sem("w_lo")
        eps_ok, ln, xt_done, xt_hi, xt_lo = m.sem("eps_ok"), m.sem("ln"), m.sem("xt_done"), m.sem("xt_hi"), m.sem("xt_lo")
        q_done, kv_done, biased = m.sem("q_done"), m.sem("kv_done"), m.sem("biased")
        std_ok, turned, cosed, roped = m.sem("std_ok"), m.sem("turned"), m.sem("cosed"), m.sem("roped")
        waited = m.sem("waited")
        block = ctx.enter_context(nc.Block())

        def older(n):
            return max(n - 1, 0)

        @block.sync
        def _(sp):
            sp.dma_start(W[:], w_dram.rearrange("(t p) n -> p t n", p=P)).then_inc(w_in, 16)
            sp.dma_start(bias[:], b_dram.partition_broadcast(P)).then_inc(tabs_in, 16)
            sp.dma_start(cos[:], cos_dram.rearrange("(j p) d -> p j d", p=P)).then_inc(tabs_in, 16)
            sp.dma_start(sin[:], sin_dram.rearrange("(j p) d -> p j d", p=P)).then_inc(tabs_in, 16)

        @block.gpsimd
        def _(pool):
            pool.wait_ge(w_in, 16)
            pool.wait_ge(w_hi, 1)
            pool.tensor_tensor(W_l[:], W[:], W_h[:].bitcast(F32), ALU.subtract).then_inc(w_lo, 1)
            pool.wait_ge(tabs_in, 48)

            def turn(b, j):
                x = raw[j % 2][:].rearrange("p (h s c) -> p h s c", s=2, c=DH // 2)
                o = rs[j % 2][:].rearrange("p (h s c) -> p h s c", s=2, c=DH // 2)
                pool.wait_ge(biased, b * (3 * QT) + 3 * j + 3)
                pool.wait_ge(roped, b * QT + older(j))
                for half in range(2):
                    sn = sin[:, j, bass.ts(half, DH // 2)].unsqueeze(1).to_broadcast([P, HQ + HKV, DH // 2])
                    pool.tensor_tensor(o[:, :, half], x[:, :, 1 - half], sn, ALU.mult).then_inc(turned, 1)

            with pool.Fori(0, BATCH) as b:
                for j in range(QT):
                    turn(b, j)

        @block.tensor
        def _(pe):
            pe.wait_ge(const_ready, 32)

            def transposes(b, j):
                pe.wait_ge(ln, b * (4 * QT) + 4 * j + 4)
                pe.wait_ge(xt_lo, b * QT + older(j))
                for t in range(DT):
                    mm = pe.transpose(X_bank[j % 2][:, bass.ts(t, P)], XN[j % 2][:, bass.ts(t, P)], ident[:])
                mm.then_inc(xt_done, 1)

            def products(b, j):
                pe.wait_ge(xt_lo, b * QT + j + 1)
                pe.wait_ge(biased, b * (3 * QT) + 3 * older(j))
                for bank, lo, hi, done in ((Q_bank, 0, NQ, q_done), (KV_bank, NQ, N, kv_done)):
                    for t in range(DT):
                        mm = product(pe, bank[j % 2][:, 0:hi - lo], (XT_h[j % 2][:, bass.ts(t, P)], XT_l[j % 2][:, bass.ts(t, P)]),
                                     (W_h[:, t, lo:hi], W_l[:, t, lo:hi]), t == 0, t == DT - 1)
                    mm.then_inc(done, 1)

            pe.wait_ge(w_lo, 1)
            with pe.Fori(0, BATCH) as b:
                for s in range(QT + 1):
                    if s < QT:
                        transposes(b, s)
                    if s >= 1:
                        products(b, s - 1)

        @block.scalar
        def _(act):
            act.wait_ge(w_in, 16)
            act.copy(W_h[:], W[:]).then_inc(w_hi, 1)
            act.wait_ge(eps_ok, 1)
            with act.Fori(0, BATCH) as b:
                for j in range(QT):
                    act.wait_ge(ln, b * (4 * QT) + 4 * j + 2)
                    act.activation(std[:], mv[:, 1:2], ACT.Sqrt, bias=eps[:, 0:1]).then_inc(std_ok, 1)
                    act.wait_ge(xt_done, b * QT + j + 1)
                    act.wait_ge(kv_done, b * QT + older(j))
                    act.copy(XT_h[j % 2][:], X_bank[j % 2][:]).then_inc(xt_hi, 1)

        @block.vector
        def _(dve):
            dve.memset(eps[:], EPS).then_inc(eps_ok, 1)
            dve.wait_ge(tabs_in, 48)

            def normalise(b, j):
                t = bass.ds(b * QT + j, 1)
                n = b * (4 * QT) + 4 * j
                dve.wait_ge(ln, n)
                dve.bn_stats(stat[:], H[:, t].rearrange("p o d -> p (o d)")).then_inc(ln, 1)
                dve.wait_ge(ln, n + 1)
                dve.sem_inc(waited, 1)
                dve.bn_aggr(mv[:], stat[:]).then_inc(ln, 1)
                dve.wait_ge(std_ok, b * QT + j + 1)
                dve.reciprocal(rstd[:], std[:]).then_inc(ln, 1)
                dve.wait_ge(ln, n + 3)
                dve.wait_ge(xt_done, b * QT + older(j))
                dve.tensor_scalar(XN[j % 2][:], H[:, t].rearrange("p o d -> p (o d)"), mv[:, 0:1], rstd[:, 0:1],
                                  ALU.subtract, ALU.mult).then_inc(ln, 1)

            def lower(b, j):
                dve.wait_ge(xt_hi, b * QT + j + 1)
                dve.tensor_tensor(XT_l[j % 2][:], X_bank[j % 2][:], XT_h[j % 2][:].bitcast(F32), ALU.subtract).then_inc(xt_lo, 1)

            def rotate(b, j):
                t = bass.ds(b * QT + j, 1)
                cs = cos[:, j].unsqueeze(1).to_broadcast([P, HQ + HKV, DH])
                heads = lambda x: x.rearrange("p (h c) -> p h c", c=DH)
                dve.wait_ge(q_done, b * QT + j + 1)
                dve.wait_ge(turned, b * (2 * QT) + 2 * older(j))
                dve.wait_ge(roped, b * QT + j)
                dve.tensor_tensor(raw[j % 2][:, 0:NQ], Q_bank[j % 2][:], bias[:, 0:NQ], ALU.add).then_inc(biased, 1)
                dve.wait_ge(kv_done, b * QT + j + 1)
                dve.tensor_tensor(raw[j % 2][:, NQ:ROT], KV_bank[j % 2][:, 0:ROT - NQ], bias[:, NQ:ROT], ALU.add).then_inc(biased, 1)
                dve.tensor_tensor(QKV[:, t, ROT:N].rearrange("p o d -> p (o d)"), KV_bank[j % 2][:, ROT - NQ:N - NQ],
                                  bias[:, ROT:N], ALU.add).then_inc(biased, 1)
                dve.wait_ge(biased, b * (3 * QT) + 3 * j + 2)
                dve.tensor_tensor(heads(rc[:]), heads(raw[j % 2][:]), cs, ALU.mult).then_inc(cosed, 1)
                dve.wait_ge(cosed, b * QT + j + 1)
                dve.wait_ge(turned, b * (2 * QT) + 2 * j + 2)
                dve.tensor_tensor(QKV[:, t, 0:ROT].rearrange("p o d -> p (o d)"), rc[:], rs[j % 2][:], ALU.add).then_inc(roped, 1)

            with dve.Fori(0, BATCH) as b:
                for s in range(QT + 1):
                    if s < QT:
                        normalise(b, s)
                        lower(b, s)
                    if s >= 1:
                        rotate(b, s - 1)


def attn_attend(nc, H, const, QKV, wo_dram):
    HQ, HKV, DH = 16, 2, 32
    R = 4
    GROUPS = HQ // R
    ROT = (HQ + HKV) * DH
    NQ = HQ * DH
    SCALE = DH ** -0.5
    U = GROUPS * QT
    SLOTS = U + 3
    ident, mask, const_ready = const

    def unit(u):
        return u // QT, QT - 1 - u % QT

    with ExitStack() as ctx:
        m = Stage(nc, ctx, "at")
        Wo = m.sb("Wo", [P, GROUPS, D])
        Wo_h = m.sb("Wo_h", [P, GROUPS, D], F32R)
        Wo_l = m.sb("Wo_l", [P, GROUPS, D], F32R)
        q_in = [m.sb(f"q_in{i}", [P, QT, P]) for i in range(2)]
        k_in = [m.sb(f"k_in{g}", [P, QT, P]) for g in range(HKV)]
        V = [m.sb(f"V{g}", [P, QT, DH]) for g in range(HKV)]
        Q_h = [m.sb(f"Q_h{i}", [P, SEQ], F32R) for i in range(2)]
        Q_l = [m.sb(f"Q_l{i}", [P, SEQ], F32R) for i in range(2)]
        K_h = [m.sb(f"K_h{g}", [P, SEQ], F32R) for g in range(HKV)]
        K_l = [m.sb(f"K_l{g}", [P, SEQ], F32R) for g in range(HKV)]
        Pr = [m.sb(f"Pr{i}", [P, R, SEQ]) for i in range(3)]
        PT = [m.sb(f"PT{i}", [P, R, SEQ]) for i in range(2)]
        O_h = m.sb("O_h", [P, GROUPS, SEQ], F32R)
        O_l = m.sb("O_l", [P, GROUPS, SEQ], F32R)
        least = m.sb("least", [P, 4, R])
        den = m.sb("den", [P, 4, R])
        rden = m.sb("rden", [P, 4, R])
        S_bank = [m.bank(f"S_bank{r}") for r in range(R)]
        T_bank = [m.bank(f"T_bank{i}") for i in range(2)]
        O_bank = m.bank("O_bank")
        X_bank = m.bank("X_bank")

        w_in, w_hi, w_lo = m.sem("w_in"), m.sem("w_hi"), m.sem("w_lo")
        q_ready, k_ready, v_ready = m.sem("q_ready"), m.sem("k_ready"), m.sem("v_ready")
        op_done, op_hi, op_lo = m.sem("op_done"), m.sem("op_hi"), m.sem("op_lo")
        wo_done, added = m.sem("wo_done"), m.sem("added")
        s_done, s_masked, p_done, rden_ok, p_norm = m.sem("s_done"), m.sem("s_masked"), m.sem("p_done"), m.sem("rden_ok"), m.sem("p_norm")
        pt_done, pt_act, pt_dve, pv_done = m.sem("pt_done"), m.sem("pt_act"), m.sem("pt_dve"), m.sem("pv_done")
        o_hi, o_lo = m.sem("o_hi"), m.sem("o_lo")
        waited = m.sem("waited")
        block = ctx.enter_context(nc.Block())

        def older(n, places=2):
            return max(n + 1 - places, 0)

        EVENTS = [(1, "q", 1, 0), (5, "k", 1, 0), (5, "q", 2, 0), (9, "q", 3, 0), (13, "k", 0, 1), (13, "q", 0, 1)]
        AHEAD = 2
        NE = len(EVENTS)
        made_for = (AHEAD, AHEAD + 1, AHEAD + 3, AHEAD + 4)

        @block.sync
        def _(sp):
            sp.dma_start(Wo[:], wo_dram.rearrange("(g p) n -> p g n", p=P)).then_inc(w_in, 16)

        @block.gpsimd
        def _(pool):
            pool.wait_ge(w_in, 16)
            pool.wait_ge(w_hi, 1)
            pool.tensor_tensor(Wo_l[:], Wo[:], Wo_h[:].bitcast(F32), ALU.subtract).then_inc(w_lo, 1)

            def bring(first, what, g):
                rows = bass.ds(first, QT)
                if what == "q":
                    pool.tensor_copy(q_in[g % 2][:], QKV[:, rows, bass.ts(g, P)]).then_inc(q_ready, 1)
                else:
                    src = QKV[:, rows, NQ + g * DH:NQ + (g + 1) * DH].unsqueeze(2).to_broadcast([P, QT, R, DH])
                    pool.tensor_copy(k_in[g][:].rearrange("p j (r c) -> p j r c", r=R), src).then_inc(k_ready, 1)
                    pool.tensor_copy(V[g][:], QKV[:, rows, ROT + g * DH:ROT + (g + 1) * DH]).then_inc(v_ready, 1)

            bring(0, "k", 0)
            bring(0, "q", 0)
            with pool.Fori(0, BATCH) as b:
                for s in range(SLOTS):
                    for i, (slot, what, g, ahead) in enumerate(EVENTS):
                        if slot == s:
                            pool.wait_ge(op_done, b * NE + AHEAD + i)
                            if what == "k":
                                pool.wait_ge(pv_done, b * U + (0 if g else 2 * QT))
                            bring((b + ahead) % BATCH * QT if ahead else b * QT, what, g)

        @block.tensor
        def _(pe):
            pe.wait_ge(const_ready, 32)

            def operand(b, i):
                _, what, g, _ = EVENTS[i]
                src = q_in[g % 2] if what == "q" else k_in[g]
                if b is None:
                    pe.wait_ge(q_ready if what == "q" else k_ready, 1)
                    pe.wait_ge(op_lo, i + AHEAD)
                else:
                    if what == "q":
                        pe.wait_ge(q_ready, b * GROUPS + (g or GROUPS) + 1)
                    else:
                        pe.wait_ge(k_ready, b * HKV + (g or HKV) + 1)
                    pe.wait_ge(op_lo, b * NE + AHEAD + i)
                    if i == 0:
                        pe.wait_ge(added, b * QT)
                for j in range(QT):
                    mm = pe.transpose(X_bank[:, bass.ts(j, P)], src[:, j], ident[:])
                mm.then_inc(op_done, 1)

            def score(b, u):
                g, q = unit(u)
                n = P * (q + 1)
                pe.wait_ge(op_lo, b * NE + made_for[g])
                Q = [(Q_h, Q_l)[x][g % 2][:, bass.ts(q, P)] for x in range(2)]
                K = [(K_h, K_l)[x][g // 2][:, 0:n] for x in range(2)]
                for n_pass, (x, y) in enumerate(((1, 0), (0, 1), (0, 0))):
                    for r in range(R):
                        rows = slice(r * DH, (r + 1) * DH)
                        if n_pass == 0:
                            pe.wait_ge(s_masked, b * (R * U) + max(R * (u - 1) + r + 1, 0))
                        mm = pe.matmul(S_bank[r][:, 0:n], Q[x][rows], K[y][rows], start=n_pass == 0, stop=n_pass == 2)
                        if n_pass == 2:
                            mm.then_inc(s_done, 1)

            def turn(b, u):
                n = unit(u)[1] + 1
                for r in range(R):
                    pe.wait_ge(p_norm, b * (R * U) + R * u + r + 1)
                    pe.wait_ge((pt_act, pt_dve)[r % 2], b * (2 * U) + 2 * u + r // 2)
                    for k in range(n):
                        mm = pe.transpose(T_bank[r % 2][:, bass.ts(k, P)], Pr[u % 3][:, r, bass.ts(k, P)], ident[:])
                    mm.then_inc(pt_done, 1)

            def apply(b, u):
                g, q = unit(u)
                pe.wait_ge(pt_act, b * (2 * U) + 2 * u + 2)
                pe.wait_ge(pt_dve, b * (2 * U) + 2 * u + 2)
                pe.wait_ge(v_ready, b * HKV + g // 2 + 1)
                pe.wait_ge(o_lo, b * GROUPS + g)
                for k in range(q + 1):
                    for r in range(R):
                        mm = pe.matmul(O_bank[r * DH:(r + 1) * DH, bass.ts(q, P)], V[g // 2][:, k], PT[u % 2][:, r, bass.ts(k, P)],
                                       start=k == 0, stop=k == q)
                mm.then_inc(pv_done, 1)

            def out(b, j):
                if j == 0:
                    pe.wait_ge(o_lo, (b + 1) * GROUPS)
                    pe.wait_ge(op_lo, (b + 1) * NE + AHEAD)
                else:
                    pe.wait_ge(added, b * QT + j)
                for g in range(GROUPS):
                    mm = product(pe, X_bank[:], (O_h[:, g, bass.ts(j, P)], O_l[:, g, bass.ts(j, P)]),
                                 (Wo_h[:, g], Wo_l[:, g]), g == 0, g == GROUPS - 1)
                mm.then_inc(wo_done, 1)

            for i in range(-AHEAD, 0):
                operand(None, i)
            pe.wait_ge(w_lo, 1)
            with pe.Fori(0, BATCH) as b:
                for s in range(SLOTS):
                    if s < U:
                        score(b, s)
                    if 0 <= s - 2 < U:
                        turn(b, s - 2)
                    for i, e in enumerate(EVENTS):
                        if e[0] == s:
                            operand(b, i)
                    if 0 <= s - 3 < U:
                        apply(b, s - 3)
                for j in range(QT):
                    out(b, j)

        def halves(i):
            _, what, g, _ = EVENTS[i]
            return (Q_h[g % 2][:], Q_l[g % 2][:]) if what == "q" else (K_h[g][:], K_l[g][:])

        @block.scalar
        def _(act):
            act.wait_ge(w_in, 16)
            act.copy(Wo_h[:], Wo[:]).then_inc(w_hi, 1)

            def upper(n, i):
                act.wait_ge(op_done, n)
                act.copy(halves(i)[0], X_bank[:]).then_inc(op_hi, 1)

            def exps(b, u):
                n = P * (unit(u)[1] + 1)
                for r in range(R):
                    act.wait_ge(s_masked, b * (R * U) + R * u + r + 1)
                    if r == 0:
                        act.wait_ge(rden_ok, b * U + older(u, 4))
                    act.activation(Pr[u % 3][:, r, 0:n], Pr[u % 3][:, r, 0:n], ACT.Exp, bias=least[:, u % 4, r:r + 1],
                                   scale=-1.0, accum_out=den[:, u % 4, r:r + 1]).then_inc(p_done, 1)

            def turned(b, u):
                n = P * (unit(u)[1] + 1)
                act.wait_ge(pv_done, b * U + older(u))
                for r in (0, 2):
                    act.wait_ge(pt_done, b * (R * U) + R * u + r + 1)
                    act.copy(PT[u % 2][:, r, 0:n], T_bank[0][:, 0:n]).then_inc(pt_act, 1)

            for i in range(-AHEAD, 0):
                upper(i + AHEAD + 1, i)
            with act.Fori(0, BATCH) as b:
                for s in range(SLOTS):
                    if s < U:
                        exps(b, s)
                    if 0 <= s - 2 < U:
                        turned(b, s - 2)
                    for i, e in enumerate(EVENTS):
                        if e[0] == s:
                            upper(b * NE + AHEAD + i + 1, i)
                    if 0 <= s - 3 < U and (s - 3) % QT == QT - 1:
                        g = (s - 3) // QT
                        act.wait_ge(pv_done, b * U + s - 2)
                        act.wait_ge(wo_done, b * QT)
                        act.copy(O_h[:, g], O_bank[:]).then_inc(o_hi, 1)

        @block.vector
        def _(dve):
            def lower(n, i):
                h, lo = halves(i)
                dve.wait_ge(op_hi, n)
                dve.tensor_tensor(lo, X_bank[:], h.bitcast(F32), ALU.subtract).then_inc(op_lo, 1)

            def mask_scores(b, u):
                n = P * (unit(u)[1] + 1)
                for r in range(R):
                    dve.wait_ge(s_done, b * (R * U) + R * u + r + 1)
                    if r == 0:
                        dve.wait_ge(pt_done, b * (R * U) + R * older(u, 3))
                    dve.sem_inc(waited, 1)
                    dve.tensor_tensor_reduce(out=Pr[u % 3][:, r, 0:n], in0=S_bank[r][:, 0:n], in1=mask[:, SEQ - n:SEQ],
                                             scale=-SCALE, scalar=-MASKED, op0=ALU.add, op1=ALU.min,
                                             accum_out=least[:, u % 4, r:r + 1]).then_inc(s_masked, 1)

            def normalise(b, u):
                dve.wait_ge(p_done, b * (R * U) + R * u + R)
                dve.reciprocal(rden[:, u % 4], den[:, u % 4]).then_inc(rden_ok, 1)
                dve.wait_ge(rden_ok, b * U + u + 1)
                n = P * (unit(u)[1] + 1)
                for r in range(R):
                    dve.tensor_scalar(Pr[u % 3][:, r, 0:n], Pr[u % 3][:, r, 0:n], rden[:, u % 4, r:r + 1], None,
                                      ALU.mult).then_inc(p_norm, 1)

            def turned(b, u):
                n = P * (unit(u)[1] + 1)
                for r in (1, 3):
                    dve.wait_ge(pt_done, b * (R * U) + R * u + r + 1)
                    dve.tensor_copy(PT[u % 2][:, r, 0:n], T_bank[1][:, 0:n]).then_inc(pt_dve, 1)

            for i in range(-AHEAD, 0):
                lower(i + AHEAD + 1, i)
            with dve.Fori(0, BATCH) as b:
                for s in range(SLOTS):
                    if s < U:
                        mask_scores(b, s)
                    if 0 <= s - 1 < U:
                        normalise(b, s - 1)
                    if 0 <= s - 2 < U:
                        dve.wait_ge(pv_done, b * U + older(s - 2))
                        turned(b, s - 2)
                    for i, e in enumerate(EVENTS):
                        if e[0] == s:
                            lower(b * NE + AHEAD + i + 1, i)
                    if 0 <= s - 3 < U and (s - 3) % QT == QT - 1:
                        g = (s - 3) // QT
                        dve.wait_ge(o_hi, b * GROUPS + g + 1)
                        dve.tensor_tensor(O_l[:, g], O_bank[:], O_h[:, g].bitcast(F32), ALU.subtract).then_inc(o_lo, 1)
                for j in range(QT):
                    t = bass.ds(b * QT + j, 1)
                    dve.wait_ge(wo_done, b * QT + j + 1)
                    h = H[:, t].rearrange("p o d -> p (o d)")
                    dve.tensor_tensor(h, X_bank[:], h, ALU.add).then_inc(added, 1)


def block_project(nc, H, const, h_dram, q_dram, k_dram, v_dram, w_dram, ln1_dram, norm_dram, cos_dram, sin_dram):
    HQ, HKV, DH, RD = 16, 4, 128, 64
    NQ, NK = HQ * DH, HKV * DH
    N = NQ + 2 * NK
    ROT = NQ + NK
    CH = N // D
    LN_EPS, RMS_EPS = 1e-5, 1e-6
    ORDER = (4, 0, 1, 2, 3, 5)
    ident, _, const_ready = const

    with ExitStack() as ctx:
        m = Stage(nc, ctx, "bp")
        W_h = m.sb("W_h", [P, DT, N], F32R)
        W_l = m.sb("W_l", [P, DT, N], F32R)
        ln1 = m.sb("ln1", [P, D])
        norm = m.sb("norm", [P, ROT])
        cos = m.sb("cos", [P, QT, RD])
        sin = m.sb("sin", [P, QT, RD])
        XN = m.sb("XN", [P, D])
        XT_h = [m.sb(f"XT_h{i}", [P, D], F32R) for i in range(2)]
        XT_l = [m.sb(f"XT_l{i}", [P, D], F32R) for i in range(2)]
        raw = [m.sb(f"raw{i}", [P, N]) for i in range(2)]
        W = raw
        rc = m.sb("rc", [P, HQ + HKV, RD])
        rs = m.sb("rs", [P, HQ + HKV, RD])
        unused = m.sb("unused", [P, D], mybir.dt.bfloat16)
        stat = m.sb("stat", [P, 6])
        mv = m.sb("mv", [P, 2])
        eps = m.sb("eps", [P, 2])
        ssx, ssq, ssqs, ssk = m.sb("ssx", [P, 1]), m.sb("ssq", [P, 4]), m.sb("ssqs", [P, 1]), m.sb("ssk", [P, 1])
        std, rstd = m.sb("std", [P, 4]), m.sb("rstd", [P, 4])
        X_bank = [m.bank(f"X_bank{i}") for i in range(2)]
        C_bank = [m.bank(f"C_bank{i}") for i in range(CH)]

        w_in = [m.sem(f"w_in{i}") for i in range(2)]
        w_hi, w_lo, tabs_in, saved = m.sem("w_hi"), m.sem("w_lo"), m.sem("tabs_in"), m.sem("saved")
        eps_ok, ln, std_ok, rms_sum, rms_std = m.sem("eps_ok"), m.sem("ln"), m.sem("std_ok"), m.sem("rms_sum"), m.sem("rms_std")
        xt_done, xt_hi, xt_lo = m.sem("xt_done"), m.sem("xt_hi"), m.sem("xt_lo")
        c_done, squared, v_out = m.sem("c_done"), m.sem("squared"), m.sem("v_out")
        k_std, q_std, k_inv, q_inv = m.sem("k_std"), m.sem("q_std"), m.sem("k_inv"), m.sem("q_inv")
        left, turned, cosed, roped, scaled = m.sem("left"), m.sem("turned"), m.sem("cosed"), m.sem("roped"), m.sem("scaled")
        stored = [m.sem(f"stored{i}") for i in range(2)]
        waited = m.sem("waited")
        block = ctx.enter_context(nc.Block())

        def older(n):
            return max(n - 1, 0)

        def heads(x):
            return x[:, 0:ROT].rearrange("p (h c) -> p h c", c=DH)[:, :, 0:RD]

        q_view = q_dram.rearrange("(b g) (j p) n -> b j p g n", b=BATCH, p=P)
        k_view = k_dram.rearrange("(b g) (j p) n -> b j p g n", b=BATCH, p=P)
        v_view = v_dram.rearrange("(b g) (j p) n -> b j p g n", b=BATCH, p=P)

        @block.sync
        def _(sp):
            for t in range(DT):
                if t >= 2:
                    sp.wait_ge(w_lo, t - 1)
                sp.dma_start(W[t % 2][:], w_dram[bass.ts(t, P)]).then_inc(w_in[t % 2], 16)
                if t == 1:
                    sp.dma_start(h_dram, H[:]).then_inc(saved, 16)
                    sp.dma_start(ln1[:], ln1_dram.partition_broadcast(P)).then_inc(tabs_in, 16)
                    sp.dma_start(norm[:], norm_dram.partition_broadcast(P)).then_inc(tabs_in, 16)
                    sp.dma_start(cos[:], cos_dram.rearrange("(j p) d -> p j d", p=P)).then_inc(tabs_in, 16)
                    sp.dma_start(sin[:], sin_dram.rearrange("(j p) d -> p j d", p=P)).then_inc(tabs_in, 16)
            with sp.Fori(0, BATCH) as b:
                for j in range(QT):
                    r = raw[j % 2]
                    sp.wait_ge(scaled, b * QT + j + 1)
                    sp.wait_ge(v_out, b * QT + j + 1)
                    for view, lo, hi in ((q_view, 0, NQ), (k_view, NQ, ROT), (v_view, ROT, N)):
                        sp.dma_start(view[bass.ds(b, 1), j].rearrange("o p g n -> p (o g) n"),
                                     r[:, lo:hi].rearrange("p (g n) -> p g n", g=HKV)).then_inc(stored[j % 2], 16)
            for i in range(2):
                sp.wait_ge(stored[i], 16 * 3 * TILES // 2)

        @block.gpsimd
        def _(pool):
            for t in range(DT):
                pool.wait_ge(w_hi, t + 1)
                pool.tensor_tensor(W_l[:, t], W[t % 2][:], W_h[:, t].bitcast(F32), ALU.subtract).then_inc(w_lo, 1)
            pool.wait_ge(tabs_in, 64)
            with pool.Fori(0, BATCH) as b:
                for j in range(QT):
                    x = heads(raw[j % 2]).rearrange("p h (s c) -> p h s c", s=2)
                    o = rs[:].rearrange("p h (s c) -> p h s c", s=2)
                    pool.wait_ge(left, b * (5 * QT) + 5 * j + 5)
                    pool.wait_ge(roped, b * QT + j)
                    for half in range(2):
                        sn = sin[:, j, bass.ts(half, RD // 2)].unsqueeze(1).to_broadcast([P, HQ + HKV, RD // 2])
                        pool.tensor_tensor(o[:, :, half], x[:, :, 1 - half], sn, ALU.mult).then_inc(turned, 1)

        @block.tensor
        def _(pe):
            pe.wait_ge(const_ready, 32)

            def transposes(b, j):
                pe.wait_ge(ln, b * (7 * QT) + 7 * j + 7)
                pe.wait_ge(xt_lo, b * QT + older(j))
                for t in range(DT):
                    mm = pe.transpose(X_bank[j % 2][:, bass.ts(t, P)], XN[:, bass.ts(t, P)], ident[:])
                mm.then_inc(xt_done, 1)

            def products(b, j):
                pe.wait_ge(xt_lo, b * QT + j + 1)
                for i, c in enumerate(ORDER):
                    if c < 5:
                        pe.wait_ge(left, b * (5 * QT) + 5 * j - 5 + i + 1 if j else b * (5 * QT))
                    else:
                        pe.wait_ge(v_out, b * QT + j)
                    for t in range(DT):
                        mm = product(pe, C_bank[c][:], (XT_h[j % 2][:, bass.ts(t, P)], XT_l[j % 2][:, bass.ts(t, P)]),
                                     (W_h[:, t, bass.ts(c, D)], W_l[:, t, bass.ts(c, D)]), t == 0, t == DT - 1)
                    mm.then_inc(c_done, 1)

            pe.wait_ge(w_lo, DT)
            with pe.Fori(0, BATCH) as b:
                transposes(b, 0)
                for j in range(QT):
                    if j + 1 < QT:
                        transposes(b, j + 1)
                    products(b, j)

        @block.scalar
        def _(act):
            for t in range(DT):
                act.wait_ge(w_in[t % 2], 16 * (t // 2 + 1))
                act.copy(W_h[:, t], W[t % 2][:]).then_inc(w_hi, 1)
            act.wait_ge(eps_ok, 2)

            def norms(b, j):
                t = bass.ds(b * QT + j, 1)
                n = b * (7 * QT) + 7 * j
                act.wait_ge(ln, n + 2)
                act.activation(std[:, 0:1], mv[:, 1:2], ACT.Sqrt, bias=eps[:, 0:1]).then_inc(std_ok, 1)
                act.wait_ge(eps_ok, 2)
                act.wait_ge(ln, n + 4)
                act.activation(unused[:], H[:, t].rearrange("p o d -> p (o d)"), ACT.Square, accum_out=ssx[:, 0:1]).then_inc(rms_sum, 1)
                act.wait_ge(rms_sum, b * QT + j + 1)
                act.activation(std[:, 1:2], ssx[:, 0:1], ACT.Sqrt, bias=eps[:, 1:2], scale=1.0 / D).then_inc(rms_std, 1)
                act.wait_ge(xt_done, b * QT + j + 1)
                act.copy(XT_h[j % 2][:], X_bank[j % 2][:]).then_inc(xt_hi, 1)

            def squares(b, j):
                for i, c in enumerate(ORDER):
                    act.wait_ge(c_done, b * (CH * QT) + CH * j + i + 1)
                    if c == 5:
                        if j >= 2:
                            act.wait_ge(stored[j % 2], b * (16 * 3 * QT // 2) + 16 * 3 * (j // 2))
                        else:
                            act.wait_ge(stored[j % 2], b * (16 * 3 * QT // 2))
                        act.copy(raw[j % 2][:, ROT:N], C_bank[c][:]).then_inc(v_out, 1)
                        continue
                    act.wait_ge(squared, b * (5 * QT) + 5 * j + i)
                    if c == 4:
                        act.activation(unused[:], C_bank[c][:], ACT.Square, accum_out=ssk[:, 0:1]).then_inc(squared, 1)
                        act.wait_ge(squared, b * (5 * QT) + 5 * j + 1)
                        act.activation(std[:, 3:4], ssk[:, 0:1], ACT.Sqrt, bias=eps[:, 1:2], scale=1.0 / NK).then_inc(k_std, 1)
                    else:
                        act.activation(unused[:], C_bank[c][:], ACT.Square, accum_out=ssq[:, c:c + 1]).then_inc(squared, 1)
                act.wait_ge(q_inv, b * (2 * QT) + 2 * j + 1)
                act.activation(std[:, 2:3], ssqs[:, 0:1], ACT.Sqrt, bias=eps[:, 1:2], scale=1.0 / NQ).then_inc(q_std, 1)

            def scale_queries(b, j):
                act.wait_ge(roped, b * QT + j + 1)
                act.wait_ge(q_inv, b * (2 * QT) + 2 * j + 2)
                act.activation(raw[j % 2][:, 0:NQ], raw[j % 2][:, 0:NQ], ACT.Copy, scale=rstd[:, 2:3]).then_inc(scaled, 1)

            with act.Fori(0, BATCH) as b:
                norms(b, 0)
                for j in range(QT):
                    if j + 1 < QT:
                        norms(b, j + 1)
                    squares(b, j)
                    scale_queries(b, j)

        @block.vector
        def _(dve):
            dve.memset(eps[:, 0:1], LN_EPS).then_inc(eps_ok, 1)
            dve.memset(eps[:, 1:2], RMS_EPS).then_inc(eps_ok, 1)
            dve.wait_ge(tabs_in, 64)
            dve.wait_ge(saved, 16)

            def norms(b, j):
                x = H[:, bass.ds(b * QT + j, 1)].rearrange("p o d -> p (o d)")
                n = b * (7 * QT) + 7 * j
                dve.wait_ge(ln, n)
                dve.bn_stats(stat[:], x).then_inc(ln, 1)
                dve.wait_ge(ln, n + 1)
                dve.sem_inc(waited, 1)
                dve.bn_aggr(mv[:], stat[:]).then_inc(ln, 1)
                dve.wait_ge(std_ok, b * QT + j + 1)
                dve.reciprocal(rstd[:, 0:1], std[:, 0:1]).then_inc(ln, 1)
                dve.wait_ge(ln, n + 3)
                dve.tensor_scalar(x, x, mv[:, 0:1], rstd[:, 0:1], ALU.subtract, ALU.mult).then_inc(ln, 1)
                dve.wait_ge(rms_std, b * QT + j + 1)
                dve.reciprocal(rstd[:, 1:2], std[:, 1:2]).then_inc(ln, 1)
                dve.wait_ge(xt_done, b * QT + j)
                dve.wait_ge(ln, n + 5)
                dve.tensor_scalar(XN[:], x, rstd[:, 1:2], None, ALU.mult).then_inc(ln, 1)
                dve.wait_ge(ln, n + 6)
                dve.tensor_tensor(XN[:], XN[:], ln1[:], ALU.mult).then_inc(ln, 1)
                dve.wait_ge(xt_hi, b * QT + j + 1)
                dve.tensor_tensor(XT_l[j % 2][:], X_bank[j % 2][:], XT_h[j % 2][:].bitcast(F32), ALU.subtract).then_inc(xt_lo, 1)

            def leave(b, j):
                r = raw[j % 2]
                dve.wait_ge(stored[j % 2], b * (16 * 3 * QT // 2) + 16 * 3 * (j // 2))
                for i, c in enumerate(ORDER[:5]):
                    w = norm[:, bass.ts(c, D)]
                    dve.wait_ge(squared, b * (5 * QT) + 5 * j + i + 1)
                    if c == 4:
                        dve.wait_ge(k_std, b * QT + j + 1)
                        dve.reciprocal(rstd[:, 3:4], std[:, 3:4]).then_inc(k_inv, 1)
                        dve.wait_ge(k_inv, b * QT + j + 1)
                        dve.scalar_tensor_tensor(out=r[:, bass.ts(c, D)], in0=C_bank[c][:], scalar=rstd[:, 3:4], in1=w,
                                                 op0=ALU.mult, op1=ALU.mult).then_inc(left, 1)
                    else:
                        dve.tensor_tensor(r[:, bass.ts(c, D)], C_bank[c][:], w, ALU.mult).then_inc(left, 1)
                dve.wait_ge(q_std, b * QT + j)
                dve.reduce_sum(ssqs[:], ssq[:], AX_X).then_inc(q_inv, 1)
                cs = cos[:, j].unsqueeze(1).to_broadcast([P, HQ + HKV, RD])
                dve.wait_ge(left, b * (5 * QT) + 5 * j + 5)
                dve.wait_ge(roped, b * QT + j)
                dve.tensor_tensor(rc[:], heads(r), cs, ALU.mult).then_inc(cosed, 1)
                dve.wait_ge(scaled, b * QT + j)
                dve.wait_ge(q_std, b * QT + j + 1)
                dve.reciprocal(rstd[:, 2:3], std[:, 2:3]).then_inc(q_inv, 1)
                dve.wait_ge(cosed, b * QT + j + 1)
                dve.wait_ge(turned, b * (2 * QT) + 2 * j + 2)
                dve.tensor_tensor(heads(r), rc[:], rs[:], ALU.add).then_inc(roped, 1)

            with dve.Fori(0, BATCH) as b:
                norms(b, 0)
                for j in range(QT):
                    if j + 1 < QT:
                        norms(b, j + 1)
                    leave(b, j)


def block_attend(nc, X1, const, q_dram, k_dram, v_dram, wo_dram):
    HQ, HKV, DH = 16, 4, 128
    R = HQ // HKV
    SCALE = float(DH) ** -0.5
    JOBS = BATCH * HKV
    U = R * QT
    SLOTS = U + 3
    ident, mask, const_ready = const

    def unit(u):
        return u // QT, QT - 1 - u % QT

    with ExitStack() as ctx:
        m = Stage(nc, ctx, "ba")
        Wo = [m.sb(f"Wo{i}", [P, D]) for i in range(2)]
        Wo_h = m.sb("Wo_h", [P, HQ, D], F32R)
        Wo_l = m.sb("Wo_l", [P, HQ, D], F32R)
        q_in = [m.sb(f"q_in{i}", [P, QT, P]) for i in range(2)]
        k_in = m.sb("k_in", [P, QT, P])
        v_in = m.sb("v_in", [P, QT, P])
        Q_h = [m.sb(f"Q_h{i}", [P, SEQ], F32R) for i in range(2)]
        Q_l = [m.sb(f"Q_l{i}", [P, SEQ], F32R) for i in range(2)]
        K_h, K_l = m.sb("K_h", [P, SEQ], F32R), m.sb("K_l", [P, SEQ], F32R)
        V_h, V_l = m.sb("V_h", [P, QT, P], F32R), m.sb("V_l", [P, QT, P], F32R)
        Pr = [m.sb(f"Pr{i}", [P, SEQ]) for i in range(4)]
        PT_h = [m.sb(f"PT_h{i}", [P, QT, SEQ], F32R) for i in range(2)]
        PT_l = [m.sb(f"PT_l{i}", [P, QT, SEQ], F32R) for i in range(2)]
        O_h = m.sb("O_h", [P, R, SEQ], F32R)
        O_l = m.sb("O_l", [P, R, SEQ], F32R)
        least, den, rden = m.sb("least", [P, 4]), m.sb("den", [P, 4]), m.sb("rden", [P, 4])
        S_bank = [m.bank(f"S_bank{i}") for i in range(2)]
        T_bank = [m.bank(f"T_bank{i}") for i in range(2)]
        O_bank = m.bank("O_bank")
        X_bank = m.bank("X_bank")
        Y_bank = [m.bank(f"Y_bank{i}") for i in range(2)]

        w_in = [m.sem(f"w_in{i}") for i in range(2)]
        w_hi, w_lo = m.sem("w_hi"), m.sem("w_lo")
        q_loaded = [m.sem(f"q_loaded{i}") for i in range(2)]
        k_loaded, v_loaded = m.sem("k_loaded"), m.sem("v_loaded")
        v_hi, v_lo = m.sem("v_hi"), m.sem("v_lo")
        op_done, op_hi, op_lo = m.sem("op_done"), m.sem("op_hi"), m.sem("op_lo")
        s_done, s_masked, p_done, rden_ok, p_norm = m.sem("s_done"), m.sem("s_masked"), m.sem("p_done"), m.sem("rden_ok"), m.sem("p_norm")
        pt_done, pt_hi, pt_lo, pv_done = m.sem("pt_done"), m.sem("pt_hi"), m.sem("pt_lo"), m.sem("pv_done")
        o_hi, o_lo, wo_done, added = m.sem("o_hi"), m.sem("o_lo"), m.sem("wo_done"), m.sem("added")
        waited = m.sem("waited")
        block = ctx.enter_context(nc.Block())

        def older(n, places=2):
            return max(n + 1 - places, 0)

        EVENTS = [(1, "q", 1), (5, "q", 2), (9, "q", 3), (13, "q", 0), (SLOTS - 1, "k", 0)]
        NE = len(EVENTS)
        AHEAD = 2
        made_for = (2, 3, 4, 5)

        def blocked(dram, job, lo, n):
            return dram[bass.ds(job, 1), :, lo:lo + n].rearrange("o (j p) n -> p (o j) n", p=P)

        @block.sync
        def _(sp):
            sp.dma_start(k_in[:], blocked(k_dram, 0, 0, P)).then_inc(k_loaded, 16)
            sp.dma_start(q_in[0][:], blocked(q_dram, 0, 0, P)).then_inc(q_loaded[0], 16)
            sp.dma_start(v_in[:], blocked(v_dram, 0, 0, P)).then_inc(v_loaded, 16)
            for h in range(HQ):
                if h >= 2:
                    sp.wait_ge(w_lo, h - 1)
                sp.dma_start(Wo[h % 2][:], wo_dram[bass.ts(h, P)]).then_inc(w_in[h % 2], 16)
            with sp.Fori(0, JOBS) as i:
                for e, (_, what, h) in enumerate(EVENTS[:4]):
                    sp.wait_ge(op_done, i * NE + (0, 2, 3, 4)[e])
                    nxt = i if h else (i + 1) % JOBS
                    sp.dma_start(q_in[h % 2][:], blocked(q_dram, nxt, h * P, P)).then_inc(q_loaded[h % 2], 16)
                    if e == 0:
                        sp.wait_ge(op_done, i * NE + AHEAD)
                        sp.dma_start(k_in[:], blocked(k_dram, (i + 1) % JOBS, 0, P)).then_inc(k_loaded, 16)
                        sp.wait_ge(v_lo, i + 1)
                        sp.dma_start(v_in[:], blocked(v_dram, (i + 1) % JOBS, 0, P)).then_inc(v_loaded, 16)
            for s, n in ((k_loaded, JOBS + 1), (v_loaded, JOBS + 1), (q_loaded[0], 2 * JOBS + 1), (q_loaded[1], 2 * JOBS)):
                sp.wait_ge(s, 16 * n)

        @block.gpsimd
        def _(pool):
            for h in range(HQ):
                pool.wait_ge(w_hi, h + 1)
                pool.tensor_tensor(Wo_l[:, h], Wo[h % 2][:], Wo_h[:, h].bitcast(F32), ALU.subtract).then_inc(w_lo, 1)
            with pool.Fori(0, JOBS) as i:
                pool.wait_ge(v_hi, i + 1)
                pool.tensor_tensor(V_l[:], v_in[:], V_h[:].bitcast(F32), ALU.subtract).then_inc(v_lo, 1)

        @block.tensor
        def _(pe):
            pe.wait_ge(const_ready, 32)

            def operand(i, e):
                what, h = ("k", 0) if i is None and e == 0 else ("q", 0) if i is None else EVENTS[e][1:]
                src = k_in if what == "k" else q_in[h % 2]
                if i is None:
                    pe.wait_ge(k_loaded if what == "k" else q_loaded[0], 16)
                    pe.wait_ge(op_lo, e)
                else:
                    if what == "k":
                        pe.wait_ge(k_loaded, i * 16 + 32)
                    else:
                        pe.wait_ge(q_loaded[h % 2], i * 32 + {1: 16, 2: 32, 3: 32, 0: 48}[h])
                    pe.wait_ge(op_lo, i * NE + AHEAD + e)
                for j in range(QT):
                    mm = pe.transpose(X_bank[:, bass.ts(j, P)], src[:, j], ident[:])
                mm.then_inc(op_done, 1)

            def score(i, u):
                h, q = unit(u)
                n = P * (q + 1)
                pe.wait_ge(op_lo, i * NE + made_for[h])
                pe.wait_ge(s_masked, i * U + older(u))
                product(pe, S_bank[u % 2][:, 0:n], (Q_h[h % 2][:, bass.ts(q, P)], Q_l[h % 2][:, bass.ts(q, P)]),
                        (K_h[:, 0:n], K_l[:, 0:n]), True, True).then_inc(s_done, 1)

            def turn(i, u):
                pe.wait_ge(p_norm, i * U + u + 1)
                pe.wait_ge(pt_lo, i * U + older(u))
                for k in range(unit(u)[1] + 1):
                    mm = pe.transpose(T_bank[u % 2][:, bass.ts(k, P)], Pr[u % 4][:, bass.ts(k, P)], ident[:])
                mm.then_inc(pt_done, 1)

            def apply(i, h):
                pe.wait_ge(pt_lo, i * U + QT * (h + 1))
                pe.wait_ge(v_lo, i + 1)
                pe.wait_ge(o_lo, i * R + h)
                for k in range(QT):
                    w = slice(k * P, SEQ)
                    mm = product(pe, O_bank[:, w], (V_h[:, k], V_l[:, k]), (PT_h[h % 2][:, k, w], PT_l[h % 2][:, k, w]),
                                 k == 0, k == QT - 1)
                mm.then_inc(pv_done, 1)

            def out(i, g, j):
                if j == 0:
                    pe.wait_ge(o_lo, i * R + R)
                pe.wait_ge(added, i * QT + older(j))
                for h in range(R):
                    w = bass.ds(g * R + h, 1)
                    mm = product(pe, Y_bank[j % 2][:], (O_h[:, h, bass.ts(j, P)], O_l[:, h, bass.ts(j, P)]),
                                 (Wo_h[:, w].rearrange("p o n -> p (o n)"), Wo_l[:, w].rearrange("p o n -> p (o n)")),
                                 h == 0, h == R - 1)
                mm.then_inc(wo_done, 1)

            for e in range(AHEAD):
                operand(None, e)
            pe.wait_ge(w_lo, HQ)
            with pe.Fori(0, BATCH) as b:
                with pe.Fori(0, HKV) as g:
                    i = b * HKV + g
                    for s in range(SLOTS):
                        if s < U:
                            score(i, s)
                        if 0 <= s - 2 < U:
                            turn(i, s - 2)
                        for e, ev in enumerate(EVENTS[:4]):
                            if ev[0] == s:
                                operand(i, e)
                        if 0 <= s - 3 < U and (s - 3) % QT == QT - 1:
                            apply(i, (s - 3) // QT)
                    operand(i, 4)
                    for j in range(QT):
                        out(i, g, j)

        def halves(what, h):
            return (Q_h[h % 2][:], Q_l[h % 2][:]) if what == "q" else (K_h[:], K_l[:])

        @block.scalar
        def _(act):
            for h in range(HQ):
                act.wait_ge(w_in[h % 2], 16 * (h // 2 + 1))
                act.copy(Wo_h[:, h], Wo[h % 2][:]).then_inc(w_hi, 1)

            def upper(n, what, h):
                act.wait_ge(op_done, n)
                act.copy(halves(what, h)[0], X_bank[:]).then_inc(op_hi, 1)

            def exps(i, u):
                n = P * (unit(u)[1] + 1)
                act.wait_ge(s_masked, i * U + u + 1)
                act.wait_ge(rden_ok, i * U + older(u, 4))
                act.activation(Pr[u % 4][:, 0:n], Pr[u % 4][:, 0:n], ACT.Exp, bias=least[:, u % 4:u % 4 + 1],
                               scale=-1.0, accum_out=den[:, u % 4:u % 4 + 1]).then_inc(p_done, 1)

            def turned(i, u):
                h, q = unit(u)
                act.wait_ge(pt_done, i * U + u + 1)
                act.wait_ge(pv_done, i * R + older(h))
                act.copy(PT_h[h % 2][:, 0:q + 1, bass.ts(q, P)], T_bank[u % 2][:, 0:P * (q + 1)].rearrange("p (k n) -> p k n", n=P))\
                   .then_inc(pt_hi, 1)

            upper(1, "k", 0)
            upper(2, "q", 0)
            with act.Fori(0, JOBS) as i:
                act.wait_ge(v_loaded, i * 16 + 16)
                act.wait_ge(pv_done, i * R)
                act.copy(V_h[:], v_in[:]).then_inc(v_hi, 1)
                for s in range(SLOTS):
                    if s < U:
                        exps(i, s)
                    if 0 <= s - 2 < U:
                        turned(i, s - 2)
                    for e, (slot, what, h) in enumerate(EVENTS[:4]):
                        if slot == s:
                            upper(i * NE + AHEAD + e + 1, what, h)
                    if 0 <= s - 3 < U and (s - 3) % QT == QT - 1:
                        h = (s - 3) // QT
                        act.wait_ge(wo_done, i * QT)
                        act.wait_ge(pv_done, i * R + h + 1)
                        act.copy(O_h[:, h], O_bank[:]).then_inc(o_hi, 1)
                upper(i * NE + AHEAD + NE, "k", 0)

        @block.vector
        def _(dve):
            def lower(n, what, h):
                hi, lo = halves(what, h)
                dve.wait_ge(op_hi, n)
                dve.tensor_tensor(lo, X_bank[:], hi.bitcast(F32), ALU.subtract).then_inc(op_lo, 1)

            def mask_scores(i, u):
                n = P * (unit(u)[1] + 1)
                dve.wait_ge(s_done, i * U + u + 1)
                dve.wait_ge(pt_done, i * U + older(u, 4))
                dve.sem_inc(waited, 1)
                dve.tensor_tensor_reduce(out=Pr[u % 4][:, 0:n], in0=S_bank[u % 2][:, 0:n], in1=mask[:, SEQ - n:SEQ],
                                         scale=-SCALE, scalar=-MASKED, op0=ALU.add, op1=ALU.min,
                                         accum_out=least[:, u % 4:u % 4 + 1]).then_inc(s_masked, 1)

            def turned(i, u):
                h, q = unit(u)
                dve.wait_ge(pt_hi, i * U + u + 1)
                w = (slice(None), slice(0, q + 1), bass.ts(q, P))
                dve.tensor_tensor(PT_l[h % 2][w], T_bank[u % 2][:, 0:P * (q + 1)].rearrange("p (k n) -> p k n", n=P),
                                  PT_h[h % 2][w].bitcast(F32), ALU.subtract).then_inc(pt_lo, 1)

            lower(1, "k", 0)
            lower(2, "q", 0)
            with dve.Fori(0, BATCH) as b:
                with dve.Fori(0, HKV) as g:
                    i = b * HKV + g
                    for s in range(SLOTS):
                        if s < U:
                            mask_scores(i, s)
                        if 0 <= s - 1 < U:
                            u = s - 1
                            dve.wait_ge(p_done, i * U + u + 1)
                            dve.reciprocal(rden[:, u % 4:u % 4 + 1], den[:, u % 4:u % 4 + 1]).then_inc(rden_ok, 1)
                            n = P * (unit(u)[1] + 1)
                            dve.wait_ge(rden_ok, i * U + u + 1)
                            dve.tensor_scalar(Pr[u % 4][:, 0:n], Pr[u % 4][:, 0:n], rden[:, u % 4:u % 4 + 1], None,
                                              ALU.mult).then_inc(p_norm, 1)
                        if 0 <= s - 2 < U:
                            turned(i, s - 2)
                        for e, (slot, what, h) in enumerate(EVENTS[:4]):
                            if slot == s:
                                lower(i * NE + AHEAD + e + 1, what, h)
                        if 0 <= s - 3 < U and (s - 3) % QT == QT - 1:
                            h = (s - 3) // QT
                            dve.wait_ge(o_hi, i * R + h + 1)
                            dve.tensor_tensor(O_l[:, h], O_bank[:], O_h[:, h].bitcast(F32), ALU.subtract).then_inc(o_lo, 1)
                    lower(i * NE + AHEAD + NE, "k", 0)
                    for j in range(QT):
                        x = X1[:, bass.ds(b * QT + j, 1)].rearrange("p o d -> p (o d)")
                        dve.wait_ge(wo_done, i * QT + j + 1)
                        dve.tensor_tensor(x, Y_bank[j % 2][:], x, ALU.add).then_inc(added, 1)


def route(nc, H, const, h_dram, T_h, T_l, comb, ln2_dram, router_dram, rbias_dram, before_dram):
    E = 8
    TOPK = 2
    RMS_EPS = 1e-6
    ident, _, const_ready = const

    with ExitStack() as ctx:
        m = Stage(nc, ctx, "ro")
        ln2 = m.sb("ln2", [P, D])
        Wr = m.sb("Wr", [P, DT, E])
        rbias = m.sb("rbias", [P, E])
        before = m.sb("before", [P, E, E])
        h_in = [m.sb(f"h_in{j}", [P, D]) for j in range(QT)]
        XN = [m.sb(f"XN{i}", [P, D]) for i in range(2)]
        XT = [m.sb(f"XT{i}", [P, D]) for i in range(2)]
        unused = m.sb("unused", [P, D], mybir.dt.bfloat16)
        eps = m.sb("eps", [P, 1])
        ssx, std, rstd = m.sb("ssx", [P, 1]), m.sb("std", [P, 1]), m.sb("rstd", [P, 1])
        grow, sig, score = m.sb("grow", [P, QT, E]), m.sb("sig", [P, QT, E]), m.sb("score", [P, QT, E])
        above, equal = m.sb("above", [P, QT, E, E]), m.sb("equal", [P, QT, E, E])
        rank, chosen, total = m.sb("rank", [P, QT, E]), m.sb("chosen", [P, QT, E]), m.sb("total", [P, QT])
        X_bank = [m.bank(f"X_bank{i}") for i in range(2)]
        L_bank = m.bank("L_bank")

        tabs_in, eps_ok = m.sem("tabs_in"), m.sem("eps_ok")
        h_loaded = [m.sem(f"h_loaded{j}") for j in range(QT)]
        squared, std_ok, nrm = m.sem("squared"), m.sem("std_ok"), m.sem("nrm")
        xt_done, xt_hi, xt_lo, l_done, grown, sel = m.sem("xt_done"), m.sem("xt_hi"), m.sem("xt_lo"), m.sem("l_done"), m.sem("grown"), m.sem("sel")
        waited = m.sem("waited")
        block = ctx.enter_context(nc.Block())
        NRM = 4
        SEL = 12

        def older(n):
            return max(n - 1, 0)

        @block.sync
        def _(sp):
            sp.dma_start(ln2[:], ln2_dram.partition_broadcast(P)).then_inc(tabs_in, 16)
            sp.dma_start(Wr[:], router_dram.rearrange("(t p) e -> p t e", p=P)).then_inc(tabs_in, 16)
            sp.dma_start(rbias[:], rbias_dram.partition_broadcast(P)).then_inc(tabs_in, 16)
            sp.dma_start(before[:], before_dram.partition_broadcast(P)).then_inc(tabs_in, 16)
            with sp.Fori(0, BATCH) as b:
                for j in range(QT):
                    sp.wait_ge(nrm, b * (NRM * QT))
                    sp.dma_start(h_in[j][:], h_dram[:, bass.ds(b * QT + j, 1)].rearrange("p o d -> p (o d)")).then_inc(h_loaded[j], 16)
            for j in range(QT):
                sp.wait_ge(h_loaded[j], 16 * BATCH)

        @block.tensor
        def _(pe):
            pe.wait_ge(const_ready, 32)
            pe.wait_ge(tabs_in, 64)
            with pe.Fori(0, BATCH) as b:
                for s in range(QT + 1):
                    if s < QT:
                        j = s
                        pe.wait_ge(nrm, b * (NRM * QT) + NRM * j + 3)
                        pe.wait_ge(xt_lo, b * (2 * QT) + 2 * older(j))
                        for t in range(DT):
                            mm = pe.transpose(X_bank[j % 2][:, bass.ts(t, P)], XN[j % 2][:, bass.ts(t, P)], ident[:])
                        mm.then_inc(xt_done, 1)
                    if s >= 1:
                        j = s - 1
                        pe.wait_ge(xt_lo, b * (2 * QT) + 2 * j + 2)
                        if j == 0:
                            pe.wait_ge(grown, b)
                            pe.wait_ge(sel, b * SEL)
                        for t in range(DT):
                            mm = pe.matmul(L_bank[:, bass.ts(j, E)], XT[j % 2][:, bass.ts(t, P)], Wr[:, t], start=t == 0, stop=t == DT - 1)
                        mm.then_inc(l_done, 1)

        @block.scalar
        def _(act):
            act.wait_ge(eps_ok, 1)
            with act.Fori(0, BATCH) as b:
                for j in range(QT):
                    n = b * QT + j
                    act.wait_ge(eps_ok, 1)
                    act.wait_ge(std_ok, n)
                    act.activation(unused[:], H[:, bass.ds(n, 1)].rearrange("p o d -> p (o d)"), ACT.Square, accum_out=ssx[:]).then_inc(squared, 1)
                    act.wait_ge(squared, n + 1)
                    act.activation(std[:], ssx[:], ACT.Sqrt, bias=eps[:, 0:1], scale=1.0 / D).then_inc(std_ok, 1)
                    act.wait_ge(eps_ok, 1)
                    act.wait_ge(xt_done, n + 1)
                    act.copy(T_h[:, :, bass.ds(n * P, P)], X_bank[j % 2][:].rearrange("p (t n) -> p t n", n=P)).then_inc(xt_hi, 1)
                act.wait_ge(l_done, b * QT + QT)
                act.wait_ge(sel, b * SEL)
                act.activation(grow[:].rearrange("p j e -> p (j e)"), L_bank[:, 0:QT * E], ACT.Exp, scale=-1.0).then_inc(grown, 1)

        @block.vector
        def _(dve):
            dve.memset(eps[:], RMS_EPS).then_inc(eps_ok, 1)
            dve.wait_ge(tabs_in, 64)

            def normalise(b, j):
                n = b * QT + j
                k = b * (NRM * QT) + NRM * j
                x = H[:, bass.ds(n, 1)].rearrange("p o d -> p (o d)")
                dve.wait_ge(std_ok, n + 1)
                dve.wait_ge(nrm, k)
                dve.reciprocal(rstd[:], std[:]).then_inc(nrm, 1)
                dve.wait_ge(xt_done, b * QT + older(j))
                dve.wait_ge(nrm, k + 1)
                dve.tensor_scalar(XN[j % 2][:], x, rstd[:, 0:1], None, ALU.mult).then_inc(nrm, 1)
                dve.wait_ge(nrm, k + 2)
                dve.tensor_tensor(XN[j % 2][:], XN[j % 2][:], ln2[:], ALU.mult).then_inc(nrm, 1)
                dve.wait_ge(h_loaded[j], b * 16 + 16)
                dve.tensor_tensor(x, x, h_in[j][:], ALU.add).then_inc(nrm, 1)

            def lower(b, j):
                n = b * QT + j
                w = bass.ds(n * P, P)
                x = X_bank[j % 2][:].rearrange("p (t n) -> p t n", n=P)
                dve.wait_ge(xt_hi, n + 1)
                dve.tensor_tensor(T_l[:, :, w], x, T_h[:, :, w].bitcast(F32), ALU.subtract).then_inc(xt_lo, 1)
                dve.wait_ge(l_done, b * QT + older(j))
                dve.tensor_copy(XT[j % 2][:], X_bank[j % 2][:]).then_inc(xt_lo, 1)

            def select(b):
                n = b * SEL
                by_e = lambda x: x[:].unsqueeze(3).to_broadcast([P, QT, E, E])
                by_f = lambda x: x[:].unsqueeze(2).to_broadcast([P, QT, E, E])
                dve.wait_ge(grown, b + 1)
                dve.tensor_scalar(grow[:], grow[:], 1.0, None, ALU.add).then_inc(sel, 1)
                dve.wait_ge(sel, n + 1)
                dve.reciprocal(sig[:], grow[:]).then_inc(sel, 1)
                dve.wait_ge(sel, n + 2)
                dve.tensor_tensor(score[:], sig[:], rbias[:].unsqueeze(1).to_broadcast([P, QT, E]), ALU.add).then_inc(sel, 1)
                dve.wait_ge(sel, n + 3)
                dve.tensor_tensor(above[:], by_f(score), by_e(score), ALU.is_gt).then_inc(sel, 1)
                dve.tensor_tensor(equal[:], by_f(score), by_e(score), ALU.is_equal).then_inc(sel, 1)
                dve.wait_ge(sel, n + 5)
                for j in range(QT):
                    last = dve.tensor_tensor(equal[:, j], equal[:, j], before[:], ALU.mult)
                last.then_inc(sel, 1)
                dve.wait_ge(sel, n + 6)
                dve.tensor_tensor(above[:], above[:], equal[:], ALU.add).then_inc(sel, 1)
                dve.wait_ge(sel, n + 7)
                dve.reduce_sum(rank[:], above[:], AX_X).then_inc(sel, 1)
                dve.wait_ge(sel, n + 8)
                dve.scalar_tensor_tensor(out=chosen[:], in0=rank[:], scalar=TOPK - 0.5, in1=sig[:], op0=ALU.is_lt, op1=ALU.mult).then_inc(sel, 1)
                dve.wait_ge(sel, n + 9)
                dve.reduce_sum(total[:], chosen[:], AX_X).then_inc(sel, 1)
                dve.wait_ge(sel, n + 10)
                dve.reciprocal(total[:], total[:]).then_inc(sel, 1)
                dve.wait_ge(sel, n + 11)
                dve.tensor_tensor(comb[:, :, bass.ds(b * QT, QT)].rearrange("p e j -> p j e"), chosen[:],
                                  total[:].unsqueeze(2).to_broadcast([P, QT, E]), ALU.mult).then_inc(sel, 1)

            with dve.Fori(0, BATCH) as b:
                for s in range(QT + 1):
                    if s < QT:
                        normalise(b, s)
                    if s >= 1:
                        lower(b, s - 1)
                select(b)


def experts(nc, H, T_h, T_l, comb, out, wg_dram, wu_dram, wd_dram):
    E, I = 8, 256
    IT = I // P
    CHUNKS = TILES * P // 512
    CT = TILES // CHUNKS
    PAIR = 2
    U = PAIR * CHUNKS

    with ExitStack() as ctx:
        m = Stage(nc, ctx, "ex")
        Win = m.sb("Win", [P, DT, 2 * I])
        Wdin = m.sb("Wdin", [P, IT, D])
        W_h = [m.sb(f"W_h{i}", [P, DT, 2 * I], F32R) for i in range(PAIR)]
        W_l = [m.sb(f"W_l{i}", [P, DT, 2 * I], F32R) for i in range(PAIR)]
        Wd_h = [m.sb(f"Wd_h{i}", [P, IT, D], F32R) for i in range(PAIR)]
        Wd_l = [m.sb(f"Wd_l{i}", [P, IT, D], F32R) for i in range(PAIR)]
        gate = [m.sb(f"gate{i}", [P, 512]) for i in range(IT)]
        act_ = [m.sb(f"act{i}", [P, 512]) for i in range(IT)]
        A_h = [m.sb(f"A_h{i}", [P, IT, 512], F32R) for i in range(2)]
        A_l = [m.sb(f"A_l{i}", [P, IT, 512], F32R) for i in range(2)]
        G_bank = [m.bank(f"G_bank{i}") for i in range(IT)]
        U_bank = [m.bank(f"U_bank{i}") for i in range(IT)]
        Y_bank = [m.bank(f"Y_bank{i}") for i in range(4)]

        w_in, wd_in = [m.sem(f"w_in{i}") for i in range(2)], m.sem("wd_in")
        w_hi, w_lo = m.sem("w_hi"), m.sem("w_lo")
        g_done, u_done, gated, acted, a_hi, a_lo = (m.sem(x) for x in ("g_done", "u_done", "gated", "acted", "a_hi", "a_lo"))
        y_done, added, stored = m.sem("y_done"), m.sem("added"), m.sem("stored")
        waited = m.sem("waited")
        block = ctx.enter_context(nc.Block())
        NY = U * CT
        NEXT = {1: 1, CHUNKS + 1: 2}

        def older(n):
            return max(n - 1, 0)

        @block.sync
        def _(sp):
            with sp.Fori(0, E + 1) as e:
                sp.wait_ge(w_lo, e * 2)
                for i, w in enumerate((wg_dram, wu_dram)):
                    sp.dma_start(Win[:, :, bass.ts(i, I)], w[bass.ds(e % E, 1)].rearrange("o (t p) i -> p (o t) i", p=P)).then_inc(w_in[i], 16)
                sp.dma_start(Wdin[:], wd_dram[bass.ds(e % E, 1)].rearrange("o (t p) n -> p (o t) n", p=P)).then_inc(wd_in, 16)
            for in_sem in (*w_in, wd_in):
                sp.wait_ge(in_sem, 16 * (E + 1))
            for c in range(CHUNKS):
                sp.wait_ge(added, (E - 1) * TILES + CT * (c + 1))
                sp.dma_start(out[bass.ts(c, 512)].rearrange("(t p) d -> p t d", p=P), H[:, bass.ts(c, CT)]).then_inc(stored, 16)
            sp.wait_ge(stored, 16 * CHUNKS)

        @block.gpsimd
        def _(pool):
            def halve(e, x):
                pool.wait_ge(w_hi, e * 2 + 1)
                pool.tensor_tensor(W_l[x][:], Win[:], W_h[x][:].bitcast(F32), ALU.subtract).then_inc(w_lo, 1)
                pool.wait_ge(w_hi, e * 2 + 2)
                pool.tensor_tensor(Wd_l[x][:], Wdin[:], Wd_h[x][:].bitcast(F32), ALU.subtract).then_inc(w_lo, 1)

            def lower(u, n):
                for i in range(IT):
                    pool.wait_ge(a_hi, n * IT + i + 1)
                    pool.tensor_tensor(A_l[u % 2][:, i], act_[i][:], A_h[u % 2][:, i].bitcast(F32), ALU.subtract).then_inc(a_lo, 1)

            halve(0, 0)
            with pool.Fori(0, E // PAIR) as k:
                for u in range(U):
                    lower(u, k * U + u)
                    if u in NEXT:
                        halve(k * PAIR + NEXT[u], NEXT[u] % PAIR)

        @block.scalar
        def _(act):
            def halve(k, x):
                e, y = k * PAIR + x, x % PAIR
                act.wait_ge(w_in[0], e * 16 + 16)
                act.wait_ge(w_in[1], e * 16 + 16)
                act.copy(W_h[y][:], Win[:]).then_inc(w_hi, 1)
                act.wait_ge(wd_in, e * 16 + 16)
                act.copy(Wd_h[y][:], Wdin[:]).then_inc(w_hi, 1)

            halve(0, 0)
            with act.Fori(0, E // PAIR) as k:
                for u in range(U):
                    for i in range(IT):
                        act.wait_ge(acted, k * (U * IT) + older(u * IT + i))
                        act.wait_ge(g_done, k * (U * IT) + u * IT + i + 1)
                        act.activation(gate[i][:], G_bank[i][:], ACT.Silu).then_inc(gated, 1)
                    act.wait_ge(y_done, k * NY + CT * max(u - 1, 0))
                    for i in range(IT):
                        act.wait_ge(acted, k * (U * IT) + u * IT + i + 1)
                        act.copy(A_h[u % 2][:, i], act_[i][:]).then_inc(a_hi, 1)
                    if u in NEXT:
                        act.wait_ge(y_done, k * NY + (CT * CHUNKS if u > CHUNKS else 0))
                        halve(k, NEXT[u])

        @block.vector
        def _(dve):
            def accumulate(k, u):
                x, c = u // CHUNKS, u % CHUNKS
                for j in range(CT):
                    t = c * CT + j
                    w = comb[:, bass.ds(k * PAIR + x, 1), t:t + 1].rearrange("p o t -> p (o t)")
                    dve.wait_ge(y_done, k * NY + u * CT + j + 1)
                    dve.scalar_tensor_tensor(out=H[:, t], in0=Y_bank[j][:], scalar=w, in1=H[:, t], op0=ALU.mult, op1=ALU.add).then_inc(added, 1)

            with dve.Fori(0, E // PAIR) as k:
                for u in range(U + 1):
                    if u < U:
                        for i in range(IT):
                            dve.wait_ge(a_lo, k * (U * IT) + older(u * IT + i))
                            dve.wait_ge(u_done, k * (U * IT) + u * IT + i + 1)
                            dve.wait_ge(gated, k * (U * IT) + u * IT + i + 1)
                            dve.tensor_tensor(act_[i][:], U_bank[i][:], gate[i][:], ALU.mult).then_inc(acted, 1)
                    if u >= 1:
                        accumulate(k, u - 1)

        @block.tensor
        def _(pe):
            def gate_up(k, u):
                x, c = u // CHUNKS, u % CHUNKS
                w = bass.ts(c, 512)
                if c == 0:
                    pe.wait_ge(w_lo, k * (2 * PAIR) + 2 * x + 2)
                for i in range(IT):
                    for n, (bank, done, free) in enumerate(((G_bank, g_done, gated), (U_bank, u_done, acted))):
                        pe.wait_ge(free, k * (U * IT) + older(u * IT + i))
                        ic = slice(n * I + i * P, n * I + (i + 1) * P)
                        for t in range(DT):
                            mm = product(pe, bank[i][:], (W_h[x][:, t, ic], W_l[x][:, t, ic]), (T_h[:, t, w], T_l[:, t, w]),
                                         t == 0, t == DT - 1)
                        mm.then_inc(done, 1)

            def down(k, u):
                x = u // CHUNKS
                pe.wait_ge(a_lo, k * (U * IT) + u * IT + IT)
                for j in range(CT):
                    pe.wait_ge(added, k * NY + max(u * CT + j + 1 - CT, 0))
                    for i in range(IT):
                        mm = product(pe, Y_bank[j][:], (A_h[u % 2][:, i, bass.ts(j, P)], A_l[u % 2][:, i, bass.ts(j, P)]),
                                     (Wd_h[x][:, i], Wd_l[x][:, i]), i == 0, i == IT - 1)
                    mm.then_inc(y_done, 1)

            with pe.Fori(0, E // PAIR) as k:
                for u in range(U + 1):
                    if u < U:
                        gate_up(k, u)
                    if u >= 1:
                        down(k, u - 1)


def bass_lm_tower(nc, ids, tok_w, attn_w, attn_b, attn_wo, ln1, ln2, blk_w, blk_norm, blk_wo, router, rbias, wg, wu, wd,
                  pos, iota, ident_d, mask_d, cos32, sin32, cos64, sin64, before, out):
    h_dram = nc.dram_tensor("h_saved", [P, TILES, D], F32, kind="Internal").ap()
    q_dram = nc.dram_tensor("q_rows", [16, SEQ, 512], F32, kind="Internal").ap()
    k_dram = nc.dram_tensor("k_rows", [16, SEQ, 128], F32, kind="Internal").ap()
    v_dram = nc.dram_tensor("v_rows", [16, SEQ, 128], F32, kind="Internal").ap()
    with ExitStack() as ctx:
        H = ctx.enter_context(nc.sbuf_tensor("H", [P, TILES, D], F32))
        ident = ctx.enter_context(nc.sbuf_tensor("ident", [P, P], F32))
        mask = ctx.enter_context(nc.sbuf_tensor("mask", [P, SEQ], F32))
        const_ready = ctx.enter_context(nc.semaphore("const_ready"))
        with nc.Block() as block:
            @block.sync
            def _(sp):
                sp.dma_start(ident[:], ident_d).then_inc(const_ready, 16)
                sp.dma_start(mask[:], mask_d).then_inc(const_ready, 16)
        const = ident, mask, const_ready
        token_stage(nc, H, const, tok_w, ids, pos, iota)
        with nc.sbuf_tensor("QKV", [P, TILES, 640], F32) as QKV:
            attn_project(nc, H, const, QKV, attn_w, attn_b, cos32, sin32)
            attn_attend(nc, H, const, QKV, attn_wo)
        block_project(nc, H, const, h_dram, q_dram, k_dram, v_dram, blk_w, ln1, blk_norm, cos64, sin64)
        block_attend(nc, H, const, q_dram, k_dram, v_dram, blk_wo)
        with (nc.sbuf_tensor("T_h", [P, DT, TILES * P], F32R) as T_h, nc.sbuf_tensor("T_l", [P, DT, TILES * P], F32R) as T_l,
              nc.sbuf_tensor("comb", [P, 8, TILES], F32) as comb):
            route(nc, H, const, h_dram, T_h, T_l, comb, ln2, router, rbias, before)
            experts(nc, H, T_h, T_l, comb, out, wg, wu, wd)


def tables():
    f = np.float32
    half = np.arange(0, D, 2, dtype=f)
    div = np.exp(-(np.log(f(10000.0)) / f(D)) * half).astype(f)
    ang = np.arange(SEQ, dtype=f)[:, None] * div
    pos = np.zeros((SEQ, D), f)
    pos[:, 0::2], pos[:, 1::2] = np.sin(ang), np.cos(ang)
    mask = np.zeros((P, SEQ), f)
    mask[:, SEQ - P:] = np.where(np.arange(P)[None, :] > np.arange(P)[:, None], f(MASKED), f(0))
    def angles(dim, theta):
        i = np.arange(dim // 2, dtype=f)
        if theta == 1e4:
            inv = f(theta) ** (-i / f(dim // 2))
        else:
            inv = f(1) / f(theta) ** (np.arange(0, dim, 2, dtype=f) / f(dim))
        a = np.arange(SEQ, dtype=f)[:, None] * inv.astype(f)[None]
        c, s = np.cos(a), np.sin(a)
        return np.concatenate([c, c], 1), np.concatenate([-s, s], 1)

    cos32, sin32 = angles(32, 1e4)
    cos64, sin64 = angles(64, 1e6)
    return {"cos32": cos32, "sin32": sin32, "cos64": cos64, "sin64": sin64, "pos": pos, "iota": np.tile(np.arange(D, dtype=f), (P, 1)), "ident": np.eye(P, dtype=f), "mask": mask,
            "before": (np.arange(8)[None, :] < np.arange(8)[:, None]).astype(f)}


def kernel(**inputs):
    import concourse.bacc as _bacc
    from concourse.bass_utils import run_bass_kernel_spmd as _run

    x = {k: np.asarray(v) for k, v in inputs.items()}
    c = tables()
    cat, flat = np.concatenate, np.ascontiguousarray
    arrays = {
        "ids": flat(x["x"].reshape(TILES, P).T),
        "tok_w": cat([x["L0_tok_Wq"], x["L0_tok_Wk"]], 2),
        "attn_w": flat(cat([x["L0_attn_wq"], x["L0_attn_wk"], x["L0_attn_wv"]], 0).T),
        "attn_b": cat([x["L0_attn_bq"], x["L0_attn_bk"], x["L0_attn_bv"]]),
        "attn_wo": flat(x["L0_attn_wo"].T),
        "ln1": x["L0_ffn_ln1_w"],
        "ln2": x["L0_ffn_ln2_w"],
        "blk_w": cat([x["L0_ffn_wq"], x["L0_ffn_wk"], x["L0_ffn_wv"]], 1),
        "blk_norm": cat([x["L0_ffn_qnorm_w"], x["L0_ffn_knorm_w"]]),
        "blk_wo": x["L0_ffn_wo"],
        "router": x["L0_ffn_router_w"],
        "rbias": x["L0_ffn_router_bias"],
        "wg": x["L0_ffn_wg"],
        "wu": x["L0_ffn_wu"],
        "wd": x["L0_ffn_wd"],
    }
    arrays |= {k: c[k] for k in ("pos", "iota", "ident", "mask", "cos32", "sin32", "cos64", "sin64", "before")}
    nc = _bacc.Bacc("TRN2", target_bir_lowering=False, num_devices=1)
    args = [nc.dram_tensor(f"in_{k}", a.shape, mybir.dt.from_np(a.dtype), kind="ExternalInput").ap() for k, a in arrays.items()]
    out = nc.dram_tensor("out", [TILES * P, D], F32, kind="ExternalOutput").ap()
    bass_lm_tower(nc, *args, out)
    r = _run(nc, [{f"in_{k}": a for k, a in arrays.items()}], core_ids=[0])
    return r.results[0]["out"].reshape(BATCH, SEQ, D)
```

```python
from contextlib import ExitStack

import concourse.bass as bass
import numpy as np
from concourse import mybir

F32 = mybir.dt.float32
F32R = mybir.dt.float32r
I32 = mybir.dt.int32
ALU = mybir.AluOpType
ACT = mybir.ActivationFunctionType
AX_X = mybir.AxisListType.X

P = 128
BATCH, SEQ, D = 4, 512, 512
QT = SEQ // P
DT = D // P
TILES = BATCH * QT
MASKED = -1e30

TOK_LAYERS, TOK_DQK = 4, 128


class Stage:

    def __init__(self, nc, ctx, stage):
        self.nc, self.ctx, self.stage = nc, ctx, stage

    def sb(self, name, shape, dt=F32):
        return self.ctx.enter_context(self.nc.sbuf_tensor(f"{self.stage}_{name}", shape, dt))

    def bank(self, name):
        return self.ctx.enter_context(self.nc.psum_tensor(f"{self.stage}_{name}", [P, 512], F32))

    def sem(self, name):
        return self.ctx.enter_context(self.nc.semaphore(f"{self.stage}_{name}"))


def product(pe, out, a, b, start, stop):
    (a_h, a_l), (b_h, b_l) = a, b
    pe.matmul(out, a_l, b_h, start=start, stop=False)
    pe.matmul(out, a_h, b_l, start=False, stop=False)
    return pe.matmul(out, a_h, b_h, start=False, stop=stop)


def token_stage(nc, H, const, tok_w, ids_dram, pe_dram, iota_dram):
    SCALE = float(TOK_DQK) ** -0.5
    U = BATCH * QT
    XS = DT + 2
    NR = 8
    ident, mask, const_ready = const

    LEAD, TURN, APPLY = 6, 3, 1
    X_USES = ((0, 1), (2, 3), (DT,), (DT + 1,))
    NEXT_WEIGHTS = 6

    def sequence(w):
        return w // QT % BATCH

    def tile(w):
        return QT - 1 - w % QT

    def positive(n):
        return max(n, 0) if isinstance(n, int) else n

    with ExitStack() as ctx:
        m = Stage(nc, ctx, "tok")
        E_h = m.sb("E_h", [P, TILES, D], F32R)
        E_l = m.sb("E_l", [P, TILES, D], F32R)
        ET_h = [m.sb(f"ET_h{i}", [P, DT, SEQ], F32R) for i in range(2)]
        ET_l = [m.sb(f"ET_l{i}", [P, DT, SEQ], F32R) for i in range(2)]
        QK_h = [m.sb(f"QK_h{i}", [P, 2, SEQ], F32R) for i in range(2)]
        QK_l = [m.sb(f"QK_l{i}", [P, 2, SEQ], F32R) for i in range(2)]
        W = m.sb("W", [P, TOK_LAYERS, DT, 2 * TOK_DQK])
        W_h = m.sb("W_h", [P, DT, 2 * TOK_DQK], F32R)
        W_l = m.sb("W_l", [P, DT, 2 * TOK_DQK], F32R)
        Pr = m.sb("Pr", [P, 4, SEQ])
        pos = Pr
        PT_h = [m.sb(f"PT_h{i}", [P, SEQ], F32R) for i in range(4)]
        PT_l = [m.sb(f"PT_l{i}", [P, SEQ], F32R) for i in range(4)]
        least, den, rden = m.sb("least", [P, NR]), m.sb("den", [P, NR]), m.sb("rden", [P, NR])
        ids_i = m.sb("ids_i", [P, TILES], I32)
        ids_f = m.sb("ids_f", [P, TILES])
        iota = m.sb("iota", [P, D])

        S_bank = [m.bank(f"S_bank{i}") for i in range(2)]
        T_bank = [m.bank(f"T_bank{i}") for i in range(2)]
        O_bank = [m.bank(f"O_bank{i}") for i in range(2)]
        X_bank = [m.bank(f"X_bank{i}") for i in range(2)]

        in_ids, in_tabs, w0_in, w_in = m.sem("in_ids"), m.sem("in_tabs"), m.sem("w0_in"), m.sem("w_in")
        w_hi, w_lo, ids_ok = m.sem("w_hi"), m.sem("w_lo"), m.sem("ids_ok")
        enc, enc_hi, enc_lo = m.sem("enc"), m.sem("enc_hi"), m.sem("enc_lo")
        x_done, x_hi, x_lo = m.sem("x_done"), m.sem("x_hi"), m.sem("x_lo")
        s_done, s_masked, p_done, rden_ok = m.sem("s_done"), m.sem("s_masked"), m.sem("p_done"), m.sem("rden_ok")
        pt_done, pt_hi, pt_lo, pv_done = m.sem("pt_done"), m.sem("pt_hi"), m.sem("pt_lo"), m.sem("pv_done")
        waited = m.sem("waited")
        block = ctx.enter_context(nc.Block())

        def width(w):
            return P * (tile(w) + 1)

        def x_uses(s):
            w = s + LEAD
            return [(w // QT + 1, x) for x in X_USES[w % QT]]

        @block.sync
        def _(sp):
            w_view = tok_w.rearrange("l (t p) n -> p l t n", p=P)
            sp.dma_start(ids_i[:], ids_dram).then_inc(in_ids, 16)
            sp.dma_start(iota[:], iota_dram).then_inc(in_tabs, 16)
            sp.dma_start(pos[:], pe_dram.rearrange("(j p) d -> p j d", p=P)).then_inc(in_tabs, 16)
            sp.dma_start(W[:, 0:1], w_view[:, 0:1]).then_inc(w0_in, 16)
            sp.dma_start(W[:, 1:], w_view[:, 1:]).then_inc(w_in, 16)

        @block.gpsimd
        def _(pool):
            def split_weights(n, l):
                pool.wait_ge(w_hi, n)
                pool.tensor_tensor(W_l[:].unsqueeze(1), W[:, bass.ds(l, 1)], W_h[:].unsqueeze(1).bitcast(F32), ALU.subtract)\
                    .then_inc(w_lo, 1)

            def lower(n, t):
                pool.wait_ge(enc, n)
                pool.wait_ge(enc_hi, n)
                pool.tensor_tensor(E_l[:, t], H[:, t], E_h[:, t].bitcast(F32), ALU.subtract).then_inc(enc_lo, 1)

            split_weights(1, 0)
            for t in range(TILES):
                lower(t + 1, t)
            pool.wait_ge(w_in, 16)
            with pool.Fori(0, TOK_LAYERS) as l:
                for s in range(U):
                    if s == NEXT_WEIGHTS:
                        split_weights(l + 2, (l + 1) % TOK_LAYERS)
                    lower(l * U + TILES + s + 1, sequence(s) * QT + tile(s))

        @block.tensor
        def _(pe):
            pe.wait_ge(const_ready, 32)

            def x_use(l, sq, x):
                n = (l * BATCH + sq) * XS + x
                b = sq % BATCH
                if x < DT:
                    pe.wait_ge(enc, l * U + QT * (sq + 1))
                    pe.wait_ge(x_lo, positive(n - 1))
                    for j in range(QT):
                        mm = pe.transpose(X_bank[x % 2][:, bass.ts(j, P)], H[:, b * QT + j, bass.ts(x, P)], ident[:])
                else:
                    pe.wait_ge(w_lo, l + sq // BATCH + 1)
                    pe.wait_ge(x_lo, n - x + DT)
                    c = bass.ts(x - DT, TOK_DQK)
                    for t in range(DT):
                        mm = product(pe, X_bank[x % 2][:], (W_h[:, t, c], W_l[:, t, c]), (ET_h[b % 2][:, t], ET_l[b % 2][:, t]),
                                     t == 0, t == DT - 1)
                mm.then_inc(x_done, 1)

            def score(l, w):
                b, q, n = sequence(w), tile(w), width(w)
                pe.wait_ge(x_lo, (l * BATCH + w // QT + 1) * XS)
                pe.wait_ge(s_masked, positive(l * U + w - 1))
                product(pe, S_bank[w % 2][:, 0:n], (QK_h[b % 2][:, 0, bass.ts(q, P)], QK_l[b % 2][:, 0, bass.ts(q, P)]),
                        (QK_h[b % 2][:, 1, 0:n], QK_l[b % 2][:, 1, 0:n]), True, True).then_inc(s_done, 1)

            def turn(l, w):
                pe.wait_ge(p_done, l * U + w + 1)
                pe.wait_ge(pt_lo, positive(l * U + w - 1))
                for k in range(tile(w) + 1):
                    mm = pe.transpose(T_bank[w % 2][:, bass.ts(k, P)], Pr[:, w % 4, bass.ts(k, P)], ident[:])
                mm.then_inc(pt_done, 1)

            def apply(l, w):
                b, q = sequence(w), tile(w)
                pe.wait_ge(pt_lo, l * U + w + 1)
                pe.wait_ge(enc_lo, l * U + QT * (w // QT + 1))
                pe.wait_ge(enc, l * U + TILES + w - 1)
                pe.wait_ge(enc_hi, l * U + TILES + w - 1)
                for k in range(q + 1):
                    mm = product(pe, O_bank[w % 2][:], (PT_h[w % 4][:, bass.ts(k, P)], PT_l[w % 4][:, bass.ts(k, P)]),
                                 (E_h[:, b * QT + k], E_l[:, b * QT + k]), k == 0, k == q)
                mm.then_inc(pv_done, 1)

            def slot(l, s):
                score(l, s + LEAD)
                for sq, x in x_uses(s):
                    x_use(l, sq, x)
                if s + TURN >= 0:
                    turn(l, s + TURN)
                if s + APPLY >= 0:
                    apply(l, s + APPLY)

            for x in range(XS):
                x_use(0, 0, x)
            for s in range(-LEAD, 0):
                slot(0, s)
            with pe.Fori(0, TOK_LAYERS) as l:
                for s in range(U):
                    slot(l, s)

        def x_halves(sq, x):
            i = sq % BATCH % 2
            return (ET_h[i][:, x], ET_l[i][:, x]) if x < DT else (QK_h[i][:, x - DT], QK_l[i][:, x - DT])

        @block.scalar
        def _(act):
            act.wait_ge(w0_in, 16)
            act.copy(W_h[:], W[:, 0]).then_inc(w_hi, 1)
            for t in range(TILES):
                act.wait_ge(enc, t + 1)
                act.copy(E_h[:, t], H[:, t]).then_inc(enc_hi, 1)

            def take(l, sq, x):
                act.wait_ge(x_done, (l * BATCH + sq) * XS + x + 1)
                act.copy(x_halves(sq, x)[0], X_bank[x % 2][:]).then_inc(x_hi, 1)

            def exps(l, w):
                one, n = slice(w % NR, w % NR + 1), width(w)
                act.wait_ge(s_masked, l * U + w + 1)
                act.wait_ge(rden_ok, l * U + max(w - NR + 1, 0))
                act.activation(Pr[:, w % 4, 0:n], Pr[:, w % 4, 0:n], ACT.Exp, bias=least[:, one], scale=-1.0,
                               accum_out=den[:, one]).then_inc(p_done, 1)

            def turned(l, w):
                n = width(w)
                act.wait_ge(pt_done, l * U + w + 1)
                act.wait_ge(pv_done, positive(l * U + w - 3))
                act.copy(PT_h[w % 4][:, 0:n], T_bank[w % 2][:, 0:n]).then_inc(pt_hi, 1)

            def encoded(l, w):
                act.wait_ge(pv_done, l * U + w + 1)
                act.wait_ge(rden_ok, l * U + w + 1)
                act.activation(E_h[:, sequence(w) * QT + tile(w)], O_bank[w % 2][:], ACT.Copy,
                               scale=rden[:, w % NR:w % NR + 1]).then_inc(enc_hi, 1)

            def slot(l, s):
                if s + TURN >= 0:
                    turned(l, s + TURN)
                for sq, x in x_uses(s):
                    take(l, sq, x)
                if s == NEXT_WEIGHTS:
                    act.wait_ge(x_done, (l + 1) * BATCH * XS)
                    act.copy(W_h[:].unsqueeze(1), W[:, bass.ds((l + 1) % TOK_LAYERS, 1)]).then_inc(w_hi, 1)
                if s >= 0:
                    encoded(l, s)
                exps(l, s + LEAD)

            for x in range(XS):
                take(0, 0, x)
            for s in range(-LEAD, 0):
                slot(0, s)
            act.wait_ge(w_in, 16)
            with act.Fori(0, TOK_LAYERS) as l:
                for s in range(U):
                    slot(l, s)

        @block.vector
        def _(dve):
            dve.wait_ge(const_ready, 32)
            dve.wait_ge(in_ids, 16)
            dve.tensor_copy(ids_f[:], ids_i[:]).then_inc(ids_ok, 1)
            dve.wait_ge(ids_ok, 1)
            dve.wait_ge(in_tabs, 32)
            for t in range(TILES):
                dve.scalar_tensor_tensor(out=H[:, t], in0=iota[:], scalar=ids_f[:, t:t + 1], in1=pos[:, t % QT],
                                         op0=ALU.is_equal, op1=ALU.add).then_inc(enc, 1)
            dve.wait_ge(enc, TILES)

            def take(l, sq, x):
                h, lo = x_halves(sq, x)
                dve.wait_ge(x_hi, (l * BATCH + sq) * XS + x + 1)
                dve.tensor_tensor(lo, X_bank[x % 2][:], h.bitcast(F32), ALU.subtract).then_inc(x_lo, 1)

            def mask_scores(l, w):
                n = width(w)
                dve.wait_ge(s_done, l * U + w + 1)
                dve.wait_ge(pt_done, positive(l * U + w - 3))
                dve.sem_inc(waited, 1)
                dve.tensor_tensor_reduce(out=Pr[:, w % 4, 0:n], in0=S_bank[w % 2][:, 0:n], in1=mask[:, SEQ - n:SEQ],
                                         scale=-SCALE, scalar=-MASKED, op0=ALU.add, op1=ALU.min,
                                         accum_out=least[:, w % NR:w % NR + 1]).then_inc(s_masked, 1)

            def invert(l, w):
                one = slice(w % NR, w % NR + 1)
                dve.wait_ge(p_done, l * U + w + 1)
                dve.wait_ge(enc_hi, l * U + TILES + w - NR + 1)
                dve.reciprocal(rden[:, one], den[:, one]).then_inc(rden_ok, 1)

            def turned(l, w):
                n = width(w)
                dve.wait_ge(pt_hi, l * U + w + 1)
                dve.tensor_tensor(PT_l[w % 4][:, 0:n], T_bank[w % 2][:, 0:n], PT_h[w % 4][:, 0:n].bitcast(F32),
                                  ALU.subtract).then_inc(pt_lo, 1)

            def encoded(l, w):
                dve.wait_ge(rden_ok, l * U + w + 1)
                dve.wait_ge(enc_hi, l * U + TILES + w + 1)
                dve.tensor_scalar(H[:, sequence(w) * QT + tile(w)], O_bank[w % 2][:], rden[:, w % NR:w % NR + 1], None,
                                  ALU.mult).then_inc(enc, 1)

            def slot(l, s):
                mask_scores(l, s + LEAD)
                if s + TURN >= 0:
                    turned(l, s + TURN)
                for sq, x in x_uses(s):
                    take(l, sq, x)
                if s + LEAD - 1 >= 0:
                    invert(l, s + LEAD - 1)
                if s >= 0:
                    encoded(l, s)

            for x in range(XS):
                take(0, 0, x)
            for s in range(-LEAD, 0):
                slot(0, s)
            with dve.Fori(0, TOK_LAYERS) as l:
                for s in range(U):
                    slot(l, s)


def attn_project(nc, H, const, Q_jobs, K_jobs, V_jobs, w_dram, b_dram, cos_dram, sin_dram):
    HQ, HKV, DH = 16, 2, 32
    ROT = (HQ + HKV) * DH
    N = ROT + HKV * DH
    NQ = HQ * DH
    EPS = 1e-5
    ident, _, const_ready = const

    NORM, TURN, MULTIPLY, LEAVE = 4, 3, 2, 1

    def positive(n):
        return max(n, 0) if isinstance(n, int) else n

    with ExitStack() as ctx:
        m = Stage(nc, ctx, "ap")
        W = m.sb("W", [P, DT, N])
        W_h = m.sb("W_h", [P, DT, N], F32R)
        W_l = m.sb("W_l", [P, DT, N], F32R)
        bias = m.sb("bias", [P, N])
        cos = m.sb("cos", [P, QT, DH])
        sin = m.sb("sin", [P, QT, DH])
        XN = [m.sb(f"XN{i}", [P, D]) for i in range(2)]
        XT_h = [m.sb(f"XT_h{i}", [P, D], F32R) for i in range(2)]
        XT_l = [m.sb(f"XT_l{i}", [P, D], F32R) for i in range(2)]
        raw = [m.sb(f"raw{i}", [P, ROT]) for i in range(2)]
        rc = m.sb("rc", [P, ROT])
        rs = [m.sb(f"rs{i}", [P, ROT]) for i in range(2)]
        stat = m.sb("stat", [P, 6])
        mv = m.sb("mv", [P, 2])
        std = m.sb("std", [P, 1])
        rstd = m.sb("rstd", [P, 1])
        eps = m.sb("eps", [P, 1])
        X_bank = [m.bank(f"X_bank{i}") for i in range(2)]
        Q_bank = [m.bank(f"Q_bank{i}") for i in range(2)]
        KV_bank = [m.bank(f"KV_bank{i}") for i in range(2)]

        w_in, tabs_in, w_hi, w_lo = m.sem("w_in"), m.sem("tabs_in"), m.sem("w_hi"), m.sem("w_lo")
        eps_ok, ln, xt_done, xt_hi, xt_lo = m.sem("eps_ok"), m.sem("ln"), m.sem("xt_done"), m.sem("xt_hi"), m.sem("xt_lo")
        q_done, kv_done, biased = m.sem("q_done"), m.sem("kv_done"), m.sem("biased")
        std_ok, turned, cosed, roped = m.sem("std_ok"), m.sem("turned"), m.sem("cosed"), m.sem("roped")
        waited = m.sem("waited")
        block = ctx.enter_context(nc.Block())

        def sequence(b, n):
            return (b + n // QT) % BATCH if n >= QT else b

        def slots(fori, slot):
            for s in range(-NORM, 0):
                slot(0, s)
            with fori(0, BATCH) as b:
                for s in range(QT):
                    slot(b, s)

        @block.sync
        def _(sp):
            sp.dma_start(W[:], w_dram.rearrange("(t p) n -> p t n", p=P)).then_inc(w_in, 16)
            sp.dma_start(bias[:], b_dram.partition_broadcast(P)).then_inc(tabs_in, 16)
            sp.dma_start(cos[:], cos_dram.rearrange("(j p) d -> p j d", p=P)).then_inc(tabs_in, 16)
            sp.dma_start(sin[:], sin_dram.rearrange("(j p) d -> p j d", p=P)).then_inc(tabs_in, 16)

        @block.gpsimd
        def _(pool):
            pool.wait_ge(w_in, 16)
            pool.wait_ge(w_hi, 1)
            pool.tensor_tensor(W_l[:], W[:], W_h[:].bitcast(F32), ALU.subtract).then_inc(w_lo, 1)
            pool.wait_ge(tabs_in, 48)

            def turn(b, n):
                N_ = b * QT + n
                x = raw[n % 2][:].rearrange("p (h s c) -> p h s c", s=2, c=DH // 2)
                o = rs[n % 2][:].rearrange("p (h s c) -> p h s c", s=2, c=DH // 2)
                pool.wait_ge(biased, N_ * 3 + 3)
                pool.wait_ge(roped, positive(N_ - 1))
                for half in range(2):
                    sn = sin[:, n % QT, bass.ts(half, DH // 2)].unsqueeze(1).to_broadcast([P, HQ + HKV, DH // 2])
                    pool.tensor_tensor(o[:, :, half], x[:, :, 1 - half], sn, ALU.mult).then_inc(turned, 1)

            def slot(b, s):
                if s + LEAVE >= 0:
                    turn(b, s + LEAVE)

            slots(pool.Fori, slot)

        @block.tensor
        def _(pe):
            pe.wait_ge(const_ready, 32)

            def transposes(b, n):
                pe.wait_ge(ln, (b * QT + n) * 4 + 4)
                pe.wait_ge(xt_lo, positive(b * QT + n - 1))
                for t in range(DT):
                    mm = pe.transpose(X_bank[n % 2][:, bass.ts(t, P)], XN[n % 2][:, bass.ts(t, P)], ident[:])
                mm.then_inc(xt_done, 1)

            def products(b, n):
                pe.wait_ge(w_lo, 1)
                pe.wait_ge(xt_lo, b * QT + n + 1)
                pe.wait_ge(biased, positive((b * QT + n - 1) * 3))
                for bank, lo, hi, done in ((Q_bank, 0, NQ, q_done), (KV_bank, NQ, N, kv_done)):
                    for t in range(DT):
                        mm = product(pe, bank[n % 2][:, 0:hi - lo], (XT_h[n % 2][:, bass.ts(t, P)], XT_l[n % 2][:, bass.ts(t, P)]),
                                     (W_h[:, t, lo:hi], W_l[:, t, lo:hi]), t == 0, t == DT - 1)
                    mm.then_inc(done, 1)

            def slot(b, s):
                if s + TURN >= 0:
                    transposes(b, s + TURN)
                if s + MULTIPLY >= 0:
                    products(b, s + MULTIPLY)

            slots(pe.Fori, slot)

        @block.scalar
        def _(act):
            def deviation(b, n):
                act.wait_ge(ln, (b * QT + n) * 4 + 2)
                act.activation(std[:], mv[:, 1:2], ACT.Sqrt, bias=eps[:, 0:1]).then_inc(std_ok, 1)

            def upper(b, n):
                act.wait_ge(xt_done, b * QT + n + 1)
                act.wait_ge(kv_done, positive(b * QT + n - 1))
                act.copy(XT_h[n % 2][:], X_bank[n % 2][:]).then_inc(xt_hi, 1)

            def slot(b, s):
                if s + TURN >= 0:
                    upper(b, s + TURN)
                deviation(b, s + NORM)
                if s == -NORM:
                    act.wait_ge(w_in, 16)
                    act.copy(W_h[:], W[:]).then_inc(w_hi, 1)

            act.wait_ge(eps_ok, 1)
            slots(act.Fori, slot)

        @block.vector
        def _(dve):
            dve.memset(eps[:], EPS).then_inc(eps_ok, 1)
            dve.wait_ge(tabs_in, 48)

            def h_tile(b, n):
                return H[:, bass.ds(sequence(b, n) * QT + n % QT, 1)].rearrange("p o d -> p (o d)")

            def statistics(b, n):
                N4 = (b * QT + n) * 4
                dve.wait_ge(ln, N4)
                dve.bn_stats(stat[:], h_tile(b, n)).then_inc(ln, 1)
                dve.wait_ge(ln, N4 + 1)
                dve.sem_inc(waited, 1)
                dve.bn_aggr(mv[:], stat[:]).then_inc(ln, 1)

            def normalise(b, n):
                N4 = (b * QT + n) * 4
                dve.wait_ge(std_ok, b * QT + n + 1)
                dve.reciprocal(rstd[:], std[:]).then_inc(ln, 1)
                dve.wait_ge(ln, N4 + 3)
                dve.wait_ge(xt_done, positive(b * QT + n - 1))
                dve.tensor_scalar(XN[n % 2][:], h_tile(b, n), mv[:, 0:1], rstd[:, 0:1], ALU.subtract, ALU.mult).then_inc(ln, 1)

            def lower(b, n):
                dve.wait_ge(xt_hi, b * QT + n + 1)
                dve.tensor_tensor(XT_l[n % 2][:], X_bank[n % 2][:], XT_h[n % 2][:].bitcast(F32), ALU.subtract).then_inc(xt_lo, 1)

            def by_job(x):
                return x.rearrange("p (g c) -> p g c", g=HKV)

            def leave(b, n):
                N_ = b * QT + n
                heads = lambda x: x.rearrange("p (h c) -> p h c", c=DH)
                jobs = bass.ds(sequence(b, n) * HKV, HKV)
                r = raw[n % 2]
                dve.wait_ge(q_done, N_ + 1)
                dve.wait_ge(turned, positive(N_ * 2 - 2))
                dve.wait_ge(cosed, positive(N_ - 1))
                dve.tensor_tensor(r[:, 0:NQ], Q_bank[n % 2][:], bias[:, 0:NQ], ALU.add).then_inc(biased, 1)
                dve.wait_ge(kv_done, N_ + 1)
                dve.tensor_tensor(r[:, NQ:ROT], KV_bank[n % 2][:, 0:ROT - NQ], bias[:, NQ:ROT], ALU.add).then_inc(biased, 1)
                dve.tensor_tensor(V_jobs[:, jobs, n % QT], by_job(KV_bank[n % 2][:, ROT - NQ:N - NQ]), by_job(bias[:, ROT:N]), ALU.add)\
                   .then_inc(biased, 1)
                dve.wait_ge(biased, N_ * 3 + 2)
                dve.wait_ge(roped, N_)
                dve.tensor_tensor(heads(rc[:]), heads(r[:]), cos[:, n % QT].unsqueeze(1).to_broadcast([P, HQ + HKV, DH]), ALU.mult)\
                   .then_inc(cosed, 1)

            def rotate(b, n):
                N_ = b * QT + n
                jobs = bass.ds(sequence(b, n) * HKV, HKV)
                dve.wait_ge(cosed, N_ + 1)
                dve.wait_ge(turned, N_ * 2 + 2)
                dve.tensor_tensor(Q_jobs[:, jobs, n % QT], by_job(rc[:, 0:NQ]), by_job(rs[n % 2][:, 0:NQ]), ALU.add)
                dve.tensor_tensor(K_jobs[:, jobs, n % QT], by_job(rc[:, NQ:]), by_job(rs[n % 2][:, NQ:]), ALU.add).then_inc(roped, 1)

            def slot(b, s):
                statistics(b, s + NORM)
                if s + TURN >= 0:
                    lower(b, s + TURN)
                if s >= 0:
                    rotate(b, s)
                normalise(b, s + NORM)
                if s + LEAVE >= 0:
                    leave(b, s + LEAVE)

            slots(dve.Fori, slot)


def attn_attend(nc, H, const, Q_jobs, K_jobs, V_jobs, wo_dram):
    HQ, HKV, DH = 16, 2, 32
    R = HQ // HKV
    SIDE = P // DH
    HALVES = R // SIDE
    SCALE = DH ** -0.5
    JOBS = BATCH * HKV
    U = R * QT
    ident, mask, const_ready = const

    LEAD, TURN = 14, 11
    KEY_TILES = {6: (0,), 7: (1,), 8: (2, 3)}
    O_HI, O_LO = 9, 10
    OUT_TILES = {27: 0, 28: 1, 29: 2, 30: 3}
    EVENTS = [(QT * h - 3, "q", h % R) for h in range(1, R + 1)] + [(U - 2, "k", 0)]
    NE = len(EVENTS)
    BEFORE = 2

    def positive(n):
        return max(n, 0) if isinstance(n, int) else n

    with ExitStack() as ctx:
        m = Stage(nc, ctx, "at")
        Wo = m.sb("Wo", [P, HQ // SIDE, D])
        Wo_h = m.sb("Wo_h", [P, HQ // SIDE, D], F32R)
        Wo_l = m.sb("Wo_l", [P, HQ // SIDE, D], F32R)
        q_in = [m.sb(f"q_in{i}", [P, QT, P], F32R) for i in range(2)]
        k_in = m.sb("k_in", [P, QT, P], F32R)
        V = m.sb("V", [P, QT, DH])
        Q_s = [m.sb(f"Q_s{i}", [P, SEQ], F32R) for i in range(2)]
        K_s = m.sb("K_s", [P, SEQ], F32R)
        Pr = [m.sb(f"Pr{i}", [P, SEQ]) for i in range(4)]
        PT = [m.sb(f"PT{i}", [P, SIDE, QT, SEQ]) for i in range(2)]
        O_h = m.sb("O_h", [P, HALVES, SEQ], F32R)
        O_l = m.sb("O_l", [P, HALVES, SEQ], F32R)
        least, den, rden = m.sb("least", [P, 4]), m.sb("den", [P, 4]), m.sb("rden", [P, 4])
        S_bank = [m.bank(f"S_bank{i}") for i in range(2)]
        T_bank = [m.bank(f"T_bank{i}") for i in range(2)]
        O_bank = m.bank("O_bank")
        X_bank = m.bank("X_bank")
        Y_bank = [m.bank(f"Y_bank{i}") for i in range(2)]

        w_in, w_hi, w_lo = m.sem("w_in"), m.sem("w_hi"), m.sem("w_lo")
        q_ready, k_ready, v_ready = m.sem("q_ready"), m.sem("k_ready"), m.sem("v_ready")
        stacked, op_done, op_ready = m.sem("stacked"), m.sem("op_done"), m.sem("op_ready")
        s_done, s_masked, p_done, rden_ok, p_norm = m.sem("s_done"), m.sem("s_masked"), m.sem("p_done"), m.sem("rden_ok"), m.sem("p_norm")
        pt_done, pt_ok, pv_done = m.sem("pt_done"), m.sem("pt_ok"), m.sem("pv_done")
        o_hi, o_lo, wo_done, added = m.sem("o_hi"), m.sem("o_lo"), m.sem("wo_done"), m.sem("added")
        waited = m.sem("waited")
        block = ctx.enter_context(nc.Block())

        def width(w):
            return P * (QT - w % QT)

        def events(s):
            far, unit = divmod(s + LEAD, U)
            return [(e, far, what, h) for e, (at, what, h) in enumerate(EVENTS) if at == unit]

        @block.sync
        def _(sp):
            sp.dma_start(Wo[:], wo_dram.rearrange("(g p) n -> p g n", p=P)).then_inc(w_in, 16)

        @block.gpsimd
        def _(pool):
            def bring(n, job, what, h):
                jobs, rows = (Q_jobs, q_in[h % 2]) if what == "q" else (K_jobs, k_in)
                src = jobs[:, bass.ds(job, 1), :, bass.ts(h, DH)].rearrange("p o j c -> p (o j) c")
                src = src.unsqueeze(2).to_broadcast([P, QT, 2, DH])
                if what == "q":
                    r = rows[:].rearrange("p j (s r c) -> p j s r c", s=2, c=DH)
                    hi, lo = r[:, :, 0], r[:, :, 1]
                else:
                    r = rows[:].rearrange("p j (r s c) -> p j r s c", s=2, c=DH)
                    hi, lo = r[:, :, :, 0], r[:, :, :, 1]
                pool.tensor_copy(hi, src).then_inc(stacked, 1)
                pool.wait_ge(stacked, n)
                pool.sem_inc(waited, 1)
                pool.tensor_tensor(lo, src, hi.bitcast(F32), ALU.subtract).then_inc(q_ready if what == "q" else k_ready, 1)

            def slot(i, s):
                for e, far, what, h in events(s):
                    before = BEFORE if what == "k" else R if h == 0 else h if h >= 3 else h - 1
                    pool.wait_ge(op_done, positive((i + far) * NE + before))
                    job = i + far + (h == 0)
                    if not isinstance(job, int):
                        job = job % JOBS
                    bring((i + far) * NE + BEFORE + e + 1, job, what, h)

            bring(1, 0, "q", 0)
            bring(2, 0, "k", 0)
            pool.wait_ge(w_in, 16)
            pool.wait_ge(w_hi, 1)
            pool.tensor_tensor(Wo_l[:], Wo[:], Wo_h[:].bitcast(F32), ALU.subtract).then_inc(w_lo, 1)
            for s in range(-LEAD, 0):
                slot(0, s)
            with pool.Fori(0, JOBS) as i:
                pool.wait_ge(pv_done, i * HALVES)
                pool.tensor_copy(V[:].unsqueeze(1), V_jobs[:, bass.ds(i, 1)]).then_inc(v_ready, 1)
                for s in range(U):
                    slot(i, s)

        @block.tensor
        def _(pe):
            pe.wait_ge(const_ready, 32)

            def transposed(src):
                for j in range(QT):
                    mm = pe.transpose(X_bank[:, bass.ts(j, P)], src[:, j].bitcast(F32), ident[:])
                mm.then_inc(op_done, 1)

            def operand(i, e, what, h):
                if what == "k":
                    pe.wait_ge(k_ready, i + 2)
                else:
                    pe.wait_ge(q_ready, i * R + (h or R) + 1)
                pe.wait_ge(op_ready, i * NE + BEFORE + e)
                transposed(k_in if what == "k" else q_in[h % 2])

            def score(i, w):
                h, q = w // QT % R, QT - 1 - w % QT
                n = width(w)
                pe.wait_ge(op_ready, (i + w // U) * NE + BEFORE + h)
                pe.wait_ge(s_masked, positive(i * U + w - 1))
                pe.matmul(S_bank[w % 2][:, 0:n], Q_s[h % 2][:, bass.ts(q, P)], K_s[:, 0:n], start=True, stop=True)\
                  .then_inc(s_done, 1)

            def turn(i, w):
                pe.wait_ge(p_norm, i * U + w + 1)
                pe.wait_ge(pt_ok, positive(i * U + w - 1))
                for k in range(width(w) // P):
                    mm = pe.transpose(T_bank[w % 2][:, bass.ts(k, P)], Pr[w % 4][:, bass.ts(k, P)], ident[:])
                mm.then_inc(pt_done, 1)

            def apply(i, f, k):
                if k == 0:
                    pe.wait_ge(pt_ok, i * U + (f + 1) * SIDE * QT)
                    pe.wait_ge(v_ready, i + 1)
                    pe.wait_ge(o_lo, i * HALVES + f)
                for r in range(SIDE):
                    mm = pe.matmul(O_bank[r * DH:(r + 1) * DH, k * P:], V[:, k], PT[f][:, r, k, k * P:],
                                   start=k == 0, stop=k == QT - 1)
                if k == QT - 1:
                    mm.then_inc(pv_done, 1)

            def out(i, g, j):
                pe.wait_ge(o_lo, i * HALVES + HALVES)
                pe.wait_ge(added, i * QT + max(j - 1, 0))
                for f in range(HALVES):
                    w = bass.ds(g * HALVES + f, 1)
                    mm = product(pe, Y_bank[j % 2][:], (O_h[:, f, bass.ts(j, P)], O_l[:, f, bass.ts(j, P)]),
                                 (Wo_h[:, w].rearrange("p o n -> p (o n)"), Wo_l[:, w].rearrange("p o n -> p (o n)")),
                                 f == 0, f == HALVES - 1)
                mm.then_inc(wo_done, 1)

            def slot(i, g, s):
                score(i, s + LEAD)
                if s + TURN >= 0:
                    turn(i, s + TURN)
                for e, far, what, h in events(s):
                    operand(i + far, e, what, h)
                if s >= 0:
                    f, at = divmod(s, SIDE * QT)
                    for k in KEY_TILES.get(at, ()):
                        apply(i, f, k)
                    if s in OUT_TILES:
                        out(i, g, OUT_TILES[s])

            pe.wait_ge(q_ready, 1)
            transposed(q_in[0])
            pe.wait_ge(k_ready, 1)
            pe.wait_ge(op_ready, 1)
            transposed(k_in)
            for s in range(-LEAD, 0):
                slot(0, 0, s)
            pe.wait_ge(w_lo, 1)
            with pe.Fori(0, BATCH) as b:
                with pe.Fori(0, HKV) as g:
                    for s in range(U):
                        slot(b * HKV + g, g, s)

        @block.scalar
        def _(act):
            def operand(n, what, h):
                act.wait_ge(op_done, n)
                act.copy((Q_s[h % 2] if what == "q" else K_s)[:], X_bank[:]).then_inc(op_ready, 1)

            def exps(i, w):
                n = width(w)
                act.wait_ge(s_masked, i * U + w + 1)
                act.wait_ge(rden_ok, positive(i * U + w - 3))
                act.activation(Pr[w % 4][:, 0:n], Pr[w % 4][:, 0:n], ACT.Exp, bias=least[:, w % 4:w % 4 + 1],
                               scale=-1.0, accum_out=den[:, w % 4:w % 4 + 1]).then_inc(p_done, 1)

            def turned(i, w):
                r, q = w // QT % R, QT - 1 - w % QT
                act.wait_ge(pt_done, i * U + w + 1)
                act.wait_ge(pv_done, i * HALVES + max(w // (SIDE * QT) - 1, 0))
                act.copy(PT[r // SIDE][:, r % SIDE, 0:q + 1, bass.ts(q, P)], T_bank[w % 2][:, 0:P * (q + 1)].rearrange("p (k n) -> p k n", n=P))\
                   .then_inc(pt_ok, 1)

            def slot(i, s):
                if s + TURN >= 0:
                    turned(i, s + TURN)
                for e, far, what, h in events(s):
                    if what == "k":
                        act.wait_ge(s_done, (i + far) * U + U)
                    operand((i + far) * NE + BEFORE + e + 1, what, h)
                if s >= 0 and s % (SIDE * QT) == O_HI:
                    f = s // (SIDE * QT)
                    act.wait_ge(pv_done, i * HALVES + f + 1)
                    act.wait_ge(wo_done, i * QT)
                    act.copy(O_h[:, f], O_bank[:]).then_inc(o_hi, 1)
                exps(i, s + LEAD)

            operand(1, "q", 0)
            operand(2, "k", 0)
            act.wait_ge(w_in, 16)
            act.copy(Wo_h[:], Wo[:]).then_inc(w_hi, 1)
            for s in range(-LEAD, 0):
                slot(0, s)
            with act.Fori(0, JOBS) as i:
                for s in range(U):
                    slot(i, s)

        @block.vector
        def _(dve):
            dve.wait_ge(const_ready, 32)

            def mask_scores(i, w):
                n = width(w)
                dve.wait_ge(s_done, i * U + w + 1)
                dve.wait_ge(pt_done, positive(i * U + w - 3))
                dve.sem_inc(waited, 1)
                dve.tensor_tensor_reduce(out=Pr[w % 4][:, 0:n], in0=S_bank[w % 2][:, 0:n], in1=mask[:, SEQ - n:SEQ],
                                         scale=-SCALE, scalar=-MASKED, op0=ALU.add, op1=ALU.min,
                                         accum_out=least[:, w % 4:w % 4 + 1]).then_inc(s_masked, 1)

            def normalise(i, w):
                n = width(w)
                one = slice(w % 4, w % 4 + 1)
                dve.wait_ge(p_done, i * U + w + 1)
                dve.reciprocal(rden[:, one], den[:, one]).then_inc(rden_ok, 1)
                dve.wait_ge(rden_ok, i * U + w + 1)
                dve.tensor_scalar(Pr[w % 4][:, 0:n], Pr[w % 4][:, 0:n], rden[:, one], None, ALU.mult).then_inc(p_norm, 1)

            def slot(i, b, s):
                mask_scores(i, s + LEAD)
                if s >= 0 and s % (SIDE * QT) == O_LO:
                    f = s // (SIDE * QT)
                    dve.wait_ge(o_hi, i * HALVES + f + 1)
                    dve.tensor_tensor(O_l[:, f], O_bank[:], O_h[:, f].bitcast(F32), ALU.subtract).then_inc(o_lo, 1)
                if s + LEAD - 1 >= 0:
                    normalise(i, s + LEAD - 1)
                if s - 1 in OUT_TILES:
                    j = OUT_TILES[s - 1]
                    x = H[:, bass.ds(b * QT + j, 1)].rearrange("p o d -> p (o d)")
                    dve.wait_ge(wo_done, i * QT + j + 1)
                    dve.tensor_tensor(x, Y_bank[j % 2][:], x, ALU.add).then_inc(added, 1)

            for s in range(-LEAD, 0):
                slot(0, 0, s)
            with dve.Fori(0, BATCH) as b:
                with dve.Fori(0, HKV) as g:
                    for s in range(U):
                        slot(b * HKV + g, b, s)


def block_project(nc, H, const, h_dram, q_dram, k_dram, v_dram, w_dram, ln1_dram, norm_dram, cos_dram, sin_dram):
    HQ, HKV, DH, RD = 16, 4, 128, 64
    NQ, NK = HQ * DH, HKV * DH
    N = NQ + 2 * NK
    ROT = NQ + NK
    CH = N // D
    LN_EPS, RMS_EPS = 1e-5, 1e-6
    ORDER = (4, 0, 1, 2, 3, 5)
    ident, _, const_ready = const

    with ExitStack() as ctx:
        m = Stage(nc, ctx, "bp")
        W_h = m.sb("W_h", [P, DT, N], F32R)
        W_l = m.sb("W_l", [P, DT, N], F32R)
        ln1 = m.sb("ln1", [P, D])
        norm = m.sb("norm", [P, ROT])
        cos = m.sb("cos", [P, QT, RD])
        sin = m.sb("sin", [P, QT, RD])
        XN = m.sb("XN", [P, D])
        XT_h = [m.sb(f"XT_h{i}", [P, D], F32R) for i in range(2)]
        XT_l = [m.sb(f"XT_l{i}", [P, D], F32R) for i in range(2)]
        raw = [m.sb(f"raw{i}", [P, N]) for i in range(2)]
        W = [r[:, 0:DT * D].rearrange("p (t n) -> p t n", n=D) for r in raw]
        rc = m.sb("rc", [P, HQ + HKV, RD])
        rs = m.sb("rs", [P, HQ + HKV, RD])
        unused = m.sb("unused", [P, D], mybir.dt.bfloat16)
        stat = m.sb("stat", [P, 6])
        mv = m.sb("mv", [P, 2])
        eps = m.sb("eps", [P, 2])
        ssx, ssq, ssqs, ssk = m.sb("ssx", [P, 1]), m.sb("ssq", [P, 4]), m.sb("ssqs", [P, 1]), m.sb("ssk", [P, 1])
        std, rstd = m.sb("std", [P, 4]), m.sb("rstd", [P, 4])
        X_bank = [m.bank(f"X_bank{i}") for i in range(2)]
        C_bank = [m.bank(f"C_bank{i}") for i in range(CH)]

        w_in = [m.sem(f"w_in{i}") for i in range(2)]
        w_hi, w_lo, tabs_in, saved = m.sem("w_hi"), m.sem("w_lo"), m.sem("tabs_in"), m.sem("saved")
        eps_ok, ln, std_ok, rms_sum, rms_std = m.sem("eps_ok"), m.sem("ln"), m.sem("std_ok"), m.sem("rms_sum"), m.sem("rms_std")
        xt_done, xt_hi, xt_lo = m.sem("xt_done"), m.sem("xt_hi"), m.sem("xt_lo")
        c_done, squared, v_out = m.sem("c_done"), m.sem("squared"), m.sem("v_out")
        k_std, q_std, k_inv, q_inv = m.sem("k_std"), m.sem("q_std"), m.sem("k_inv"), m.sem("q_inv")
        left, turned, cosed, roped, scaled = m.sem("left"), m.sem("turned"), m.sem("cosed"), m.sem("roped"), m.sem("scaled")
        stored = [m.sem(f"stored{i}") for i in range(2)]
        waited = m.sem("waited")
        block = ctx.enter_context(nc.Block())

        def older(n):
            return max(n - 1, 0)

        def heads(x):
            return x[:, 0:ROT].rearrange("p (h c) -> p h c", c=DH)[:, :, 0:RD]

        q_view = q_dram.rearrange("(b g) (j p) n -> b j p g n", b=BATCH, p=P)
        k_view = k_dram.rearrange("(b g) (j p) n -> b j p g n", b=BATCH, p=P)
        v_view = v_dram.rearrange("(b g) (j p) n -> b j p g n", b=BATCH, p=P)

        @block.sync
        def _(sp):
            for i, c in enumerate(ORDER):
                if i >= 2:
                    sp.wait_ge(w_lo, i - 1)
                sp.dma_start(W[i % 2], w_dram[:, bass.ts(c, D)].rearrange("(t p) n -> p t n", p=P)).then_inc(w_in[i % 2], 16)
                if i == 1:
                    sp.dma_start(h_dram, H[:]).then_inc(saved, 16)
                    sp.dma_start(ln1[:], ln1_dram.partition_broadcast(P)).then_inc(tabs_in, 16)
                    sp.dma_start(norm[:], norm_dram.partition_broadcast(P)).then_inc(tabs_in, 16)
                    sp.dma_start(cos[:], cos_dram.rearrange("(j p) d -> p j d", p=P)).then_inc(tabs_in, 16)
                    sp.dma_start(sin[:], sin_dram.rearrange("(j p) d -> p j d", p=P)).then_inc(tabs_in, 16)
            with sp.Fori(0, BATCH) as b:
                for j in range(QT):
                    r = raw[j % 2]
                    sp.wait_ge(scaled, b * QT + j + 1)
                    sp.wait_ge(v_out, b * QT + j + 1)
                    for view, lo, hi in ((q_view, 0, NQ), (k_view, NQ, ROT), (v_view, ROT, N)):
                        sp.dma_start(view[bass.ds(b, 1), j].rearrange("o p g n -> p (o g) n"),
                                     r[:, lo:hi].rearrange("p (g n) -> p g n", g=HKV)).then_inc(stored[j % 2], 16)
            for i in range(2):
                sp.wait_ge(stored[i], 16 * 3 * TILES // 2)

        @block.gpsimd
        def _(pool):
            for i, c in enumerate(ORDER):
                w = bass.ts(c, D)
                pool.wait_ge(w_hi, i + 1)
                pool.tensor_tensor(W_l[:, :, w], W[i % 2], W_h[:, :, w].bitcast(F32), ALU.subtract).then_inc(w_lo, 1)
            pool.wait_ge(tabs_in, 64)
            with pool.Fori(0, BATCH) as b:
                for j in range(QT):
                    x = heads(raw[j % 2]).rearrange("p h (s c) -> p h s c", s=2)
                    o = rs[:].rearrange("p h (s c) -> p h s c", s=2)
                    pool.wait_ge(left, b * (5 * QT) + 5 * j + 5)
                    pool.wait_ge(roped, b * QT + j)
                    for half in range(2):
                        sn = sin[:, j, bass.ts(half, RD // 2)].unsqueeze(1).to_broadcast([P, HQ + HKV, RD // 2])
                        pool.tensor_tensor(o[:, :, half], x[:, :, 1 - half], sn, ALU.mult).then_inc(turned, 1)

        @block.tensor
        def _(pe):
            pe.wait_ge(const_ready, 32)

            def transposes(b, j):
                pe.wait_ge(ln, b * (7 * QT) + 7 * j + 7)
                pe.wait_ge(xt_lo, b * QT + (j - 1 if j else 0))
                for t in range(DT):
                    mm = pe.transpose(X_bank[j % 2][:, bass.ts(t, P)], XN[:, bass.ts(t, P)], ident[:])
                mm.then_inc(xt_done, 1)

            def products(b, j, again):
                pe.wait_ge(xt_lo, b * QT + j + 1)
                for i, c in enumerate(ORDER):
                    if not again:
                        pe.wait_ge(w_lo, i + 1)
                    if c < 5:
                        pe.wait_ge(left, b * (5 * QT) + 5 * j - 5 + i + 1 if j else b * (5 * QT))
                    else:
                        pe.wait_ge(v_out, b * QT + j)
                    for t in range(DT):
                        mm = product(pe, C_bank[c][:], (XT_h[j % 2][:, bass.ts(t, P)], XT_l[j % 2][:, bass.ts(t, P)]),
                                     (W_h[:, t, bass.ts(c, D)], W_l[:, t, bass.ts(c, D)]), t == 0, t == DT - 1)
                    mm.then_inc(c_done, 1)
                    if i == CH - 2 and (j + 1 < QT or again != "last"):
                        transposes(b, j + 1)

            transposes(0, 0)
            for j in range(QT):
                products(0, j, "" if j == 0 else "more")
            with pe.Fori(1, BATCH - 1) as b:
                for j in range(QT):
                    products(b, j, "more")
            for j in range(QT):
                products(BATCH - 1, j, "last")

        @block.scalar
        def _(act):
            def halve(i):
                act.wait_ge(w_in[i % 2], 16 * (i // 2 + 1))
                act.copy(W_h[:, :, bass.ts(ORDER[i], D)], W[i % 2]).then_inc(w_hi, 1)

            act.wait_ge(eps_ok, 2)

            def norms(b, j):
                t = bass.ds(b * QT + j, 1)
                n = b * (7 * QT) + 7 * j
                act.wait_ge(ln, n + 2)
                act.activation(std[:, 0:1], mv[:, 1:2], ACT.Sqrt, bias=eps[:, 0:1]).then_inc(std_ok, 1)
                act.wait_ge(eps_ok, 2)
                act.wait_ge(ln, n + 4)
                act.activation(unused[:], H[:, t].rearrange("p o d -> p (o d)"), ACT.Square, accum_out=ssx[:, 0:1]).then_inc(rms_sum, 1)
                act.wait_ge(rms_sum, b * QT + j + 1)
                act.activation(std[:, 1:2], ssx[:, 0:1], ACT.Sqrt, bias=eps[:, 1:2], scale=1.0 / D).then_inc(rms_std, 1)
                act.wait_ge(xt_done, b * QT + j + 1)
                act.copy(XT_h[j % 2][:], X_bank[j % 2][:]).then_inc(xt_hi, 1)

            def squares(b, j):
                for i, c in enumerate(ORDER):
                    act.wait_ge(c_done, b * (CH * QT) + CH * j + i + 1)
                    if c == 5:
                        if j >= 2:
                            act.wait_ge(stored[j % 2], b * (16 * 3 * QT // 2) + 16 * 3 * (j // 2))
                        else:
                            act.wait_ge(stored[j % 2], b * (16 * 3 * QT // 2))
                        act.copy(raw[j % 2][:, ROT:N], C_bank[c][:]).then_inc(v_out, 1)
                        continue
                    act.wait_ge(squared, b * (5 * QT) + 5 * j + i)
                    if c == 4:
                        act.activation(unused[:], C_bank[c][:], ACT.Square, accum_out=ssk[:, 0:1]).then_inc(squared, 1)
                        act.wait_ge(squared, b * (5 * QT) + 5 * j + 1)
                        act.activation(std[:, 3:4], ssk[:, 0:1], ACT.Sqrt, bias=eps[:, 1:2], scale=1.0 / NK).then_inc(k_std, 1)
                    else:
                        act.activation(unused[:], C_bank[c][:], ACT.Square, accum_out=ssq[:, c:c + 1]).then_inc(squared, 1)
                act.wait_ge(q_inv, b * (2 * QT) + 2 * j + 1)
                act.activation(std[:, 2:3], ssqs[:, 0:1], ACT.Sqrt, bias=eps[:, 1:2], scale=1.0 / NQ).then_inc(q_std, 1)

            def scale_queries(b, j):
                act.wait_ge(roped, b * QT + j + 1)
                act.wait_ge(q_inv, b * (2 * QT) + 2 * j + 2)
                act.activation(raw[j % 2][:, 0:NQ], raw[j % 2][:, 0:NQ], ACT.Copy, scale=rstd[:, 2:3]).then_inc(scaled, 1)

            norms(0, 0)
            for i in range(CH):
                halve(i)
            with act.Fori(0, BATCH - 1) as b:
                for j in range(QT):
                    norms(b, j + 1)
                    squares(b, j)
                    scale_queries(b, j)
            for j in range(QT):
                if j + 1 < QT:
                    norms(BATCH - 1, j + 1)
                squares(BATCH - 1, j)
                scale_queries(BATCH - 1, j)

        @block.vector
        def _(dve):
            dve.memset(eps[:, 0:1], LN_EPS).then_inc(eps_ok, 1)
            dve.memset(eps[:, 1:2], RMS_EPS).then_inc(eps_ok, 1)
            dve.wait_ge(tabs_in, 64)
            dve.wait_ge(saved, 16)

            def norms(b, j):
                x = H[:, bass.ds(b * QT + j, 1)].rearrange("p o d -> p (o d)")
                n = b * (7 * QT) + 7 * j
                dve.wait_ge(ln, n)
                dve.bn_stats(stat[:], x).then_inc(ln, 1)
                dve.wait_ge(ln, n + 1)
                dve.sem_inc(waited, 1)
                dve.bn_aggr(mv[:], stat[:]).then_inc(ln, 1)
                dve.wait_ge(std_ok, b * QT + j + 1)
                dve.reciprocal(rstd[:, 0:1], std[:, 0:1]).then_inc(ln, 1)
                dve.wait_ge(ln, n + 3)
                dve.tensor_scalar(x, x, mv[:, 0:1], rstd[:, 0:1], ALU.subtract, ALU.mult).then_inc(ln, 1)
                dve.wait_ge(rms_std, b * QT + j + 1)
                dve.reciprocal(rstd[:, 1:2], std[:, 1:2]).then_inc(ln, 1)
                dve.wait_ge(xt_done, b * QT + j)
                dve.wait_ge(ln, n + 5)
                dve.tensor_scalar(XN[:], x, rstd[:, 1:2], None, ALU.mult).then_inc(ln, 1)
                dve.wait_ge(ln, n + 6)
                dve.tensor_tensor(XN[:], XN[:], ln1[:], ALU.mult).then_inc(ln, 1)
                dve.wait_ge(xt_hi, b * QT + j + 1)
                dve.tensor_tensor(XT_l[j % 2][:], X_bank[j % 2][:], XT_h[j % 2][:].bitcast(F32), ALU.subtract).then_inc(xt_lo, 1)

            def leave(b, j):
                r = raw[j % 2]
                dve.wait_ge(stored[j % 2], b * (16 * 3 * QT // 2) + 16 * 3 * (j // 2))
                for i, c in enumerate(ORDER[:5]):
                    w = norm[:, bass.ts(c, D)]
                    dve.wait_ge(squared, b * (5 * QT) + 5 * j + i + 1)
                    if c == 4:
                        dve.wait_ge(k_std, b * QT + j + 1)
                        dve.reciprocal(rstd[:, 3:4], std[:, 3:4]).then_inc(k_inv, 1)
                        dve.wait_ge(k_inv, b * QT + j + 1)
                        dve.scalar_tensor_tensor(out=r[:, bass.ts(c, D)], in0=C_bank[c][:], scalar=rstd[:, 3:4], in1=w,
                                                 op0=ALU.mult, op1=ALU.mult).then_inc(left, 1)
                    else:
                        dve.tensor_tensor(r[:, bass.ts(c, D)], C_bank[c][:], w, ALU.mult).then_inc(left, 1)
                dve.wait_ge(q_std, b * QT + j)
                dve.reduce_sum(ssqs[:], ssq[:], AX_X).then_inc(q_inv, 1)
                cs = cos[:, j].unsqueeze(1).to_broadcast([P, HQ + HKV, RD])
                dve.wait_ge(left, b * (5 * QT) + 5 * j + 5)
                dve.wait_ge(roped, b * QT + j)
                dve.tensor_tensor(rc[:], heads(r), cs, ALU.mult).then_inc(cosed, 1)
                dve.wait_ge(scaled, b * QT + j)
                dve.wait_ge(q_std, b * QT + j + 1)
                dve.reciprocal(rstd[:, 2:3], std[:, 2:3]).then_inc(q_inv, 1)
                dve.wait_ge(cosed, b * QT + j + 1)
                dve.wait_ge(turned, b * (2 * QT) + 2 * j + 2)
                dve.tensor_tensor(heads(r), rc[:], rs[:], ALU.add).then_inc(roped, 1)

            norms(0, 0)
            with dve.Fori(0, BATCH - 1) as b:
                for j in range(QT):
                    norms(b, j + 1)
                    leave(b, j)
            for j in range(QT):
                if j + 1 < QT:
                    norms(BATCH - 1, j + 1)
                leave(BATCH - 1, j)


def block_attend(nc, X1, const, q_dram, k_dram, v_dram, wo_dram):
    HQ, HKV, DH = 16, 4, 128
    R = HQ // HKV
    SCALE = float(DH) ** -0.5
    JOBS = BATCH * HKV
    U = R * QT
    ident, mask, const_ready = const

    LEAD, TURN = 13, 10
    APPLY = 5
    KEY_TILES = {3: (0,), 0: (1,), 1: (2, 3)}
    SPLIT = 2
    VALUES = {9: 0, 10: 1}
    OUT_TILES = {11: 0, 12: 1, 13: 2, 14: 3}
    WEIGHTS, RELOADS = {-12: 0, -11: 1, -5: 2, -2: 3}, {-8: 2, -7: 3}
    EVENTS = [(1, "q", 1), (5, "q", 2), (9, "q", 3), (13, "q", 0), (14, "k", 0)]
    NE = len(EVENTS)
    BEFORE = 2
    PRIOR = (0, 1, 3, 4, 2)

    def positive(n):
        return max(n, 0) if isinstance(n, int) else n

    with ExitStack() as ctx:
        m = Stage(nc, ctx, "ba")
        Wo = [m.sb(f"Wo{i}", [P, R, D]) for i in range(2)]
        Wo_h = m.sb("Wo_h", [P, HQ, D], F32R)
        Wo_l = m.sb("Wo_l", [P, HQ, D], F32R)
        q_in = [m.sb(f"q_in{i}", [P, QT, P]) for i in range(2)]
        k_in = m.sb("k_in", [P, QT, P])
        v_in = m.sb("v_in", [P, QT, P])
        Q_h = [m.sb(f"Q_h{i}", [P, SEQ], F32R) for i in range(2)]
        Q_l = [m.sb(f"Q_l{i}", [P, SEQ], F32R) for i in range(2)]
        K_h, K_l = m.sb("K_h", [P, SEQ], F32R), m.sb("K_l", [P, SEQ], F32R)
        V_h, V_l = m.sb("V_h", [P, QT, P], F32R), m.sb("V_l", [P, QT, P], F32R)
        Pr = [m.sb(f"Pr{i}", [P, SEQ]) for i in range(4)]
        PT_h = [m.sb(f"PT_h{i}", [P, QT, SEQ], F32R) for i in range(2)]
        PT_l = [m.sb(f"PT_l{i}", [P, QT, SEQ], F32R) for i in range(2)]
        O_h = m.sb("O_h", [P, R, SEQ], F32R)
        O_l = m.sb("O_l", [P, R, SEQ], F32R)
        least, den, rden = m.sb("least", [P, 4]), m.sb("den", [P, 4]), m.sb("rden", [P, 4])
        S_bank = [m.bank(f"S_bank{i}") for i in range(2)]
        T_bank = [m.bank(f"T_bank{i}") for i in range(2)]
        O_bank = m.bank("O_bank")
        X_bank = m.bank("X_bank")
        Y_bank = [m.bank(f"Y_bank{i}") for i in range(2)]

        w_in = [m.sem(f"w_in{i}") for i in range(2)]
        w_hi, w_lo = m.sem("w_hi"), m.sem("w_lo")
        q_loaded = [m.sem(f"q_loaded{i}") for i in range(2)]
        k_loaded, v_loaded = m.sem("k_loaded"), m.sem("v_loaded")
        v_hi, v_lo, half_applied = m.sem("v_hi"), m.sem("v_lo"), m.sem("half_applied")
        op_done, op_hi, op_lo = m.sem("op_done"), m.sem("op_hi"), m.sem("op_lo")
        s_done, s_masked, p_done, rden_ok, p_norm = m.sem("s_done"), m.sem("s_masked"), m.sem("p_done"), m.sem("rden_ok"), m.sem("p_norm")
        pt_done, pt_hi, pt_lo, pv_done = m.sem("pt_done"), m.sem("pt_hi"), m.sem("pt_lo"), m.sem("pv_done")
        o_hi, o_lo, wo_done, added = m.sem("o_hi"), m.sem("o_lo"), m.sem("wo_done"), m.sem("added")
        waited = m.sem("waited")
        block = ctx.enter_context(nc.Block())

        def width(w):
            return P * (QT - w % QT)

        def events(s):
            far, unit = divmod(s + LEAD, U)
            return [(e, far, what, h) for e, (at, what, h) in enumerate(EVENTS) if at == unit]

        def blocked(dram, job, lo, n):
            return dram[bass.ds(job, 1), :, lo:lo + n].rearrange("o (j p) n -> p (o j) n", p=P)

        wo_view = wo_dram.rearrange("(g h p) n -> g p h n", g=HKV, p=P)

        @block.sync
        def _(sp):
            sp.dma_start(q_in[0][:], blocked(q_dram, 0, 0, P)).then_inc(q_loaded[0], 16)
            sp.dma_start(k_in[:], blocked(k_dram, 0, 0, P)).then_inc(k_loaded, 16)
            sp.dma_start(v_in[:], blocked(v_dram, 0, 0, P)).then_inc(v_loaded, 16)
            for g in range(2):
                sp.dma_start(Wo[g][:], wo_view[g]).then_inc(w_in[g], 16)

            def query_load(i, e):
                h = EVENTS[e][2]
                sp.wait_ge(op_done, i * NE + PRIOR[e])
                job = i if h else i + 1
                sp.dma_start(q_in[h % 2][:], blocked(q_dram, job % JOBS, h * P, P)).then_inc(q_loaded[h % 2], 16)

            with sp.Fori(0, JOBS) as i:
                query_load(i, 0)
                query_load(i, 1)
                sp.wait_ge(op_done, i * NE + PRIOR[4])
                sp.dma_start(k_in[:], blocked(k_dram, (i + 1) % JOBS, 0, P)).then_inc(k_loaded, 16)
                sp.wait_ge(v_lo, (i + 1) * 2)
                sp.dma_start(v_in[:], blocked(v_dram, (i + 1) % JOBS, 0, P)).then_inc(v_loaded, 16)
                query_load(i, 2)
                query_load(i, 3)
            for e in range(3):
                query_load(JOBS, e)
            for loaded, n in ((k_loaded, JOBS + 1), (v_loaded, JOBS + 1), (q_loaded[0], 2 * JOBS + 2), (q_loaded[1], 2 * JOBS + 2)):
                sp.wait_ge(loaded, 16 * n)

        @block.gpsimd
        def _(pool):
            def values(i, half):
                w = bass.ts(half, QT // 2)
                pool.wait_ge(v_hi, i * 2 + half + 1)
                pool.tensor_tensor(V_l[:, w], v_in[:, w], V_h[:, w].bitcast(F32), ALU.subtract).then_inc(v_lo, 1)

            for half in range(2):
                values(0, half)
            for g in range(HKV):
                w = bass.ts(g, R)
                pool.wait_ge(w_hi, g + 1)
                pool.tensor_tensor(Wo_l[:, w], Wo[g % 2][:], Wo_h[:, w].bitcast(F32), ALU.subtract).then_inc(w_lo, 1)
            with pool.Fori(0, JOBS) as i:
                for half in range(2):
                    values(i + 1, half)

        @block.tensor
        def _(pe):
            pe.wait_ge(const_ready, 32)

            def transposed(src):
                for j in range(QT):
                    mm = pe.transpose(X_bank[:, bass.ts(j, P)], src[:, j], ident[:])
                mm.then_inc(op_done, 1)

            def operand(i, e, what, h):
                if what == "k":
                    pe.wait_ge(k_loaded, i * 16 + 32)
                else:
                    pe.wait_ge(q_loaded[h % 2], i * 32 + {1: 16, 2: 32, 3: 32, 0: 48}[h])
                pe.wait_ge(op_lo, i * NE + BEFORE + e)
                transposed(k_in if what == "k" else q_in[h % 2])

            def score(i, w):
                h, q = w // QT % R, QT - 1 - w % QT
                n = width(w)
                pe.wait_ge(op_lo, (i + w // U) * NE + BEFORE + h)
                pe.wait_ge(s_masked, positive(i * U + w - 1))
                product(pe, S_bank[w % 2][:, 0:n], (Q_h[h % 2][:, bass.ts(q, P)], Q_l[h % 2][:, bass.ts(q, P)]),
                        (K_h[:, 0:n], K_l[:, 0:n]), True, True).then_inc(s_done, 1)

            def turn(i, w):
                pe.wait_ge(p_norm, i * U + w + 1)
                pe.wait_ge(pt_lo, positive(i * U + w - 1))
                for k in range(width(w) // P):
                    mm = pe.transpose(T_bank[w % 2][:, bass.ts(k, P)], Pr[w % 4][:, bass.ts(k, P)], ident[:])
                mm.then_inc(pt_done, 1)

            def apply(i, hw, k):
                if k == 0:
                    pe.wait_ge(pt_lo, i * U + QT * (hw + 1))
                    pe.wait_ge(o_lo, i * R + hw)
                if k in (0, 2):
                    pe.wait_ge(v_lo, (i + hw // R) * 2 + k // 2 + 1)
                w = slice(k * P, SEQ)
                mm = product(pe, O_bank[:, w], (V_h[:, k], V_l[:, k]), (PT_h[hw % 2][:, k, w], PT_l[hw % 2][:, k, w]),
                             k == 0, k == QT - 1)
                if k == 1:
                    mm.then_inc(half_applied, 1)
                if k == QT - 1:
                    mm.then_inc(pv_done, 1)

            def out(i, g, j):
                pe.wait_ge(w_lo, HKV)
                pe.wait_ge(o_lo, i * R + R)
                pe.wait_ge(added, i * QT + max(j - 1, 0))
                for h in range(R):
                    w = bass.ds(g * R + h, 1)
                    mm = product(pe, Y_bank[j % 2][:], (O_h[:, h, bass.ts(j, P)], O_l[:, h, bass.ts(j, P)]),
                                 (Wo_h[:, w].rearrange("p o n -> p (o n)"), Wo_l[:, w].rearrange("p o n -> p (o n)")),
                                 h == 0, h == R - 1)
                mm.then_inc(wo_done, 1)

            def slot(i, g, s):
                score(i, s + LEAD)
                if s + TURN >= 0:
                    turn(i, s + TURN)
                for e, far, what, h in events(s):
                    operand(i + far, e, what, h)
                if s + APPLY >= 0:
                    for k in KEY_TILES.get(s % QT, ()):
                        apply(i, (s + APPLY) // QT, k)
                if s in OUT_TILES:
                    out(i, g, OUT_TILES[s])

            pe.wait_ge(q_loaded[0], 16)
            transposed(q_in[0])
            pe.wait_ge(k_loaded, 16)
            pe.wait_ge(op_lo, 1)
            transposed(k_in)
            for s in range(-LEAD, 0):
                slot(0, 0, s)
            with pe.Fori(0, BATCH) as b:
                with pe.Fori(0, HKV) as g:
                    for s in range(U):
                        slot(b * HKV + g, g, s)
            for key_tile in range(1, QT):
                apply(JOBS - 1, (U - 1 + APPLY) // QT, key_tile)

        def halves(what, h):
            return (Q_h[h % 2][:], Q_l[h % 2][:]) if what == "q" else (K_h[:], K_l[:])

        @block.scalar
        def _(act):
            def upper(n, what, h):
                act.wait_ge(op_done, n)
                act.copy(halves(what, h)[0], X_bank[:]).then_inc(op_hi, 1)

            def values(i, half):
                w = bass.ts(half, QT // 2)
                act.wait_ge(v_loaded, i * 16 + 16)
                act.wait_ge(pv_done if half else half_applied, i * R)
                act.copy(V_h[:, w], v_in[:, w]).then_inc(v_hi, 1)

            def exps(i, w):
                n = width(w)
                act.wait_ge(s_masked, i * U + w + 1)
                act.wait_ge(rden_ok, positive(i * U + w - 3))
                act.activation(Pr[w % 4][:, 0:n], Pr[w % 4][:, 0:n], ACT.Exp, bias=least[:, w % 4:w % 4 + 1],
                               scale=-1.0, accum_out=den[:, w % 4:w % 4 + 1]).then_inc(p_done, 1)

            def turned(i, w):
                hw, q = w // QT, QT - 1 - w % QT
                act.wait_ge(pt_done, i * U + w + 1)
                act.wait_ge(pv_done, positive(i * R + hw - 1))
                act.copy(PT_h[hw % 2][:, 0:q + 1, bass.ts(q, P)], T_bank[w % 2][:, 0:P * (q + 1)].rearrange("p (k n) -> p k n", n=P))\
                   .then_inc(pt_hi, 1)

            def slot(i, s):
                if s + TURN >= 0:
                    turned(i, s + TURN)
                for e, far, what, h in events(s):
                    if what == "k":
                        act.wait_ge(s_done, (i + far) * U + U)
                    upper((i + far) * NE + BEFORE + e + 1, what, h)
                if s in VALUES:
                    values(i + 1, VALUES[s])
                if s + SPLIT >= 0 and (s + SPLIT) % QT == 0:
                    hw = (s + SPLIT) // QT
                    act.wait_ge(pv_done, i * R + hw + 1)
                    act.wait_ge(wo_done, (i + hw // R) * QT)
                    act.copy(O_h[:, hw % R], O_bank[:]).then_inc(o_hi, 1)
                exps(i, s + LEAD)

            upper(1, "q", 0)
            upper(2, "k", 0)
            for half in range(2):
                values(0, half)
            for s in range(-LEAD, 0):
                slot(0, s)
                if s in RELOADS:
                    g = RELOADS[s]
                    act.wait_ge(w_lo, g - 1)
                    act.dma_start(Wo[g % 2][:], wo_view[g]).then_inc(w_in[g % 2], 16)
                if s in WEIGHTS:
                    g = WEIGHTS[s]
                    act.wait_ge(w_in[g % 2], 16 * (g // 2 + 1))
                    act.copy(Wo_h[:, bass.ts(g, R)], Wo[g % 2][:]).then_inc(w_hi, 1)
            with act.Fori(0, JOBS) as i:
                for s in range(U):
                    slot(i, s)

        @block.vector
        def _(dve):
            def lower(n, what, h):
                hi, lo = halves(what, h)
                dve.wait_ge(op_hi, n)
                dve.tensor_tensor(lo, X_bank[:], hi.bitcast(F32), ALU.subtract).then_inc(op_lo, 1)

            def mask_scores(i, w):
                n = width(w)
                dve.wait_ge(s_done, i * U + w + 1)
                dve.wait_ge(pt_done, positive(i * U + w - 3))
                dve.sem_inc(waited, 1)
                dve.tensor_tensor_reduce(out=Pr[w % 4][:, 0:n], in0=S_bank[w % 2][:, 0:n], in1=mask[:, SEQ - n:SEQ],
                                         scale=-SCALE, scalar=-MASKED, op0=ALU.add, op1=ALU.min,
                                         accum_out=least[:, w % 4:w % 4 + 1]).then_inc(s_masked, 1)

            def normalise(i, w):
                n = width(w)
                one = slice(w % 4, w % 4 + 1)
                dve.wait_ge(p_done, i * U + w + 1)
                dve.reciprocal(rden[:, one], den[:, one]).then_inc(rden_ok, 1)
                dve.wait_ge(rden_ok, i * U + w + 1)
                dve.tensor_scalar(Pr[w % 4][:, 0:n], Pr[w % 4][:, 0:n], rden[:, one], None, ALU.mult).then_inc(p_norm, 1)

            def turned(i, w):
                hw, q = w // QT, QT - 1 - w % QT
                dve.wait_ge(pt_hi, i * U + w + 1)
                to = (slice(None), slice(0, q + 1), bass.ts(q, P))
                dve.tensor_tensor(PT_l[hw % 2][to], T_bank[w % 2][:, 0:P * (q + 1)].rearrange("p (k n) -> p k n", n=P),
                                  PT_h[hw % 2][to].bitcast(F32), ALU.subtract).then_inc(pt_lo, 1)

            def slot(i, b, s):
                mask_scores(i, s + LEAD)
                if s + TURN >= 0:
                    turned(i, s + TURN)
                for e, far, what, h in events(s):
                    lower((i + far) * NE + BEFORE + e + 1, what, h)
                if s + LEAD - 1 >= 0:
                    normalise(i, s + LEAD - 1)
                if s + SPLIT >= 0 and (s + SPLIT) % QT == 0:
                    hw = (s + SPLIT) // QT
                    dve.wait_ge(o_hi, i * R + hw + 1)
                    dve.tensor_tensor(O_l[:, hw % R], O_bank[:], O_h[:, hw % R].bitcast(F32), ALU.subtract).then_inc(o_lo, 1)
                if s - 1 in OUT_TILES:
                    j = OUT_TILES[s - 1]
                    x = X1[:, bass.ds(b * QT + j, 1)].rearrange("p o d -> p (o d)")
                    dve.wait_ge(wo_done, i * QT + j + 1)
                    dve.tensor_tensor(x, Y_bank[j % 2][:], x, ALU.add).then_inc(added, 1)

            dve.wait_ge(const_ready, 32)
            lower(1, "q", 0)
            lower(2, "k", 0)
            for s in range(-LEAD, 0):
                slot(0, 0, s)
            with dve.Fori(0, BATCH) as b:
                with dve.Fori(0, HKV) as g:
                    for s in range(U):
                        slot(b * HKV + g, b, s)


def route(nc, H, const, h_dram, T_h, T_l, comb, ln2_dram, router_dram, rbias_dram, before_dram):
    E = 8
    TOPK = 2
    RMS_EPS = 1e-6
    ident, _, const_ready = const

    with ExitStack() as ctx:
        m = Stage(nc, ctx, "ro")
        ln2 = m.sb("ln2", [P, D])
        Wr = m.sb("Wr", [P, DT, E])
        rbias = m.sb("rbias", [P, E])
        before = m.sb("before", [P, E, E])
        h_in = [m.sb(f"h_in{j}", [P, D]) for j in range(QT)]
        XN = [m.sb(f"XN{i}", [P, D]) for i in range(2)]
        XT = [m.sb(f"XT{i}", [P, D]) for i in range(2)]
        unused = m.sb("unused", [P, D], mybir.dt.bfloat16)
        eps = m.sb("eps", [P, 1])
        ssx, std, rstd = m.sb("ssx", [P, 1]), m.sb("std", [P, 1]), m.sb("rstd", [P, 1])
        grow, sig, score = m.sb("grow", [P, QT, E]), m.sb("sig", [P, QT, E]), m.sb("score", [P, QT, E])
        above, equal = m.sb("above", [P, QT, E, E]), m.sb("equal", [P, QT, E, E])
        rank, chosen, total = m.sb("rank", [P, QT, E]), m.sb("chosen", [P, QT, E]), m.sb("total", [P, QT])
        X_bank = [m.bank(f"X_bank{i}") for i in range(2)]
        L_bank = m.bank("L_bank")

        tabs_in, eps_ok = m.sem("tabs_in"), m.sem("eps_ok")
        h_loaded = [m.sem(f"h_loaded{j}") for j in range(QT)]
        squared, std_ok, nrm = m.sem("squared"), m.sem("std_ok"), m.sem("nrm")
        xt_done, xt_hi, xt_lo, l_done, grown, sel = m.sem("xt_done"), m.sem("xt_hi"), m.sem("xt_lo"), m.sem("l_done"), m.sem("grown"), m.sem("sel")
        waited = m.sem("waited")
        block = ctx.enter_context(nc.Block())
        NRM = 4
        SEL = 12

        def older(n):
            return max(n - 1, 0)

        @block.sync
        def _(sp):
            sp.dma_start(ln2[:], ln2_dram.partition_broadcast(P)).then_inc(tabs_in, 16)
            sp.dma_start(Wr[:], router_dram.rearrange("(t p) e -> p t e", p=P)).then_inc(tabs_in, 16)
            sp.dma_start(rbias[:], rbias_dram.partition_broadcast(P)).then_inc(tabs_in, 16)
            sp.dma_start(before[:], before_dram.partition_broadcast(P)).then_inc(tabs_in, 16)
            with sp.Fori(0, BATCH) as b:
                for j in range(QT):
                    sp.wait_ge(nrm, b * (NRM * QT))
                    sp.dma_start(h_in[j][:], h_dram[:, bass.ds(b * QT + j, 1)].rearrange("p o d -> p (o d)")).then_inc(h_loaded[j], 16)
            for j in range(QT):
                sp.wait_ge(h_loaded[j], 16 * BATCH)

        @block.tensor
        def _(pe):
            pe.wait_ge(const_ready, 32)
            pe.wait_ge(tabs_in, 64)
            with pe.Fori(0, BATCH) as b:
                for s in range(QT + 1):
                    if s < QT:
                        j = s
                        pe.wait_ge(nrm, b * (NRM * QT) + NRM * j + 3)
                        pe.wait_ge(xt_lo, b * (2 * QT) + 2 * older(j))
                        for t in range(DT):
                            mm = pe.transpose(X_bank[j % 2][:, bass.ts(t, P)], XN[j % 2][:, bass.ts(t, P)], ident[:])
                        mm.then_inc(xt_done, 1)
                    if s >= 1:
                        j = s - 1
                        pe.wait_ge(xt_lo, b * (2 * QT) + 2 * j + 2)
                        if j == 0:
                            pe.wait_ge(grown, b)
                            pe.wait_ge(sel, b * SEL)
                        for t in range(DT):
                            mm = pe.matmul(L_bank[:, bass.ts(j, E)], XT[j % 2][:, bass.ts(t, P)], Wr[:, t], start=t == 0, stop=t == DT - 1)
                        mm.then_inc(l_done, 1)

        @block.scalar
        def _(act):
            act.wait_ge(eps_ok, 1)
            with act.Fori(0, BATCH) as b:
                for j in range(QT):
                    n = b * QT + j
                    act.wait_ge(eps_ok, 1)
                    act.wait_ge(std_ok, n)
                    act.activation(unused[:], H[:, bass.ds(n, 1)].rearrange("p o d -> p (o d)"), ACT.Square, accum_out=ssx[:]).then_inc(squared, 1)
                    act.wait_ge(squared, n + 1)
                    act.activation(std[:], ssx[:], ACT.Sqrt, bias=eps[:, 0:1], scale=1.0 / D).then_inc(std_ok, 1)
                    act.wait_ge(eps_ok, 1)
                    act.wait_ge(xt_done, n + 1)
                    act.copy(T_h[:, :, bass.ds(n * P, P)], X_bank[j % 2][:].rearrange("p (t n) -> p t n", n=P)).then_inc(xt_hi, 1)
                act.wait_ge(l_done, b * QT + QT)
                act.wait_ge(sel, b * SEL)
                act.activation(grow[:].rearrange("p j e -> p (j e)"), L_bank[:, 0:QT * E], ACT.Exp, scale=-1.0).then_inc(grown, 1)

        @block.vector
        def _(dve):
            dve.memset(eps[:], RMS_EPS).then_inc(eps_ok, 1)
            dve.wait_ge(tabs_in, 64)

            def normalise(b, j):
                n = b * QT + j
                k = b * (NRM * QT) + NRM * j
                x = H[:, bass.ds(n, 1)].rearrange("p o d -> p (o d)")
                dve.wait_ge(std_ok, n + 1)
                dve.wait_ge(nrm, k)
                dve.reciprocal(rstd[:], std[:]).then_inc(nrm, 1)
                dve.wait_ge(xt_done, b * QT + older(j))
                dve.wait_ge(nrm, k + 1)
                dve.tensor_scalar(XN[j % 2][:], x, rstd[:, 0:1], None, ALU.mult).then_inc(nrm, 1)
                dve.wait_ge(nrm, k + 2)
                dve.tensor_tensor(XN[j % 2][:], XN[j % 2][:], ln2[:], ALU.mult).then_inc(nrm, 1)
                dve.wait_ge(h_loaded[j], b * 16 + 16)
                dve.tensor_tensor(x, x, h_in[j][:], ALU.add).then_inc(nrm, 1)

            def lower(b, j):
                n = b * QT + j
                w = bass.ds(n * P, P)
                x = X_bank[j % 2][:].rearrange("p (t n) -> p t n", n=P)
                dve.wait_ge(xt_hi, n + 1)
                dve.tensor_tensor(T_l[:, :, w], x, T_h[:, :, w].bitcast(F32), ALU.subtract).then_inc(xt_lo, 1)
                dve.wait_ge(l_done, b * QT + older(j))
                dve.tensor_copy(XT[j % 2][:], X_bank[j % 2][:]).then_inc(xt_lo, 1)

            def select(b):
                n = b * SEL
                by_e = lambda x: x[:].unsqueeze(3).to_broadcast([P, QT, E, E])
                by_f = lambda x: x[:].unsqueeze(2).to_broadcast([P, QT, E, E])
                dve.wait_ge(grown, b + 1)
                dve.tensor_scalar(grow[:], grow[:], 1.0, None, ALU.add).then_inc(sel, 1)
                dve.wait_ge(sel, n + 1)
                dve.reciprocal(sig[:], grow[:]).then_inc(sel, 1)
                dve.wait_ge(sel, n + 2)
                dve.tensor_tensor(score[:], sig[:], rbias[:].unsqueeze(1).to_broadcast([P, QT, E]), ALU.add).then_inc(sel, 1)
                dve.wait_ge(sel, n + 3)
                dve.tensor_tensor(above[:], by_f(score), by_e(score), ALU.is_gt).then_inc(sel, 1)
                dve.tensor_tensor(equal[:], by_f(score), by_e(score), ALU.is_equal).then_inc(sel, 1)
                dve.wait_ge(sel, n + 5)
                for j in range(QT):
                    last = dve.tensor_tensor(equal[:, j], equal[:, j], before[:], ALU.mult)
                last.then_inc(sel, 1)
                dve.wait_ge(sel, n + 6)
                dve.tensor_tensor(above[:], above[:], equal[:], ALU.add).then_inc(sel, 1)
                dve.wait_ge(sel, n + 7)
                dve.reduce_sum(rank[:], above[:], AX_X).then_inc(sel, 1)
                dve.wait_ge(sel, n + 8)
                dve.scalar_tensor_tensor(out=chosen[:], in0=rank[:], scalar=TOPK - 0.5, in1=sig[:], op0=ALU.is_lt, op1=ALU.mult).then_inc(sel, 1)
                dve.wait_ge(sel, n + 9)
                dve.reduce_sum(total[:], chosen[:], AX_X).then_inc(sel, 1)
                dve.wait_ge(sel, n + 10)
                dve.reciprocal(total[:], total[:]).then_inc(sel, 1)
                dve.wait_ge(sel, n + 11)
                dve.tensor_tensor(comb[:, :, bass.ds(b * QT, QT)].rearrange("p e j -> p j e"), chosen[:],
                                  total[:].unsqueeze(2).to_broadcast([P, QT, E]), ALU.mult).then_inc(sel, 1)

            with dve.Fori(0, BATCH) as b:
                for s in range(QT + 1):
                    if s < QT:
                        normalise(b, s)
                    if s >= 1:
                        lower(b, s - 1)
                select(b)


def experts(nc, H, T_h, T_l, comb, out, wg_dram, wu_dram, wd_dram):
    E, I = 8, 256
    IT = I // P
    CHUNKS = TILES * P // 512
    CT = TILES // CHUNKS
    PAIR = 2
    U = PAIR * CHUNKS

    with ExitStack() as ctx:
        m = Stage(nc, ctx, "ex")
        Win = m.sb("Win", [P, DT, 2 * I])
        Wdin = m.sb("Wdin", [P, IT, D])
        W_h = [m.sb(f"W_h{i}", [P, DT, 2 * I], F32R) for i in range(PAIR)]
        W_l = [m.sb(f"W_l{i}", [P, DT, 2 * I], F32R) for i in range(PAIR)]
        Wd_h = [m.sb(f"Wd_h{i}", [P, IT, D], F32R) for i in range(PAIR)]
        Wd_l = [m.sb(f"Wd_l{i}", [P, IT, D], F32R) for i in range(PAIR)]
        gate = [m.sb(f"gate{i}", [P, 512]) for i in range(IT)]
        act_ = [m.sb(f"act{i}", [P, 512]) for i in range(IT)]
        A_h = [m.sb(f"A_h{i}", [P, IT, 512], F32R) for i in range(2)]
        A_l = [m.sb(f"A_l{i}", [P, IT, 512], F32R) for i in range(2)]
        G_bank = [m.bank(f"G_bank{i}") for i in range(IT)]
        U_bank = [m.bank(f"U_bank{i}") for i in range(IT)]
        Y_bank = [m.bank(f"Y_bank{i}") for i in range(4)]

        w_in, wd_in = [m.sem(f"w_in{i}") for i in range(2)], m.sem("wd_in")
        w_hi, w_lo = m.sem("w_hi"), m.sem("w_lo")
        g_done, u_done, gated, acted, a_hi, a_lo = (m.sem(x) for x in ("g_done", "u_done", "gated", "acted", "a_hi", "a_lo"))
        y_done, added, stored = m.sem("y_done"), m.sem("added"), m.sem("stored")
        waited = m.sem("waited")
        block = ctx.enter_context(nc.Block())
        NY = U * CT
        NEXT = {1: 1, CHUNKS + 1: 2}

        def older(n):
            return max(n - 1, 0)

        @block.sync
        def _(sp):
            with sp.Fori(0, E + 1) as e:
                sp.wait_ge(w_lo, e * 2)
                for i, w in enumerate((wg_dram, wu_dram)):
                    sp.dma_start(Win[:, :, bass.ts(i, I)], w[bass.ds(e % E, 1)].rearrange("o (t p) i -> p (o t) i", p=P)).then_inc(w_in[i], 16)
                sp.dma_start(Wdin[:], wd_dram[bass.ds(e % E, 1)].rearrange("o (t p) n -> p (o t) n", p=P)).then_inc(wd_in, 16)
            for in_sem in (*w_in, wd_in):
                sp.wait_ge(in_sem, 16 * (E + 1))
            for c in range(CHUNKS):
                sp.wait_ge(added, (E - 1) * TILES + CT * (c + 1))
                sp.dma_start(out[bass.ts(c, 512)].rearrange("(t p) d -> p t d", p=P), H[:, bass.ts(c, CT)]).then_inc(stored, 16)
            sp.wait_ge(stored, 16 * CHUNKS)

        @block.gpsimd
        def _(pool):
            def halve(e, x):
                pool.wait_ge(w_hi, e * 2 + 1)
                pool.tensor_tensor(W_l[x][:], Win[:], W_h[x][:].bitcast(F32), ALU.subtract).then_inc(w_lo, 1)
                pool.wait_ge(w_hi, e * 2 + 2)
                pool.tensor_tensor(Wd_l[x][:], Wdin[:], Wd_h[x][:].bitcast(F32), ALU.subtract).then_inc(w_lo, 1)

            def lower(u, n):
                for i in range(IT):
                    pool.wait_ge(a_hi, n * IT + i + 1)
                    pool.tensor_tensor(A_l[u % 2][:, i], act_[i][:], A_h[u % 2][:, i].bitcast(F32), ALU.subtract).then_inc(a_lo, 1)

            halve(0, 0)
            with pool.Fori(0, E // PAIR) as k:
                for u in range(U):
                    lower(u, k * U + u)
                    if u in NEXT:
                        halve(k * PAIR + NEXT[u], NEXT[u] % PAIR)

        @block.scalar
        def _(act):
            def halve(k, x):
                e, y = k * PAIR + x, x % PAIR
                act.wait_ge(w_in[0], e * 16 + 16)
                act.wait_ge(w_in[1], e * 16 + 16)
                act.copy(W_h[y][:], Win[:]).then_inc(w_hi, 1)
                act.wait_ge(wd_in, e * 16 + 16)
                act.copy(Wd_h[y][:], Wdin[:]).then_inc(w_hi, 1)

            halve(0, 0)
            with act.Fori(0, E // PAIR) as k:
                for u in range(U):
                    for i in range(IT):
                        act.wait_ge(acted, k * (U * IT) + older(u * IT + i))
                        act.wait_ge(g_done, k * (U * IT) + u * IT + i + 1)
                        act.activation(gate[i][:], G_bank[i][:], ACT.Silu).then_inc(gated, 1)
                    act.wait_ge(y_done, k * NY + CT * max(u - 1, 0))
                    for i in range(IT):
                        act.wait_ge(acted, k * (U * IT) + u * IT + i + 1)
                        act.copy(A_h[u % 2][:, i], act_[i][:]).then_inc(a_hi, 1)
                    if u in NEXT:
                        act.wait_ge(y_done, k * NY + (CT * CHUNKS if u > CHUNKS else 0))
                        halve(k, NEXT[u])

        @block.vector
        def _(dve):
            def accumulate(k, u):
                x, c = u // CHUNKS, u % CHUNKS
                for j in range(CT):
                    t = c * CT + j
                    w = comb[:, bass.ds(k * PAIR + x, 1), t:t + 1].rearrange("p o t -> p (o t)")
                    dve.wait_ge(y_done, k * NY + u * CT + j + 1)
                    dve.scalar_tensor_tensor(out=H[:, t], in0=Y_bank[j][:], scalar=w, in1=H[:, t], op0=ALU.mult, op1=ALU.add).then_inc(added, 1)

            with dve.Fori(0, E // PAIR) as k:
                for u in range(U + 1):
                    if u < U:
                        for i in range(IT):
                            dve.wait_ge(a_lo, k * (U * IT) + older(u * IT + i))
                            dve.wait_ge(u_done, k * (U * IT) + u * IT + i + 1)
                            dve.wait_ge(gated, k * (U * IT) + u * IT + i + 1)
                            dve.tensor_tensor(act_[i][:], U_bank[i][:], gate[i][:], ALU.mult).then_inc(acted, 1)
                    if u >= 1:
                        accumulate(k, u - 1)

        @block.tensor
        def _(pe):
            def gate_up(k, u):
                x, c = u // CHUNKS, u % CHUNKS
                w = bass.ts(c, 512)
                if c == 0:
                    pe.wait_ge(w_lo, k * (2 * PAIR) + 2 * x + 2)
                for i in range(IT):
                    for n, (bank, done, free) in enumerate(((G_bank, g_done, gated), (U_bank, u_done, acted))):
                        pe.wait_ge(free, k * (U * IT) + older(u * IT + i))
                        ic = slice(n * I + i * P, n * I + (i + 1) * P)
                        for t in range(DT):
                            mm = product(pe, bank[i][:], (W_h[x][:, t, ic], W_l[x][:, t, ic]), (T_h[:, t, w], T_l[:, t, w]),
                                         t == 0, t == DT - 1)
                        mm.then_inc(done, 1)

            def down(k, u):
                x = u // CHUNKS
                pe.wait_ge(a_lo, k * (U * IT) + u * IT + IT)
                for j in range(CT):
                    pe.wait_ge(added, k * NY + max(u * CT + j + 1 - CT, 0))
                    for i in range(IT):
                        mm = product(pe, Y_bank[j][:], (A_h[u % 2][:, i, bass.ts(j, P)], A_l[u % 2][:, i, bass.ts(j, P)]),
                                     (Wd_h[x][:, i], Wd_l[x][:, i]), i == 0, i == IT - 1)
                    mm.then_inc(y_done, 1)

            with pe.Fori(0, E // PAIR) as k:
                for u in range(U + 1):
                    if u < U:
                        gate_up(k, u)
                    if u >= 1:
                        down(k, u - 1)


def bass_lm_tower(nc, ids, tok_w, attn_w, attn_b, attn_wo, ln1, ln2, blk_w, blk_norm, blk_wo, router, rbias, wg, wu, wd,
                  pos, iota, ident_d, mask_d, cos32, sin32, cos64, sin64, before, out):
    h_dram = nc.dram_tensor("h_saved", [P, TILES, D], F32, kind="Internal").ap()
    q_dram = nc.dram_tensor("q_rows", [16, SEQ, 512], F32, kind="Internal").ap()
    k_dram = nc.dram_tensor("k_rows", [16, SEQ, 128], F32, kind="Internal").ap()
    v_dram = nc.dram_tensor("v_rows", [16, SEQ, 128], F32, kind="Internal").ap()
    with ExitStack() as ctx:
        H = ctx.enter_context(nc.sbuf_tensor("H", [P, TILES, D], F32))
        ident = ctx.enter_context(nc.sbuf_tensor("ident", [P, P], F32))
        mask = ctx.enter_context(nc.sbuf_tensor("mask", [P, SEQ], F32))
        const_ready = ctx.enter_context(nc.semaphore("const_ready"))
        with nc.Block() as block:
            @block.sync
            def _(sp):
                sp.dma_start(ident[:], ident_d).then_inc(const_ready, 16)
                sp.dma_start(mask[:], mask_d).then_inc(const_ready, 16)
        const = ident, mask, const_ready
        token_stage(nc, H, const, tok_w, ids, pos, iota)
        with (nc.sbuf_tensor("Q_jobs", [P, BATCH * 2, QT, 256], F32) as Q_jobs,
              nc.sbuf_tensor("K_jobs", [P, BATCH * 2, QT, 32], F32) as K_jobs,
              nc.sbuf_tensor("V_jobs", [P, BATCH * 2, QT, 32], F32) as V_jobs):
            attn_project(nc, H, const, Q_jobs, K_jobs, V_jobs, attn_w, attn_b, cos32, sin32)
            attn_attend(nc, H, const, Q_jobs, K_jobs, V_jobs, attn_wo)
        block_project(nc, H, const, h_dram, q_dram, k_dram, v_dram, blk_w, ln1, blk_norm, cos64, sin64)
        block_attend(nc, H, const, q_dram, k_dram, v_dram, blk_wo)
        with (nc.sbuf_tensor("T_h", [P, DT, TILES * P], F32R) as T_h, nc.sbuf_tensor("T_l", [P, DT, TILES * P], F32R) as T_l,
              nc.sbuf_tensor("comb", [P, 8, TILES], F32) as comb):
            route(nc, H, const, h_dram, T_h, T_l, comb, ln2, router, rbias, before)
            experts(nc, H, T_h, T_l, comb, out, wg, wu, wd)


def tables():
    f = np.float32
    half = np.arange(0, D, 2, dtype=f)
    div = np.exp(-(np.log(f(10000.0)) / f(D)) * half).astype(f)
    ang = np.arange(SEQ, dtype=f)[:, None] * div
    pos = np.zeros((SEQ, D), f)
    pos[:, 0::2], pos[:, 1::2] = np.sin(ang), np.cos(ang)
    mask = np.zeros((P, SEQ), f)
    mask[:, SEQ - P:] = np.where(np.arange(P)[None, :] > np.arange(P)[:, None], f(MASKED), f(0))
    def angles(dim, theta):
        i = np.arange(dim // 2, dtype=f)
        if theta == 1e4:
            inv = f(theta) ** (-i / f(dim // 2))
        else:
            inv = f(1) / f(theta) ** (np.arange(0, dim, 2, dtype=f) / f(dim))
        a = np.arange(SEQ, dtype=f)[:, None] * inv.astype(f)[None]
        c, s = np.cos(a), np.sin(a)
        return np.concatenate([c, c], 1), np.concatenate([-s, s], 1)

    cos32, sin32 = angles(32, 1e4)
    cos64, sin64 = angles(64, 1e6)
    return {"cos32": cos32, "sin32": sin32, "cos64": cos64, "sin64": sin64, "pos": pos, "iota": np.tile(np.arange(D, dtype=f), (P, 1)), "ident": np.eye(P, dtype=f), "mask": mask,
            "before": (np.arange(8)[None, :] < np.arange(8)[:, None]).astype(f)}


def kernel(**inputs):
    import concourse.bacc as _bacc
    from concourse.bass_utils import run_bass_kernel_spmd as _run

    x = {k: np.asarray(v) for k, v in inputs.items()}
    c = tables()
    cat, flat = np.concatenate, np.ascontiguousarray
    arrays = {
        "ids": flat(x["x"].reshape(TILES, P).T),
        "tok_w": cat([x["L0_tok_Wq"], x["L0_tok_Wk"]], 2),
        "attn_w": flat(cat([x["L0_attn_wq"], x["L0_attn_wk"], x["L0_attn_wv"]], 0).T),
        "attn_b": cat([x["L0_attn_bq"], x["L0_attn_bk"], x["L0_attn_bv"]]),
        "attn_wo": flat(x["L0_attn_wo"].T),
        "ln1": x["L0_ffn_ln1_w"],
        "ln2": x["L0_ffn_ln2_w"],
        "blk_w": cat([x["L0_ffn_wq"], x["L0_ffn_wk"], x["L0_ffn_wv"]], 1),
        "blk_norm": cat([x["L0_ffn_qnorm_w"], x["L0_ffn_knorm_w"]]),
        "blk_wo": x["L0_ffn_wo"],
        "router": x["L0_ffn_router_w"],
        "rbias": x["L0_ffn_router_bias"],
        "wg": x["L0_ffn_wg"],
        "wu": x["L0_ffn_wu"],
        "wd": x["L0_ffn_wd"],
    }
    arrays |= {k: c[k] for k in ("pos", "iota", "ident", "mask", "cos32", "sin32", "cos64", "sin64", "before")}
    nc = _bacc.Bacc("TRN2", target_bir_lowering=False, num_devices=1)
    args = [nc.dram_tensor(f"in_{k}", a.shape, mybir.dt.from_np(a.dtype), kind="ExternalInput").ap() for k, a in arrays.items()]
    out = nc.dram_tensor("out", [TILES * P, D], F32, kind="ExternalOutput").ap()
    bass_lm_tower(nc, *args, out)
    r = _run(nc, [{f"in_{k}": a for k, a in arrays.items()}], core_ids=[0])
    return r.results[0]["out"].reshape(BATCH, SEQ, D)
```

```python
from contextlib import ExitStack

import concourse.bass as bass
import numpy as np
from concourse import mybir

F32 = mybir.dt.float32
F32R = mybir.dt.float32r
I32 = mybir.dt.int32
ALU = mybir.AluOpType
ACT = mybir.ActivationFunctionType
AX_X = mybir.AxisListType.X

P = 128
BATCH, SEQ, D = 4, 512, 512
QT = SEQ // P
DT = D // P
TILES = BATCH * QT
MASKED = -1e30

TOK_LAYERS, TOK_DQK = 4, 128


class Stage:

    def __init__(self, nc, ctx, stage):
        self.nc, self.ctx, self.stage = nc, ctx, stage

    def sb(self, name, shape, dt=F32):
        return self.ctx.enter_context(self.nc.sbuf_tensor(f"{self.stage}_{name}", shape, dt))

    def bank(self, name):
        return self.ctx.enter_context(self.nc.psum_tensor(f"{self.stage}_{name}", [P, 512], F32))

    def sem(self, name):
        return self.ctx.enter_context(self.nc.semaphore(f"{self.stage}_{name}"))


def product(pe, out, a, b, start, stop):
    (a_h, a_l), (b_h, b_l) = a, b
    pe.matmul(out, a_l, b_h, start=start, stop=False)
    pe.matmul(out, a_h, b_l, start=False, stop=False)
    return pe.matmul(out, a_h, b_h, start=False, stop=stop)


class WeightsAhead:
    ATTN_WIDTH = 640
    ORDER = (4, 0, 1, 2, 3, 5)

    def __init__(self, nc, ctx):
        m = Stage(nc, ctx, "wa")
        buffer = m.sb("buffer", [P, 2 * DT * D])
        self.attn = buffer[:, 0:DT * self.ATTN_WIDTH].rearrange("p (t n) -> p t n", t=DT)
        self.chunk = [buffer[:, bass.ts(i, DT * D)].rearrange("p (t n) -> p t n", t=DT) for i in range(2)]
        self.attn_in = m.sem("attn_in")
        self.chunk_in = [m.sem(f"chunk_in{i}") for i in range(2)]

    def load_attn(self, sp, w_dram):
        sp.dma_start(self.attn, w_dram.rearrange("(t p) n -> p t n", p=P)).then_inc(self.attn_in, 16)

    def load_chunk(self, sp, i, w_dram):
        sp.dma_start(self.chunk[i], w_dram[:, bass.ts(self.ORDER[i], D)].rearrange("(t p) n -> p t n", p=P))\
          .then_inc(self.chunk_in[i], 16)


class JobsAhead:

    def __init__(self, nc, ctx, weights):
        m = Stage(nc, ctx, "ja")
        part = [weights.chunk[1][:, i].rearrange("p (j n) -> p j n", n=P) for i in range(4)]
        self.q_in, self.k_in, self.v_in = part[0:2], part[2], part[3]
        self.Wo = weights.chunk[0]
        self.q_loaded, self.k_loaded, self.v_loaded, self.wo_in = (m.sem(x) for x in ("q_loaded", "k_loaded", "v_loaded", "wo_in"))
        self.stored = [m.sem(f"stored{i}") for i in range(2)]

    def load(self, sp, q_dram, k_dram, v_dram, wo_dram):
        for place, dram, loaded in ((self.q_in[0], q_dram, self.q_loaded), (self.k_in, k_dram, self.k_loaded),
                                    (self.v_in, v_dram, self.v_loaded)):
            sp.dma_start(place, dram[0, :, 0:P].rearrange("(j p) n -> p j n", p=P)).then_inc(loaded, 16)
        sp.dma_start(self.Wo, wo_dram[0:DT * P].rearrange("(h p) n -> p h n", p=P)).then_inc(self.wo_in, 16)


def token_stage(nc, H, const, ahead, tok_w, attn_w_dram, ids_dram, pe_dram, iota_dram):
    SCALE = float(TOK_DQK) ** -0.5
    U = BATCH * QT
    XS = DT + 2
    NR = 8
    ident, mask, const_ready, waited = const

    LEAD, TURN, APPLY = 6, 3, 1
    X_USES = ((0, 1), (2, 3), (DT,), (DT + 1,))
    NEXT_WEIGHTS = 6

    def sequence(w):
        return w // QT % BATCH

    def tile(w):
        return QT - 1 - w % QT

    def positive(n):
        return max(n, 0) if isinstance(n, int) else n

    with ExitStack() as ctx:
        m = Stage(nc, ctx, "tok")
        E_h = m.sb("E_h", [P, TILES, D], F32R)
        E_l = m.sb("E_l", [P, TILES, D], F32R)
        ET_h = m.sb("ET_h", [P, DT, SEQ], F32R)
        ET_l = m.sb("ET_l", [P, DT, SEQ], F32R)
        QK_h = [m.sb(f"QK_h{i}", [P, 2, SEQ], F32R) for i in range(2)]
        QK_l = [m.sb(f"QK_l{i}", [P, 2, SEQ], F32R) for i in range(2)]
        W = m.sb("W", [P, TOK_LAYERS, DT, 2 * TOK_DQK])
        W_h = m.sb("W_h", [P, DT, 2 * TOK_DQK], F32R)
        W_l = m.sb("W_l", [P, DT, 2 * TOK_DQK], F32R)
        Pr = m.sb("Pr", [P, 4, SEQ])
        pos = Pr
        PT_h = [m.sb(f"PT_h{i}", [P, SEQ], F32R) for i in range(4)]
        PT_l = [m.sb(f"PT_l{i}", [P, SEQ], F32R) for i in range(4)]
        least, den, rden = m.sb("least", [P, NR]), m.sb("den", [P, NR]), m.sb("rden", [P, NR])
        ids_i = m.sb("ids_i", [P, TILES], I32)
        ids_f = m.sb("ids_f", [P, TILES])
        iota = m.sb("iota", [P, D])

        S_bank = [m.bank(f"S_bank{i}") for i in range(2)]
        T_bank = [m.bank(f"T_bank{i}") for i in range(2)]
        O_bank = [m.bank(f"O_bank{i}") for i in range(2)]
        X_bank = [m.bank(f"X_bank{i}") for i in range(2)]

        in_ids, in_tabs, w0_in, w_in = m.sem("in_ids"), m.sem("in_tabs"), m.sem("w0_in"), m.sem("w_in")
        w_hi, w_lo, ids_ok = m.sem("w_hi"), m.sem("w_lo"), m.sem("ids_ok")
        enc, enc_hi, enc_lo = m.sem("enc"), m.sem("enc_hi"), m.sem("enc_lo")
        x_done, x_hi, x_lo = m.sem("x_done"), m.sem("x_hi"), m.sem("x_lo")
        s_done, s_masked, p_done, rden_ok = m.sem("s_done"), m.sem("s_masked"), m.sem("p_done"), m.sem("rden_ok")
        pt_done, pt_hi, pt_lo, pv_done = m.sem("pt_done"), m.sem("pt_hi"), m.sem("pt_lo"), m.sem("pv_done")
        block = ctx.enter_context(nc.Block())

        def width(w):
            return P * (tile(w) + 1)

        def x_uses(s):
            w = s + LEAD
            return [(w // QT + 1, x) for x in X_USES[w % QT]]

        @block.sync
        def _(sp):
            w_view = tok_w.rearrange("l (t p) n -> p l t n", p=P)
            sp.dma_start(ids_i[:], ids_dram).then_inc(in_ids, 16)
            sp.dma_start(iota[:], iota_dram).then_inc(in_tabs, 16)
            sp.dma_start(pos[:], pe_dram.rearrange("(j p) d -> p j d", p=P)).then_inc(in_tabs, 16)
            sp.dma_start(W[:, 0:1], w_view[:, 0:1]).then_inc(w0_in, 16)
            sp.dma_start(W[:, 1:], w_view[:, 1:]).then_inc(w_in, 16)
            ahead.load_attn(sp, attn_w_dram)

        @block.gpsimd
        def _(pool):
            def split_weights(n, l):
                pool.wait_ge(w_hi, n)
                pool.tensor_tensor(W_l[:].unsqueeze(1), W[:, bass.ds(l, 1)], W_h[:].unsqueeze(1).bitcast(F32), ALU.subtract)\
                    .then_inc(w_lo, 1)

            def lower(n, t):
                pool.wait_ge(enc, n)
                pool.wait_ge(enc_hi, n)
                pool.tensor_tensor(E_l[:, t], H[:, t], E_h[:, t].bitcast(F32), ALU.subtract).then_inc(enc_lo, 1)

            split_weights(1, 0)
            for t in range(TILES):
                lower(t + 1, t)
            pool.wait_ge(w_in, 16)
            with pool.Fori(0, TOK_LAYERS) as l:
                for s in range(U):
                    if s == NEXT_WEIGHTS:
                        split_weights(l + 2, (l + 1) % TOK_LAYERS)
                    lower(l * U + TILES + s + 1, sequence(s) * QT + tile(s))

        @block.tensor
        def _(pe):
            pe.wait_ge(const_ready, 32)

            def x_use(l, sq, x):
                n = (l * BATCH + sq) * XS + x
                b = sq % BATCH
                if x < DT:
                    pe.wait_ge(enc, l * U + QT * (sq + 1))
                    pe.wait_ge(x_lo, positive(n - 1))
                    for j in range(QT):
                        mm = pe.transpose(X_bank[x % 2][:, bass.ts(j, P)], H[:, b * QT + j, bass.ts(x, P)], ident[:])
                else:
                    pe.wait_ge(w_lo, l + sq // BATCH + 1)
                    pe.wait_ge(x_lo, n - x + DT)
                    c = bass.ts(x - DT, TOK_DQK)
                    for t in range(DT):
                        mm = product(pe, X_bank[x % 2][:], (W_h[:, t, c], W_l[:, t, c]), (ET_h[:, t], ET_l[:, t]),
                                     t == 0, t == DT - 1)
                mm.then_inc(x_done, 1)

            def score(l, w):
                b, q, n = sequence(w), tile(w), width(w)
                pe.wait_ge(x_lo, (l * BATCH + w // QT + 1) * XS)
                pe.wait_ge(s_masked, positive(l * U + w - 1))
                product(pe, S_bank[w % 2][:, 0:n], (QK_h[b % 2][:, 0, bass.ts(q, P)], QK_l[b % 2][:, 0, bass.ts(q, P)]),
                        (QK_h[b % 2][:, 1, 0:n], QK_l[b % 2][:, 1, 0:n]), True, True).then_inc(s_done, 1)

            def turn(l, w):
                pe.wait_ge(p_done, l * U + w + 1)
                pe.wait_ge(pt_lo, positive(l * U + w - 1))
                for k in range(tile(w) + 1):
                    mm = pe.transpose(T_bank[w % 2][:, bass.ts(k, P)], Pr[:, w % 4, bass.ts(k, P)], ident[:])
                mm.then_inc(pt_done, 1)

            def apply(l, w):
                b, q = sequence(w), tile(w)
                pe.wait_ge(pt_lo, l * U + w + 1)
                pe.wait_ge(enc_lo, l * U + QT * (w // QT + 1))
                pe.wait_ge(enc, l * U + TILES + w - 1)
                pe.wait_ge(enc_hi, l * U + TILES + w - 1)
                for k in range(q + 1):
                    mm = product(pe, O_bank[w % 2][:], (PT_h[w % 4][:, bass.ts(k, P)], PT_l[w % 4][:, bass.ts(k, P)]),
                                 (E_h[:, b * QT + k], E_l[:, b * QT + k]), k == 0, k == q)
                mm.then_inc(pv_done, 1)

            def slot(l, s):
                if s + TURN >= 0:
                    turn(l, s + TURN)
                score(l, s + LEAD)
                for sq, x in x_uses(s):
                    x_use(l, sq, x)
                if s + APPLY >= 0:
                    apply(l, s + APPLY)

            for x in range(XS):
                x_use(0, 0, x)
            for s in range(-LEAD, 0):
                slot(0, s)
            with pe.Fori(0, TOK_LAYERS) as l:
                for s in range(U):
                    slot(l, s)

        def x_halves(sq, x):
            i = sq % BATCH % 2
            return (ET_h[:, x], ET_l[:, x]) if x < DT else (QK_h[i][:, x - DT], QK_l[i][:, x - DT])

        @block.scalar
        def _(act):
            act.wait_ge(w0_in, 16)
            act.copy(W_h[:], W[:, 0]).then_inc(w_hi, 1)
            for t in range(TILES):
                act.wait_ge(enc, t + 1)
                act.copy(E_h[:, t], H[:, t]).then_inc(enc_hi, 1)

            def take(l, sq, x):
                act.wait_ge(x_done, (l * BATCH + sq) * XS + x + 1)
                act.copy(x_halves(sq, x)[0], X_bank[x % 2][:]).then_inc(x_hi, 1)

            def exps(l, w):
                one, n = slice(w % NR, w % NR + 1), width(w)
                act.wait_ge(s_masked, l * U + w + 1)
                act.wait_ge(rden_ok, l * U + max(w - NR + 1, 0))
                act.activation(Pr[:, w % 4, 0:n], Pr[:, w % 4, 0:n], ACT.Exp, bias=least[:, one], scale=-1.0,
                               accum_out=den[:, one]).then_inc(p_done, 1)

            def turned(l, w):
                n = width(w)
                act.wait_ge(pt_done, l * U + w + 1)
                act.wait_ge(pv_done, positive(l * U + w - 3))
                act.copy(PT_h[w % 4][:, 0:n], T_bank[w % 2][:, 0:n]).then_inc(pt_hi, 1)

            def encoded(l, w):
                act.wait_ge(pv_done, l * U + w + 1)
                act.wait_ge(rden_ok, l * U + w + 1)
                act.activation(E_h[:, sequence(w) * QT + tile(w)], O_bank[w % 2][:], ACT.Copy,
                               scale=rden[:, w % NR:w % NR + 1]).then_inc(enc_hi, 1)

            def slot(l, s):
                if s >= 0:
                    encoded(l, s)
                if s + TURN >= 0:
                    turned(l, s + TURN)
                for sq, x in x_uses(s):
                    take(l, sq, x)
                exps(l, s + LEAD)
                if s == NEXT_WEIGHTS:
                    act.wait_ge(x_done, (l + 1) * BATCH * XS)
                    act.copy(W_h[:].unsqueeze(1), W[:, bass.ds((l + 1) % TOK_LAYERS, 1)]).then_inc(w_hi, 1)

            for x in range(XS):
                take(0, 0, x)
            for s in range(-LEAD, 0):
                slot(0, s)
            act.wait_ge(w_in, 16)
            with act.Fori(0, TOK_LAYERS) as l:
                for s in range(U):
                    slot(l, s)

        @block.vector
        def _(dve):
            dve.wait_ge(const_ready, 32)
            dve.wait_ge(in_ids, 16)
            dve.tensor_copy(ids_f[:], ids_i[:]).then_inc(ids_ok, 1)
            dve.wait_ge(ids_ok, 1)
            dve.wait_ge(in_tabs, 32)
            for t in range(TILES):
                dve.scalar_tensor_tensor(out=H[:, t], in0=iota[:], scalar=ids_f[:, t:t + 1], in1=pos[:, t % QT],
                                         op0=ALU.is_equal, op1=ALU.add).then_inc(enc, 1)
            dve.wait_ge(enc, TILES)

            def take(l, sq, x):
                h, lo = x_halves(sq, x)
                dve.wait_ge(x_hi, (l * BATCH + sq) * XS + x + 1)
                dve.tensor_tensor(lo, X_bank[x % 2][:], h.bitcast(F32), ALU.subtract).then_inc(x_lo, 1)

            def mask_scores(l, w):
                n = width(w)
                dve.wait_ge(s_done, l * U + w + 1)
                dve.wait_ge(pt_done, positive(l * U + w - 3))
                dve.sem_inc(waited, 1)
                dve.tensor_tensor_reduce(out=Pr[:, w % 4, 0:n], in0=S_bank[w % 2][:, 0:n], in1=mask[:, SEQ - n:SEQ],
                                         scale=-SCALE, scalar=-MASKED, op0=ALU.add, op1=ALU.min,
                                         accum_out=least[:, w % NR:w % NR + 1]).then_inc(s_masked, 1)

            def invert(l, w):
                one = slice(w % NR, w % NR + 1)
                dve.wait_ge(p_done, l * U + w + 1)
                dve.wait_ge(enc_hi, l * U + TILES + w - NR + 1)
                dve.reciprocal(rden[:, one], den[:, one]).then_inc(rden_ok, 1)

            def turned(l, w):
                n = width(w)
                dve.wait_ge(pt_hi, l * U + w + 1)
                dve.tensor_tensor(PT_l[w % 4][:, 0:n], T_bank[w % 2][:, 0:n], PT_h[w % 4][:, 0:n].bitcast(F32),
                                  ALU.subtract).then_inc(pt_lo, 1)

            def encoded(l, w):
                dve.wait_ge(rden_ok, l * U + w + 1)
                dve.wait_ge(enc_hi, l * U + TILES + w + 1)
                dve.tensor_scalar(H[:, sequence(w) * QT + tile(w)], O_bank[w % 2][:], rden[:, w % NR:w % NR + 1], None,
                                  ALU.mult).then_inc(enc, 1)

            def slot(l, s):
                if s >= 0:
                    encoded(l, s)
                mask_scores(l, s + LEAD)
                for sq, x in x_uses(s):
                    take(l, sq, x)
                if s + TURN >= 0:
                    turned(l, s + TURN)
                if s + LEAD - 1 >= 0:
                    invert(l, s + LEAD - 1)

            for x in range(XS):
                take(0, 0, x)
            for s in range(-LEAD, 0):
                slot(0, s)
            with dve.Fori(0, TOK_LAYERS) as l:
                for s in range(U):
                    slot(l, s)


def attn_project(nc, H, const, ahead, Q_jobs, K_jobs, V_jobs, b_dram, cos_dram, sin_dram):
    HQ, HKV, DH = 16, 2, 32
    ROT = (HQ + HKV) * DH
    N = ROT + HKV * DH
    NQ = HQ * DH
    EPS = 1e-5
    ident, _, const_ready, waited = const

    NORM, TURN, MULTIPLY, LEAVE = 4, 3, 2, 1

    def positive(n):
        return max(n, 0) if isinstance(n, int) else n

    with ExitStack() as ctx:
        m = Stage(nc, ctx, "ap")
        W, w_in = ahead.attn, ahead.attn_in
        W_h = m.sb("W_h", [P, DT, N], F32R)
        W_l = m.sb("W_l", [P, DT, N], F32R)
        bias = m.sb("bias", [P, N])
        cos = m.sb("cos", [P, QT, DH])
        sin = m.sb("sin", [P, QT, DH])
        XN = [m.sb(f"XN{i}", [P, D]) for i in range(2)]
        XT_h = [m.sb(f"XT_h{i}", [P, D], F32R) for i in range(2)]
        XT_l = [m.sb(f"XT_l{i}", [P, D], F32R) for i in range(2)]
        raw = [m.sb(f"raw{i}", [P, ROT]) for i in range(2)]
        rc = m.sb("rc", [P, ROT])
        rs = [m.sb(f"rs{i}", [P, ROT]) for i in range(2)]
        stat = m.sb("stat", [P, 6])
        mv = m.sb("mv", [P, 2])
        std = m.sb("std", [P, 1])
        rstd = m.sb("rstd", [P, 1])
        eps = m.sb("eps", [P, 1])
        X_bank = [m.bank(f"X_bank{i}") for i in range(2)]
        Q_bank = [m.bank(f"Q_bank{i}") for i in range(2)]
        KV_bank = [m.bank(f"KV_bank{i}") for i in range(2)]

        tabs_in, w_hi, w_lo = m.sem("tabs_in"), m.sem("w_hi"), m.sem("w_lo")
        eps_ok, ln, xt_done, xt_hi, xt_lo = m.sem("eps_ok"), m.sem("ln"), m.sem("xt_done"), m.sem("xt_hi"), m.sem("xt_lo")
        q_done, kv_done, biased = m.sem("q_done"), m.sem("kv_done"), m.sem("biased")
        std_ok, turned, cosed, roped = m.sem("std_ok"), m.sem("turned"), m.sem("cosed"), m.sem("roped")
        block = ctx.enter_context(nc.Block())

        def sequence(b, n):
            return (b + n // QT) % BATCH if n >= QT else b

        def slots(fori, slot):
            for s in range(-NORM, 0):
                slot(0, s)
            with fori(0, BATCH) as b:
                for s in range(QT):
                    slot(b, s)

        @block.sync
        def _(sp):
            sp.dma_start(bias[:], b_dram.partition_broadcast(P)).then_inc(tabs_in, 16)
            sp.dma_start(cos[:], cos_dram.rearrange("(j p) d -> p j d", p=P)).then_inc(tabs_in, 16)
            sp.dma_start(sin[:], sin_dram.rearrange("(j p) d -> p j d", p=P)).then_inc(tabs_in, 16)

        @block.gpsimd
        def _(pool):
            pool.wait_ge(w_in, 16)
            pool.wait_ge(w_hi, 1)
            pool.tensor_tensor(W_l[:], W, W_h[:].bitcast(F32), ALU.subtract).then_inc(w_lo, 1)
            pool.wait_ge(tabs_in, 48)

            def turn(b, n):
                N_ = b * QT + n
                x = raw[n % 2][:].rearrange("p (h s c) -> p h s c", s=2, c=DH // 2)
                o = rs[n % 2][:].rearrange("p (h s c) -> p h s c", s=2, c=DH // 2)
                pool.wait_ge(biased, N_ * 3 + 3)
                pool.wait_ge(roped, positive(N_ - 1))
                for half in range(2):
                    sn = sin[:, n % QT, bass.ts(half, DH // 2)].unsqueeze(1).to_broadcast([P, HQ + HKV, DH // 2])
                    pool.tensor_tensor(o[:, :, half], x[:, :, 1 - half], sn, ALU.mult).then_inc(turned, 1)

            def slot(b, s):
                if s + LEAVE >= 0:
                    turn(b, s + LEAVE)

            slots(pool.Fori, slot)

        @block.tensor
        def _(pe):
            pe.wait_ge(const_ready, 32)

            def transposes(b, n):
                pe.wait_ge(ln, (b * QT + n) * 4 + 4)
                pe.wait_ge(xt_lo, positive(b * QT + n - 1))
                for t in range(DT):
                    mm = pe.transpose(X_bank[n % 2][:, bass.ts(t, P)], XN[n % 2][:, bass.ts(t, P)], ident[:])
                mm.then_inc(xt_done, 1)

            def products(b, n):
                pe.wait_ge(w_lo, 1)
                pe.wait_ge(xt_lo, b * QT + n + 1)
                pe.wait_ge(biased, positive((b * QT + n - 1) * 3))
                for bank, lo, hi, done in ((Q_bank, 0, NQ, q_done), (KV_bank, NQ, N, kv_done)):
                    for t in range(DT):
                        mm = product(pe, bank[n % 2][:, 0:hi - lo], (XT_h[n % 2][:, bass.ts(t, P)], XT_l[n % 2][:, bass.ts(t, P)]),
                                     (W_h[:, t, lo:hi], W_l[:, t, lo:hi]), t == 0, t == DT - 1)
                    mm.then_inc(done, 1)

            def slot(b, s):
                if s + TURN >= 0:
                    transposes(b, s + TURN)
                if s + MULTIPLY >= 0:
                    products(b, s + MULTIPLY)

            slots(pe.Fori, slot)

        @block.scalar
        def _(act):
            def deviation(b, n):
                act.wait_ge(ln, (b * QT + n) * 4 + 2)
                act.activation(std[:], mv[:, 1:2], ACT.Sqrt, bias=eps[:, 0:1]).then_inc(std_ok, 1)

            def upper(b, n):
                act.wait_ge(xt_done, b * QT + n + 1)
                act.wait_ge(kv_done, positive(b * QT + n - 1))
                act.copy(XT_h[n % 2][:], X_bank[n % 2][:]).then_inc(xt_hi, 1)

            def slot(b, s):
                if s + TURN >= 0:
                    upper(b, s + TURN)
                deviation(b, s + NORM)
                if s == -NORM:
                    act.wait_ge(w_in, 16)
                    act.copy(W_h[:], W).then_inc(w_hi, 1)

            act.wait_ge(eps_ok, 1)
            slots(act.Fori, slot)

        @block.vector
        def _(dve):
            dve.memset(eps[:], EPS).then_inc(eps_ok, 1)
            dve.wait_ge(tabs_in, 48)

            def h_tile(b, n):
                return H[:, bass.ds(sequence(b, n) * QT + n % QT, 1)].rearrange("p o d -> p (o d)")

            def statistics(b, n):
                N4 = (b * QT + n) * 4
                dve.wait_ge(ln, N4)
                dve.bn_stats(stat[:], h_tile(b, n)).then_inc(ln, 1)
                dve.wait_ge(ln, N4 + 1)
                dve.sem_inc(waited, 1)
                dve.bn_aggr(mv[:], stat[:]).then_inc(ln, 1)

            def normalise(b, n):
                N4 = (b * QT + n) * 4
                dve.wait_ge(std_ok, b * QT + n + 1)
                dve.reciprocal(rstd[:], std[:]).then_inc(ln, 1)
                dve.wait_ge(ln, N4 + 3)
                dve.wait_ge(xt_done, positive(b * QT + n - 1))
                dve.tensor_scalar(XN[n % 2][:], h_tile(b, n), mv[:, 0:1], rstd[:, 0:1], ALU.subtract, ALU.mult).then_inc(ln, 1)

            def lower(b, n):
                dve.wait_ge(xt_hi, b * QT + n + 1)
                dve.tensor_tensor(XT_l[n % 2][:], X_bank[n % 2][:], XT_h[n % 2][:].bitcast(F32), ALU.subtract).then_inc(xt_lo, 1)

            def by_job(x):
                return x.rearrange("p (g c) -> p g c", g=HKV)

            def leave(b, n):
                N_ = b * QT + n
                heads = lambda x: x.rearrange("p (h c) -> p h c", c=DH)
                jobs = bass.ds(sequence(b, n) * HKV, HKV)
                r = raw[n % 2]
                dve.wait_ge(q_done, N_ + 1)
                dve.wait_ge(turned, positive(N_ * 2 - 2))
                dve.wait_ge(cosed, positive(N_ - 1))
                dve.tensor_tensor(r[:, 0:NQ], Q_bank[n % 2][:], bias[:, 0:NQ], ALU.add).then_inc(biased, 1)
                dve.wait_ge(kv_done, N_ + 1)
                dve.tensor_tensor(r[:, NQ:ROT], KV_bank[n % 2][:, 0:ROT - NQ], bias[:, NQ:ROT], ALU.add).then_inc(biased, 1)
                dve.tensor_tensor(V_jobs[:, jobs, n % QT], by_job(KV_bank[n % 2][:, ROT - NQ:N - NQ]), by_job(bias[:, ROT:N]), ALU.add)\
                   .then_inc(biased, 1)
                dve.wait_ge(biased, N_ * 3 + 2)
                dve.wait_ge(roped, N_)
                dve.tensor_tensor(heads(rc[:]), heads(r[:]), cos[:, n % QT].unsqueeze(1).to_broadcast([P, HQ + HKV, DH]), ALU.mult)\
                   .then_inc(cosed, 1)

            def rotate(b, n):
                N_ = b * QT + n
                jobs = bass.ds(sequence(b, n) * HKV, HKV)
                dve.wait_ge(cosed, N_ + 1)
                dve.wait_ge(turned, N_ * 2 + 2)
                dve.tensor_tensor(Q_jobs[:, jobs, n % QT], by_job(rc[:, 0:NQ]), by_job(rs[n % 2][:, 0:NQ]), ALU.add)
                dve.tensor_tensor(K_jobs[:, jobs, n % QT], by_job(rc[:, NQ:]), by_job(rs[n % 2][:, NQ:]), ALU.add).then_inc(roped, 1)

            def slot(b, s):
                statistics(b, s + NORM)
                if s + TURN >= 0:
                    lower(b, s + TURN)
                if s >= 0:
                    rotate(b, s)
                normalise(b, s + NORM)
                if s + LEAVE >= 0:
                    leave(b, s + LEAVE)

            slots(dve.Fori, slot)


def attn_attend(nc, H, const, ahead, Q_jobs, K_jobs, V_jobs, wo_dram, blk_w_dram):
    HQ, HKV, DH = 16, 2, 32
    R = HQ // HKV
    SIDE = P // DH
    HALVES = R // SIDE
    SCALE = DH ** -0.5
    JOBS = BATCH * HKV
    U = R * QT
    ident, mask, const_ready, waited = const

    LEAD, TURN = 14, 11
    KEY_TILES = {6: (0,), 7: (1,), 8: (2, 3)}
    O_HI, O_LO = 9, 10
    OUT_TILES = {27: 0, 28: 1, 29: 2, 30: 3}
    EVENTS = [(QT * h - 3, "q", h % R) for h in range(1, R + 1)] + [(U - 2, "k", 0)]
    NE = len(EVENTS)
    BEFORE = 2

    def positive(n):
        return max(n, 0) if isinstance(n, int) else n

    with ExitStack() as ctx:
        m = Stage(nc, ctx, "at")
        Wo = m.sb("Wo", [P, HQ // SIDE, D])
        Wo_h = m.sb("Wo_h", [P, HQ // SIDE, D], F32R)
        Wo_l = m.sb("Wo_l", [P, HQ // SIDE, D], F32R)
        q_in = [m.sb(f"q_in{i}", [P, QT, P], F32R) for i in range(2)]
        k_in = m.sb("k_in", [P, QT, P], F32R)
        V = m.sb("V", [P, QT, DH])
        Q_s = [m.sb(f"Q_s{i}", [P, SEQ], F32R) for i in range(2)]
        K_s = m.sb("K_s", [P, SEQ], F32R)
        Pr = [m.sb(f"Pr{i}", [P, SEQ]) for i in range(4)]
        PT = [m.sb(f"PT{i}", [P, SIDE, QT, SEQ]) for i in range(2)]
        O_h = m.sb("O_h", [P, HALVES, SEQ], F32R)
        O_l = m.sb("O_l", [P, HALVES, SEQ], F32R)
        least, den, rden = m.sb("least", [P, 4]), m.sb("den", [P, 4]), m.sb("rden", [P, 4])
        S_bank = [m.bank(f"S_bank{i}") for i in range(2)]
        T_bank = [m.bank(f"T_bank{i}") for i in range(2)]
        O_bank = m.bank("O_bank")
        X_bank = m.bank("X_bank")
        Y_bank = [m.bank(f"Y_bank{i}") for i in range(2)]

        w_in, w_hi, w_lo = m.sem("w_in"), m.sem("w_hi"), m.sem("w_lo")
        q_ready, k_ready, v_ready = m.sem("q_ready"), m.sem("k_ready"), m.sem("v_ready")
        stacked, op_done, op_ready = m.sem("stacked"), m.sem("op_done"), m.sem("op_ready")
        s_done, s_masked, p_done, rden_ok, p_norm = m.sem("s_done"), m.sem("s_masked"), m.sem("p_done"), m.sem("rden_ok"), m.sem("p_norm")
        pt_done, pt_ok, pv_done = m.sem("pt_done"), m.sem("pt_ok"), m.sem("pv_done")
        o_hi, o_lo, wo_done, added = m.sem("o_hi"), m.sem("o_lo"), m.sem("wo_done"), m.sem("added")
        block = ctx.enter_context(nc.Block())

        def width(w):
            return P * (QT - w % QT)

        def events(s):
            far, unit = divmod(s + LEAD, U)
            return [(e, far, what, h) for e, (at, what, h) in enumerate(EVENTS) if at == unit]

        @block.sync
        def _(sp):
            sp.dma_start(Wo[:], wo_dram.rearrange("(g p) n -> p g n", p=P)).then_inc(w_in, 16)
            for i in range(2):
                ahead.load_chunk(sp, i, blk_w_dram)

        @block.gpsimd
        def _(pool):
            def bring(n, job, what, h):
                jobs, rows = (Q_jobs, q_in[h % 2]) if what == "q" else (K_jobs, k_in)
                src = jobs[:, bass.ds(job, 1), :, bass.ts(h, DH)].rearrange("p o j c -> p (o j) c")
                src = src.unsqueeze(2).to_broadcast([P, QT, 2, DH])
                if what == "q":
                    r = rows[:].rearrange("p j (s r c) -> p j s r c", s=2, c=DH)
                    hi, lo = r[:, :, 0], r[:, :, 1]
                else:
                    r = rows[:].rearrange("p j (r s c) -> p j r s c", s=2, c=DH)
                    hi, lo = r[:, :, :, 0], r[:, :, :, 1]
                pool.tensor_copy(hi, src).then_inc(stacked, 1)
                pool.wait_ge(stacked, n)
                pool.sem_inc(waited, 1)
                pool.tensor_tensor(lo, src, hi.bitcast(F32), ALU.subtract).then_inc(q_ready if what == "q" else k_ready, 1)

            def slot(i, s):
                for e, far, what, h in events(s):
                    before = BEFORE if what == "k" else R if h == 0 else h if h >= 3 else h - 1
                    pool.wait_ge(op_done, positive((i + far) * NE + before))
                    job = i + far + (h == 0)
                    if not isinstance(job, int):
                        job = job % JOBS
                    bring((i + far) * NE + BEFORE + e + 1, job, what, h)

            bring(1, 0, "q", 0)
            bring(2, 0, "k", 0)
            pool.wait_ge(w_in, 16)
            pool.wait_ge(w_hi, 1)
            pool.tensor_tensor(Wo_l[:], Wo[:], Wo_h[:].bitcast(F32), ALU.subtract).then_inc(w_lo, 1)
            for s in range(-LEAD, 0):
                slot(0, s)
            with pool.Fori(0, JOBS) as i:
                pool.wait_ge(pv_done, i * HALVES)
                pool.tensor_copy(V[:].unsqueeze(1), V_jobs[:, bass.ds(i, 1)]).then_inc(v_ready, 1)
                for s in range(U):
                    slot(i, s)

        @block.tensor
        def _(pe):
            pe.wait_ge(const_ready, 32)

            def transposed(src):
                for j in range(QT):
                    mm = pe.transpose(X_bank[:, bass.ts(j, P)], src[:, j].bitcast(F32), ident[:])
                mm.then_inc(op_done, 1)

            def operand(i, e, what, h):
                if what == "k":
                    pe.wait_ge(k_ready, i + 2)
                else:
                    pe.wait_ge(q_ready, i * R + (h or R) + 1)
                pe.wait_ge(op_ready, i * NE + BEFORE + e)
                transposed(k_in if what == "k" else q_in[h % 2])

            def score(i, w):
                h, q = w // QT % R, QT - 1 - w % QT
                n = width(w)
                pe.wait_ge(op_ready, (i + w // U) * NE + BEFORE + h)
                pe.wait_ge(s_masked, positive(i * U + w - 1))
                pe.matmul(S_bank[w % 2][:, 0:n], Q_s[h % 2][:, bass.ts(q, P)], K_s[:, 0:n], start=True, stop=True)\
                  .then_inc(s_done, 1)

            def turn(i, w):
                pe.wait_ge(p_norm, i * U + w + 1)
                pe.wait_ge(pt_ok, positive(i * U + w - 1))
                for k in range(width(w) // P):
                    mm = pe.transpose(T_bank[w % 2][:, bass.ts(k, P)], Pr[w % 4][:, bass.ts(k, P)], ident[:])
                mm.then_inc(pt_done, 1)

            def apply(i, f, k):
                if k == 0:
                    pe.wait_ge(pt_ok, i * U + (f + 1) * SIDE * QT)
                    pe.wait_ge(v_ready, i + 1)
                    pe.wait_ge(o_lo, i * HALVES + f)
                for r in range(SIDE):
                    mm = pe.matmul(O_bank[r * DH:(r + 1) * DH, k * P:], V[:, k], PT[f][:, r, k, k * P:],
                                   start=k == 0, stop=k == QT - 1)
                if k == QT - 1:
                    mm.then_inc(pv_done, 1)

            def out(i, g, j):
                pe.wait_ge(o_lo, i * HALVES + HALVES)
                pe.wait_ge(added, i * QT + max(j - 1, 0))
                for f in range(HALVES):
                    w = bass.ds(g * HALVES + f, 1)
                    mm = product(pe, Y_bank[j % 2][:], (O_h[:, f, bass.ts(j, P)], O_l[:, f, bass.ts(j, P)]),
                                 (Wo_h[:, w].rearrange("p o n -> p (o n)"), Wo_l[:, w].rearrange("p o n -> p (o n)")),
                                 f == 0, f == HALVES - 1)
                mm.then_inc(wo_done, 1)

            def slot(i, g, s):
                score(i, s + LEAD)
                if s + TURN >= 0:
                    turn(i, s + TURN)
                for e, far, what, h in events(s):
                    operand(i + far, e, what, h)
                if s >= 0:
                    f, at = divmod(s, SIDE * QT)
                    for k in KEY_TILES.get(at, ()):
                        apply(i, f, k)
                    if s in OUT_TILES:
                        out(i, g, OUT_TILES[s])

            pe.wait_ge(q_ready, 1)
            transposed(q_in[0])
            pe.wait_ge(k_ready, 1)
            pe.wait_ge(op_ready, 1)
            transposed(k_in)
            for s in range(-LEAD, 0):
                slot(0, 0, s)
            pe.wait_ge(w_lo, 1)
            with pe.Fori(0, BATCH) as b:
                with pe.Fori(0, HKV) as g:
                    for s in range(U):
                        slot(b * HKV + g, g, s)

        @block.scalar
        def _(act):
            def operand(n, what, h):
                act.wait_ge(op_done, n)
                act.copy((Q_s[h % 2] if what == "q" else K_s)[:], X_bank[:]).then_inc(op_ready, 1)

            def exps(i, w):
                n = width(w)
                act.wait_ge(s_masked, i * U + w + 1)
                act.wait_ge(rden_ok, positive(i * U + w - 3))
                act.activation(Pr[w % 4][:, 0:n], Pr[w % 4][:, 0:n], ACT.Exp, bias=least[:, w % 4:w % 4 + 1],
                               scale=-1.0, accum_out=den[:, w % 4:w % 4 + 1]).then_inc(p_done, 1)

            def turned(i, w):
                r, q = w // QT % R, QT - 1 - w % QT
                act.wait_ge(pt_done, i * U + w + 1)
                act.wait_ge(pv_done, i * HALVES + max(w // (SIDE * QT) - 1, 0))
                act.copy(PT[r // SIDE][:, r % SIDE, 0:q + 1, bass.ts(q, P)], T_bank[w % 2][:, 0:P * (q + 1)].rearrange("p (k n) -> p k n", n=P))\
                   .then_inc(pt_ok, 1)

            def slot(i, s):
                for e, far, what, h in events(s):
                    if what == "k":
                        act.wait_ge(s_done, (i + far) * U + U)
                    operand((i + far) * NE + BEFORE + e + 1, what, h)
                if s >= 0 and s % (SIDE * QT) == O_HI:
                    f = s // (SIDE * QT)
                    act.wait_ge(pv_done, i * HALVES + f + 1)
                    act.wait_ge(wo_done, i * QT)
                    act.copy(O_h[:, f], O_bank[:]).then_inc(o_hi, 1)
                if s + TURN >= 0:
                    turned(i, s + TURN)
                exps(i, s + LEAD)

            operand(1, "q", 0)
            operand(2, "k", 0)
            act.wait_ge(w_in, 16)
            act.copy(Wo_h[:], Wo[:]).then_inc(w_hi, 1)
            for s in range(-LEAD, 0):
                slot(0, s)
            with act.Fori(0, JOBS) as i:
                for s in range(U):
                    slot(i, s)

        @block.vector
        def _(dve):
            dve.wait_ge(const_ready, 32)

            def mask_scores(i, w):
                n = width(w)
                dve.wait_ge(s_done, i * U + w + 1)
                dve.wait_ge(pt_done, positive(i * U + w - 3))
                dve.sem_inc(waited, 1)
                dve.tensor_tensor_reduce(out=Pr[w % 4][:, 0:n], in0=S_bank[w % 2][:, 0:n], in1=mask[:, SEQ - n:SEQ],
                                         scale=-SCALE, scalar=-MASKED, op0=ALU.add, op1=ALU.min,
                                         accum_out=least[:, w % 4:w % 4 + 1]).then_inc(s_masked, 1)

            def invert(i, w):
                one = slice(w % 4, w % 4 + 1)
                dve.wait_ge(p_done, i * U + w + 1)
                dve.reciprocal(rden[:, one], den[:, one]).then_inc(rden_ok, 1)

            def normalise(i, w):
                one, n = slice(w % 4, w % 4 + 1), width(w)
                dve.wait_ge(rden_ok, i * U + w + 1)
                dve.tensor_scalar(Pr[w % 4][:, 0:n], Pr[w % 4][:, 0:n], rden[:, one], None, ALU.mult).then_inc(p_norm, 1)

            def slot(i, b, s):
                mask_scores(i, s + LEAD)
                if s + LEAD - 1 >= 0:
                    invert(i, s + LEAD - 1)
                if s >= 0 and s % (SIDE * QT) == O_LO:
                    f = s // (SIDE * QT)
                    dve.wait_ge(o_hi, i * HALVES + f + 1)
                    dve.tensor_tensor(O_l[:, f], O_bank[:], O_h[:, f].bitcast(F32), ALU.subtract).then_inc(o_lo, 1)
                if s - 1 in OUT_TILES:
                    j = OUT_TILES[s - 1]
                    x = H[:, bass.ds(b * QT + j, 1)].rearrange("p o d -> p (o d)")
                    dve.wait_ge(wo_done, i * QT + j + 1)
                    dve.tensor_tensor(x, Y_bank[j % 2][:], x, ALU.add).then_inc(added, 1)
                if s + LEAD - 1 >= 0:
                    normalise(i, s + LEAD - 1)

            for s in range(-LEAD, 0):
                slot(0, 0, s)
            with dve.Fori(0, BATCH) as b:
                with dve.Fori(0, HKV) as g:
                    for s in range(U):
                        slot(b * HKV + g, b, s)


def block_project(nc, H, const, ahead, jobs, h_dram, q_dram, k_dram, v_dram, w_dram, wo_dram, ln1_dram, norm_dram, cos_dram, sin_dram):
    HQ, HKV, DH, RD = 16, 4, 128, 64
    NQ, NK = HQ * DH, HKV * DH
    N = NQ + 2 * NK
    ROT = NQ + NK
    CH = N // D
    KEYS, VALUES = NQ // D, ROT // D
    CHR = VALUES
    STORES = 16 * 3 * QT // 2
    LN_EPS, RMS_EPS = 1e-5, 1e-6
    ORDER = ahead.ORDER
    ident, _, const_ready, waited = const

    with ExitStack() as ctx:
        m = Stage(nc, ctx, "bp")
        W_h = m.sb("W_h", [P, DT, N], F32R)
        W_l = m.sb("W_l", [P, DT, N], F32R)
        ln1 = m.sb("ln1", [P, D])
        norm = m.sb("norm", [P, ROT])
        cos = m.sb("cos", [P, QT, RD])
        sin = m.sb("sin", [P, QT, RD])
        XN = m.sb("XN", [P, D])
        XT_h = [m.sb(f"XT_h{i}", [P, D], F32R) for i in range(2)]
        XT_l = [m.sb(f"XT_l{i}", [P, D], F32R) for i in range(2)]
        raw_both = m.sb("raw", [P, 2 * N])
        raw = [raw_both[:, bass.ts(i, N)] for i in range(2)]
        rc = m.sb("rc", [P, HQ + HKV, RD])
        rs = m.sb("rs", [P, HQ + HKV, RD])
        unused = m.sb("unused", [P, D])
        stat = m.sb("stat", [P, 6])
        mv = m.sb("mv", [P, 2])
        eps = m.sb("eps", [P, 2])
        ssx, ssq, ssqs, ssk = m.sb("ssx", [P, 1]), m.sb("ssq", [P, 4]), m.sb("ssqs", [P, 1]), m.sb("ssk", [P, 1])
        std, rstd = m.sb("std", [P, 4]), m.sb("rstd", [P, 4])
        X_bank = [m.bank(f"X_bank{i}") for i in range(2)]
        C_bank = [m.bank(f"C_bank{i}") for i in range(CH)]

        w_in = ahead.chunk_in
        early = raw_both[:].rearrange("p (i t n) -> p i t n", i=3, t=DT)
        W = (*ahead.chunk, early[:, 0], early[:, 1], early[:, 2], ahead.chunk[0])
        LOADED = ((w_in[0], 16), (w_in[1], 16), (w_in[0], 32), (w_in[1], 48), (w_in[1], 48), (w_in[0], 48))
        BY_DVE, BY_POOL = (3, 5), (0, 1, 2, 4)
        w_hi, w_lo, w_lo_v = m.sem("w_hi"), m.sem("w_lo"), m.sem("w_lo_v")
        ln1_in, tabs_in = m.sem("ln1_in"), m.sem("tabs_in")
        saved, rest_saved = m.sem("saved"), m.sem("rest_saved")
        eps_ok, ln, std_ok, rms_sum, rms_std = m.sem("eps_ok"), m.sem("ln"), m.sem("std_ok"), m.sem("rms_sum"), m.sem("rms_std")
        xt_done, xt_hi, xt_lo = m.sem("xt_done"), m.sem("xt_hi"), m.sem("xt_lo")
        c_done, squared, v_out = m.sem("c_done"), m.sem("squared"), m.sem("v_out")
        k_std, q_std, k_inv, q_inv = m.sem("k_std"), m.sem("q_std"), m.sem("k_inv"), m.sem("q_inv")
        left, turned, cosed, roped, scaled = m.sem("left"), m.sem("turned"), m.sem("cosed"), m.sem("roped"), m.sem("scaled")
        stored = jobs.stored
        block = ctx.enter_context(nc.Block())

        def lower_half(engine, i, done):
            w = bass.ts(ORDER[i], D)
            engine.wait_ge(w_hi, i + 1)
            engine.tensor_tensor(W_l[:, :, w], W[i], W_h[:, :, w].bitcast(F32), ALU.subtract).then_inc(done, 1)

        def heads(x):
            return x[:, 0:ROT].rearrange("p (h c) -> p h c", c=DH)[:, :, 0:RD]

        q_view = q_dram.rearrange("(b g) (j p) n -> b j p g n", b=BATCH, p=P)
        k_view = k_dram.rearrange("(b g) (j p) n -> b j p g n", b=BATCH, p=P)
        v_view = v_dram.rearrange("(b g) (j p) n -> b j p g n", b=BATCH, p=P)

        @block.sync
        def _(sp):
            sp.dma_start(h_dram[:, 0:1], H[:, 0:1]).then_inc(saved, 16)
            sp.dma_start(ln1[:], ln1_dram.partition_broadcast(P)).then_inc(ln1_in, 16)
            sp.dma_start(h_dram[:, 1:QT], H[:, 1:QT]).then_inc(rest_saved, 16)
            for i in range(2):
                sp.wait_ge(w_in[i], 16)
            for i in range(2, CH):
                if i == CH - 1:
                    sp.wait_ge(w_lo, 1)
                    sp.wait_ge(w_in[0], 32)
                sp.dma_start(W[i], w_dram[:, bass.ts(ORDER[i], D)].rearrange("(t p) n -> p t n", p=P)).then_inc(LOADED[i][0], 16)
            sp.dma_start(norm[:], norm_dram.partition_broadcast(P)).then_inc(tabs_in, 16)
            sp.dma_start(cos[:], cos_dram.rearrange("(j p) d -> p j d", p=P)).then_inc(tabs_in, 16)
            sp.dma_start(sin[:], sin_dram.rearrange("(j p) d -> p j d", p=P)).then_inc(tabs_in, 16)
            sp.wait_ge(rest_saved, 16)
            sp.dma_start(h_dram[:, QT:], H[:, QT:]).then_inc(rest_saved, 16)

            def store(b, j):
                r = raw[j % 2]
                sp.wait_ge(scaled, b * QT + j + 1)
                sp.wait_ge(v_out, b * QT + j + 1)
                for view, lo, hi in ((q_view, 0, NQ), (k_view, NQ, ROT), (v_view, ROT, N)):
                    sp.dma_start(view[bass.ds(b, 1), j].rearrange("o p g n -> p (o g) n"),
                                 r[:, lo:hi].rearrange("p (g n) -> p g n", g=HKV)).then_inc(stored[j % 2], 16)

            with sp.Fori(0, BATCH - 1) as b:
                for j in range(QT):
                    store(b, j)
            for i in range(2):
                sp.wait_ge(stored[i], STORES * (BATCH - 1))
            jobs.load(sp, q_dram, k_dram, v_dram, wo_dram)
            for j in range(QT):
                store(BATCH - 1, j)

        @block.gpsimd
        def _(pool):
            for i in BY_POOL:
                lower_half(pool, i, w_lo)
            pool.wait_ge(tabs_in, 48)
            with pool.Fori(0, BATCH) as b:
                for j in range(QT):
                    x = heads(raw[j % 2]).rearrange("p h (s c) -> p h s c", s=2)
                    o = rs[:].rearrange("p h (s c) -> p h s c", s=2)
                    pool.wait_ge(left, b * (CHR * QT) + CHR * j + CHR)
                    pool.wait_ge(roped, b * QT + j)
                    for half in range(2):
                        sn = sin[:, j, bass.ts(half, RD // 2)].unsqueeze(1).to_broadcast([P, HQ + HKV, RD // 2])
                        pool.tensor_tensor(o[:, :, half], x[:, :, 1 - half], sn, ALU.mult).then_inc(turned, 1)

        @block.tensor
        def _(pe):
            pe.wait_ge(const_ready, 32)

            def transposes(b, j):
                pe.wait_ge(ln, b * (7 * QT) + 7 * j + 7)
                pe.wait_ge(xt_lo, b * QT + (j - 1 if j else 0))
                for t in range(DT):
                    mm = pe.transpose(X_bank[j % 2][:, bass.ts(t, P)], XN[:, bass.ts(t, P)], ident[:])
                mm.then_inc(xt_done, 1)

            def products(b, j, first=False, last=False):
                pe.wait_ge(xt_lo, b * QT + j + 1)
                for i, c in enumerate(ORDER):
                    if first:
                        if i in BY_POOL:
                            pe.wait_ge(w_lo, BY_POOL.index(i) + 1)
                        else:
                            pe.wait_ge(w_lo_v, BY_DVE.index(i) + 1)
                    if c < VALUES:
                        pe.wait_ge(left, b * (CHR * QT) + (CHR * (j - 1) + i + 1 if j else 0))
                    else:
                        pe.wait_ge(v_out, b * QT + j)
                    for t in range(DT):
                        mm = product(pe, C_bank[c][:], (XT_h[j % 2][:, bass.ts(t, P)], XT_l[j % 2][:, bass.ts(t, P)]),
                                     (W_h[:, t, bass.ts(c, D)], W_l[:, t, bass.ts(c, D)]), t == 0, t == DT - 1)
                    mm.then_inc(c_done, 1)
                    if i == CH - 2 and not last:
                        transposes(b, j + 1)

            transposes(0, 0)
            for j in range(QT):
                products(0, j, first=j == 0)
            with pe.Fori(1, BATCH - 1) as b:
                for j in range(QT):
                    products(b, j)
            for j in range(QT):
                products(BATCH - 1, j, last=j == QT - 1)

        @block.scalar
        def _(act):
            def halve(i):
                act.wait_ge(*LOADED[i])
                act.copy(W_h[:, :, bass.ts(ORDER[i], D)], W[i]).then_inc(w_hi, 1)

            def norms(b, j):
                t = bass.ds(b * QT + j, 1)
                n = b * (7 * QT) + 7 * j
                act.wait_ge(ln, n + 2)
                act.activation(std[:, 0:1], mv[:, 1:2], ACT.Sqrt, bias=eps[:, 0:1]).then_inc(std_ok, 1)
                act.wait_ge(ln, n + 4)
                act.activation(unused[:], H[:, t].rearrange("p o d -> p (o d)"), ACT.Square, accum_out=ssx[:, 0:1]).then_inc(rms_sum, 1)
                act.wait_ge(rms_sum, b * QT + j + 1)
                act.activation(std[:, 1:2], ssx[:, 0:1], ACT.Sqrt, bias=eps[:, 1:2], scale=1.0 / D).then_inc(rms_std, 1)
                act.wait_ge(xt_done, b * QT + j + 1)
                act.copy(XT_h[j % 2][:], X_bank[j % 2][:]).then_inc(xt_hi, 1)

            def squares(b, j):
                for i, c in enumerate(ORDER):
                    act.wait_ge(c_done, b * (CH * QT) + CH * j + i + 1)
                    if c == VALUES:
                        act.wait_ge(stored[j % 2], b * STORES + 16 * 3 * (j // 2))
                        act.copy(raw[j % 2][:, ROT:N], C_bank[c][:]).then_inc(v_out, 1)
                        continue
                    act.wait_ge(squared, b * (CHR * QT) + CHR * j + i)
                    if c == KEYS:
                        act.activation(unused[:], C_bank[c][:], ACT.Square, accum_out=ssk[:, 0:1]).then_inc(squared, 1)
                        act.wait_ge(squared, b * (CHR * QT) + CHR * j + 1)
                        act.activation(std[:, 3:4], ssk[:, 0:1], ACT.Sqrt, bias=eps[:, 1:2], scale=1.0 / NK).then_inc(k_std, 1)
                    else:
                        act.activation(unused[:], C_bank[c][:], ACT.Square, accum_out=ssq[:, c:c + 1]).then_inc(squared, 1)
                act.wait_ge(q_inv, b * (2 * QT) + 2 * j + 1)
                act.activation(std[:, 2:3], ssqs[:, 0:1], ACT.Sqrt, bias=eps[:, 1:2], scale=1.0 / NQ).then_inc(q_std, 1)

            def scale_queries(b, j):
                act.wait_ge(roped, b * QT + j + 1)
                act.wait_ge(q_inv, b * (2 * QT) + 2 * j + 2)
                act.activation(raw[j % 2][:, 0:NQ], raw[j % 2][:, 0:NQ], ACT.Copy, scale=rstd[:, 2:3]).then_inc(scaled, 1)

            for i in range(2):
                halve(i)
            act.wait_ge(eps_ok, 2)
            norms(0, 0)
            for i in range(2, CH):
                halve(i)
            with act.Fori(0, BATCH - 1) as b:
                for j in range(QT):
                    norms(b, j + 1)
                    squares(b, j)
                    scale_queries(b, j)
            for j in range(QT):
                if j + 1 < QT:
                    norms(BATCH - 1, j + 1)
                squares(BATCH - 1, j)
                scale_queries(BATCH - 1, j)

        @block.vector
        def _(dve):
            dve.memset(eps[:, 0:1], LN_EPS).then_inc(eps_ok, 1)
            dve.memset(eps[:, 1:2], RMS_EPS).then_inc(eps_ok, 1)

            def norms(b, j, first=False):
                x = H[:, bass.ds(b * QT + j, 1)].rearrange("p o d -> p (o d)")
                n = b * (7 * QT) + 7 * j
                dve.wait_ge(ln, n)
                dve.bn_stats(stat[:], x).then_inc(ln, 1)
                dve.wait_ge(ln, n + 1)
                dve.sem_inc(waited, 1)
                dve.bn_aggr(mv[:], stat[:]).then_inc(ln, 1)
                dve.wait_ge(std_ok, b * QT + j + 1)
                dve.reciprocal(rstd[:, 0:1], std[:, 0:1]).then_inc(ln, 1)
                dve.wait_ge(ln, n + 3)
                if first:
                    dve.wait_ge(saved, 16)
                dve.tensor_scalar(x, x, mv[:, 0:1], rstd[:, 0:1], ALU.subtract, ALU.mult).then_inc(ln, 1)
                dve.wait_ge(rms_std, b * QT + j + 1)
                dve.reciprocal(rstd[:, 1:2], std[:, 1:2]).then_inc(ln, 1)
                dve.wait_ge(xt_done, b * QT + j)
                dve.wait_ge(ln, n + 5)
                dve.tensor_scalar(XN[:], x, rstd[:, 1:2], None, ALU.mult).then_inc(ln, 1)
                dve.wait_ge(ln, n + 6)
                if first:
                    dve.wait_ge(ln1_in, 16)
                dve.tensor_tensor(XN[:], XN[:], ln1[:], ALU.mult).then_inc(ln, 1)
                dve.wait_ge(xt_hi, b * QT + j + 1)
                dve.tensor_tensor(XT_l[j % 2][:], X_bank[j % 2][:], XT_h[j % 2][:].bitcast(F32), ALU.subtract).then_inc(xt_lo, 1)

            def leave(b, j):
                r = raw[j % 2]
                dve.wait_ge(stored[j % 2], b * STORES + 16 * 3 * (j // 2))
                for i, c in enumerate(ORDER[:CHR]):
                    w = norm[:, bass.ts(c, D)]
                    dve.wait_ge(squared, b * (CHR * QT) + CHR * j + i + 1)
                    if c == KEYS:
                        dve.wait_ge(k_std, b * QT + j + 1)
                        dve.reciprocal(rstd[:, 3:4], std[:, 3:4]).then_inc(k_inv, 1)
                        dve.wait_ge(k_inv, b * QT + j + 1)
                        dve.scalar_tensor_tensor(out=r[:, bass.ts(c, D)], in0=C_bank[c][:], scalar=rstd[:, 3:4], in1=w,
                                                 op0=ALU.mult, op1=ALU.mult).then_inc(left, 1)
                    else:
                        dve.tensor_tensor(r[:, bass.ts(c, D)], C_bank[c][:], w, ALU.mult).then_inc(left, 1)
                dve.wait_ge(q_std, b * QT + j)
                dve.reduce_sum(ssqs[:], ssq[:], AX_X).then_inc(q_inv, 1)
                cs = cos[:, j].unsqueeze(1).to_broadcast([P, HQ + HKV, RD])
                dve.wait_ge(left, b * (CHR * QT) + CHR * j + CHR)
                dve.wait_ge(roped, b * QT + j)
                dve.tensor_tensor(rc[:], heads(r), cs, ALU.mult).then_inc(cosed, 1)
                dve.wait_ge(scaled, b * QT + j)
                dve.wait_ge(q_std, b * QT + j + 1)
                dve.reciprocal(rstd[:, 2:3], std[:, 2:3]).then_inc(q_inv, 1)
                dve.wait_ge(cosed, b * QT + j + 1)
                dve.wait_ge(turned, b * (2 * QT) + 2 * j + 2)
                dve.tensor_tensor(heads(r), rc[:], rs[:], ALU.add).then_inc(roped, 1)

            norms(0, 0, first=True)
            for i in BY_DVE:
                lower_half(dve, i, w_lo_v)
            dve.wait_ge(tabs_in, 48)
            dve.wait_ge(rest_saved, 16)
            with dve.Fori(0, BATCH - 1) as b:
                for j in range(QT):
                    if j == QT - 1:
                        dve.wait_ge(rest_saved, 32)
                    norms(b, j + 1)
                    if j == 0:
                        dve.wait_ge(w_lo, len(BY_POOL))
                    leave(b, j)
            for j in range(QT):
                if j + 1 < QT:
                    norms(BATCH - 1, j + 1)
                leave(BATCH - 1, j)


def block_attend(nc, X1, const, ahead, q_dram, k_dram, v_dram, wo_dram):
    HQ, HKV, DH = 16, 4, 128
    R = HQ // HKV
    SCALE = float(DH) ** -0.5
    JOBS = BATCH * HKV
    U = R * QT
    ident, mask, const_ready, waited = const

    LEAD, TURN = 16, 13
    APPLY = 8
    KEY_TILES = {0: (0,), 1: (1,), 2: (2, 3)}
    SPLIT = 5
    VALUES = {6: 0, 7: 1}
    OUT = {0: [(0, 0)], 1: [(1, 0)], 2: [(0, 1)], 3: [(1, 1)], 5: [(0, 2)], 6: [(1, 2)], 8: [(0, 3)], 9: [(1, 3)],
           10: [(2, 0), (3, 0)], 11: [(2, 1), (3, 1)], 12: [(2, 2)], 13: [(2, 3), (3, 2)], 14: [(3, 3)]}
    ADD = {8: (0,), 9: (1,), 13: (2,), 15: (3,)}
    WEIGHTS, RELOADS = {-15: 0, -14: 1, -9: 2, -6: 3}, {-12: 2, -11: 3}
    EVENTS = [(1, "q", 1), (5, "q", 2), (9, "q", 3), (13, "q", 0), (14, "k", 0)]
    NE = len(EVENTS)
    BEFORE = 2
    PRIOR = (0, 1, 3, 4, 2)

    def positive(n):
        return max(n, 0) if isinstance(n, int) else n

    with ExitStack() as ctx:
        m = Stage(nc, ctx, "ba")
        Wo = ahead.Wo, m.sb("Wo1", [P, R, D])[:]
        Wo_h = m.sb("Wo_h", [P, HQ, D], F32R)
        Wo_l = m.sb("Wo_l", [P, HQ, D], F32R)
        q_in, k_in, v_in = ahead.q_in, ahead.k_in, ahead.v_in
        Q_h = [m.sb(f"Q_h{i}", [P, SEQ], F32R) for i in range(2)]
        Q_l = [m.sb(f"Q_l{i}", [P, SEQ], F32R) for i in range(2)]
        K_h, K_l = m.sb("K_h", [P, SEQ], F32R), m.sb("K_l", [P, SEQ], F32R)
        V_h, V_l = m.sb("V_h", [P, QT, P], F32R), m.sb("V_l", [P, QT, P], F32R)
        Pr = [m.sb(f"Pr{i}", [P, SEQ]) for i in range(4)]
        PT_h = [m.sb(f"PT_h{i}", [P, QT, SEQ], F32R) for i in range(2)]
        PT_l = [m.sb(f"PT_l{i}", [P, QT, SEQ], F32R) for i in range(2)]
        O_h = m.sb("O_h", [P, R, SEQ], F32R)
        O_l = m.sb("O_l", [P, R, SEQ], F32R)
        least, den, rden = m.sb("least", [P, 4]), m.sb("den", [P, 4]), m.sb("rden", [P, 4])
        S_bank = [m.bank(f"S_bank{i}") for i in range(2)]
        T_bank = [m.bank(f"T_bank{i}") for i in range(2)]
        O_bank = m.bank("O_bank")
        X_bank = m.bank("X_bank")
        Y_bank = [m.bank(f"Y_bank{i}") for i in range(2)]

        w_in = ahead.wo_in, m.sem("w_in1")
        w_hi, w_lo = m.sem("w_hi"), m.sem("w_lo")
        q_loaded = ahead.q_loaded, m.sem("q_loaded1")
        k_loaded, v_loaded = ahead.k_loaded, ahead.v_loaded
        v_hi, v_lo, half_applied = m.sem("v_hi"), m.sem("v_lo"), m.sem("half_applied")
        op_done, op_hi, op_lo = m.sem("op_done"), m.sem("op_hi"), m.sem("op_lo")
        s_done, s_masked, p_done, rden_ok, p_norm = m.sem("s_done"), m.sem("s_masked"), m.sem("p_done"), m.sem("rden_ok"), m.sem("p_norm")
        pt_done, pt_hi, pt_lo, pv_done = m.sem("pt_done"), m.sem("pt_hi"), m.sem("pt_lo"), m.sem("pv_done")
        o_hi, o_lo, wo_done, added = m.sem("o_hi"), m.sem("o_lo"), m.sem("wo_done"), m.sem("added")
        head_used = m.sem("head_used")
        block = ctx.enter_context(nc.Block())

        def width(w):
            return P * (QT - w % QT)

        def events(s):
            far, unit = divmod(s + LEAD, U)
            return [(e, far, what, h) for e, (at, what, h) in enumerate(EVENTS) if at == unit]

        def blocked(dram, job, lo, n):
            return dram[bass.ds(job, 1), :, lo:lo + n].rearrange("o (j p) n -> p (o j) n", p=P)

        wo_view = wo_dram.rearrange("(g h p) n -> g p h n", g=HKV, p=P)

        @block.sync
        def _(sp):
            sp.dma_start(Wo[1], wo_view[1]).then_inc(w_in[1], 16)
            for done in ahead.stored:
                sp.wait_ge(done, 16 * 3 * TILES // 2)

            def query_load(i, e):
                h = EVENTS[e][2]
                sp.wait_ge(op_done, i * NE + PRIOR[e])
                job = i if h else i + 1
                sp.dma_start(q_in[h % 2], blocked(q_dram, job % JOBS, h * P, P)).then_inc(q_loaded[h % 2], 16)

            def key_load(i):
                sp.wait_ge(op_done, i * NE + PRIOR[4])
                sp.dma_start(k_in, blocked(k_dram, (i + 1) % JOBS, 0, P)).then_inc(k_loaded, 16)

            with sp.Fori(0, JOBS) as i:
                query_load(i, 0)
                query_load(i, 1)
                key_load(i)
                query_load(i, 2)
                sp.wait_ge(v_lo, (i + 1) * 2)
                sp.dma_start(v_in, blocked(v_dram, (i + 1) % JOBS, 0, P)).then_inc(v_loaded, 16)
                query_load(i, 3)
            query_load(JOBS, 0)
            query_load(JOBS, 1)
            key_load(JOBS)
            query_load(JOBS, 2)
            query_load(JOBS, 3)
            for loaded, n in ((k_loaded, JOBS + 2), (v_loaded, JOBS + 1), (q_loaded[0], 2 * JOBS + 3), (q_loaded[1], 2 * JOBS + 2)):
                sp.wait_ge(loaded, 16 * n)

        @block.gpsimd
        def _(pool):
            def values(i, half):
                w = bass.ts(half, QT // 2)
                pool.wait_ge(v_hi, i * 2 + half + 1)
                pool.tensor_tensor(V_l[:, w], v_in[:, w], V_h[:, w].bitcast(F32), ALU.subtract).then_inc(v_lo, 1)

            for half in range(2):
                values(0, half)
            for g in range(HKV):
                w = bass.ts(g, R)
                pool.wait_ge(w_hi, g + 1)
                pool.tensor_tensor(Wo_l[:, w], Wo[g % 2], Wo_h[:, w].bitcast(F32), ALU.subtract).then_inc(w_lo, 1)
            with pool.Fori(0, JOBS) as i:
                for half in range(2):
                    values(i + 1, half)

        @block.tensor
        def _(pe):
            pe.wait_ge(const_ready, 32)

            def transposed(src):
                for j in range(QT):
                    mm = pe.transpose(X_bank[:, bass.ts(j, P)], src[:, j], ident[:])
                mm.then_inc(op_done, 1)

            def operand(i, e, what, h):
                if what == "k":
                    pe.wait_ge(k_loaded, i * 16 + 32)
                else:
                    pe.wait_ge(q_loaded[h % 2], i * 32 + {1: 16, 2: 32, 3: 32, 0: 48}[h])
                pe.wait_ge(op_lo, i * NE + BEFORE + e)
                transposed(k_in if what == "k" else q_in[h % 2])

            def score(i, w):
                h, q = w // QT % R, QT - 1 - w % QT
                n = width(w)
                pe.wait_ge(op_lo, (i + w // U) * NE + BEFORE + h)
                pe.wait_ge(s_masked, positive(i * U + w - 1))
                product(pe, S_bank[w % 2][:, 0:n], (Q_h[h % 2][:, bass.ts(q, P)], Q_l[h % 2][:, bass.ts(q, P)]),
                        (K_h[:, 0:n], K_l[:, 0:n]), True, True).then_inc(s_done, 1)

            def turn(i, w):
                pe.wait_ge(p_norm, i * U + w + 1)
                pe.wait_ge(pt_lo, positive(i * U + w - 1))
                for k in range(width(w) // P):
                    mm = pe.transpose(T_bank[w % 2][:, bass.ts(k, P)], Pr[w % 4][:, bass.ts(k, P)], ident[:])
                mm.then_inc(pt_done, 1)

            def apply(i, hw, k):
                if k == 0:
                    pe.wait_ge(pt_lo, i * U + QT * (hw + 1))
                    pe.wait_ge(o_lo, i * R + hw)
                if k in (0, 2):
                    pe.wait_ge(v_lo, (i + hw // R) * 2 + k // 2 + 1)
                w = slice(k * P, SEQ)
                mm = product(pe, O_bank[:, w], (V_h[:, k], V_l[:, k]), (PT_h[hw % 2][:, k, w], PT_l[hw % 2][:, k, w]),
                             k == 0, k == QT - 1)
                if k == 1:
                    mm.then_inc(half_applied, 1)
                if k == QT - 1:
                    mm.then_inc(pv_done, 1)

            def out(i, g, j, h):
                if h == 0:
                    pe.wait_ge(w_lo, HKV)
                    pe.wait_ge(added, i * QT + max(j - 1, 0))
                pe.wait_ge(o_lo, i * R + h + 1)
                w = bass.ds(g * R + h, 1)
                mm = product(pe, Y_bank[j % 2][:], (O_h[:, h, bass.ts(j, P)], O_l[:, h, bass.ts(j, P)]),
                             (Wo_h[:, w].rearrange("p o n -> p (o n)"), Wo_l[:, w].rearrange("p o n -> p (o n)")),
                             h == 0, h == R - 1)
                if (j, h) == (QT - 1, 0):
                    mm.then_inc(head_used, 1)
                if h == R - 1:
                    mm.then_inc(wo_done, 1)

            def slot(i, g, s):
                score(i, s + LEAD)
                if s + TURN >= 0:
                    turn(i, s + TURN)
                for e, far, what, h in events(s):
                    operand(i + far, e, what, h)
                if s + APPLY >= 0:
                    for k in KEY_TILES.get(s % QT, ()):
                        apply(i, (s + APPLY) // QT, k)
                for j, h in OUT.get(s, ()):
                    out(i, g, j, h)

            pe.wait_ge(q_loaded[0], 16)
            transposed(q_in[0])
            pe.wait_ge(k_loaded, 16)
            pe.wait_ge(op_lo, 1)
            transposed(k_in)
            for s in range(-LEAD, 0):
                slot(0, 0, s)
            with pe.Fori(0, BATCH) as b:
                with pe.Fori(0, HKV) as g:
                    for s in range(U):
                        slot(b * HKV + g, g, s)

        def halves(what, h):
            return (Q_h[h % 2][:], Q_l[h % 2][:]) if what == "q" else (K_h[:], K_l[:])

        @block.scalar
        def _(act):
            def upper(n, what, h):
                act.wait_ge(op_done, n)
                act.copy(halves(what, h)[0], X_bank[:]).then_inc(op_hi, 1)

            def values(i, half):
                w = bass.ts(half, QT // 2)
                act.wait_ge(v_loaded, i * 16 + 16)
                act.wait_ge(pv_done if half else half_applied, i * R)
                act.copy(V_h[:, w], v_in[:, w]).then_inc(v_hi, 1)

            def exps(i, w):
                n = width(w)
                act.wait_ge(s_masked, i * U + w + 1)
                act.wait_ge(rden_ok, positive(i * U + w - 3))
                act.activation(Pr[w % 4][:, 0:n], Pr[w % 4][:, 0:n], ACT.Exp, bias=least[:, w % 4:w % 4 + 1],
                               scale=-1.0, accum_out=den[:, w % 4:w % 4 + 1]).then_inc(p_done, 1)

            def turned(i, w):
                hw, q = w // QT, QT - 1 - w % QT
                act.wait_ge(pt_done, i * U + w + 1)
                act.wait_ge(pv_done, positive(i * R + hw - 1))
                act.copy(PT_h[hw % 2][:, 0:q + 1, bass.ts(q, P)], T_bank[w % 2][:, 0:P * (q + 1)].rearrange("p (k n) -> p k n", n=P))\
                   .then_inc(pt_hi, 1)

            def slot(i, s):
                if s + SPLIT >= 0 and (s + SPLIT) % QT == 0:
                    hw = (s + SPLIT) // QT
                    act.wait_ge(pv_done, i * R + hw + 1)
                    if hw % R == 0:
                        act.wait_ge(head_used, i + hw // R)
                    else:
                        act.wait_ge(wo_done, (i + hw // R) * QT)
                    act.copy(O_h[:, hw % R], O_bank[:]).then_inc(o_hi, 1)
                if s + TURN >= 0:
                    turned(i, s + TURN)
                for e, far, what, h in events(s):
                    if what == "k":
                        act.wait_ge(s_done, (i + far) * U + U)
                    upper((i + far) * NE + BEFORE + e + 1, what, h)
                if s in VALUES:
                    values(i + 1, VALUES[s])
                exps(i, s + LEAD)

            upper(1, "q", 0)
            upper(2, "k", 0)
            for half in range(2):
                values(0, half)
            for s in range(-LEAD, 0):
                slot(0, s)
                if s in RELOADS:
                    g = RELOADS[s]
                    act.wait_ge(w_lo, g - 1)
                    act.dma_start(Wo[g % 2], wo_view[g]).then_inc(w_in[g % 2], 16)
                if s in WEIGHTS:
                    g = WEIGHTS[s]
                    act.wait_ge(w_in[g % 2], 16 * (g // 2 + 1))
                    act.copy(Wo_h[:, bass.ts(g, R)], Wo[g % 2]).then_inc(w_hi, 1)
            with act.Fori(0, JOBS) as i:
                for s in range(U):
                    slot(i, s)

        @block.vector
        def _(dve):
            def lower(n, what, h):
                hi, lo = halves(what, h)
                dve.wait_ge(op_hi, n)
                dve.tensor_tensor(lo, X_bank[:], hi.bitcast(F32), ALU.subtract).then_inc(op_lo, 1)

            def mask_scores(i, w):
                n = width(w)
                dve.wait_ge(s_done, i * U + w + 1)
                dve.wait_ge(pt_done, positive(i * U + w - 3))
                dve.sem_inc(waited, 1)
                dve.tensor_tensor_reduce(out=Pr[w % 4][:, 0:n], in0=S_bank[w % 2][:, 0:n], in1=mask[:, SEQ - n:SEQ],
                                         scale=-SCALE, scalar=-MASKED, op0=ALU.add, op1=ALU.min,
                                         accum_out=least[:, w % 4:w % 4 + 1]).then_inc(s_masked, 1)

            def invert(i, w):
                one = slice(w % 4, w % 4 + 1)
                dve.wait_ge(p_done, i * U + w + 1)
                dve.reciprocal(rden[:, one], den[:, one]).then_inc(rden_ok, 1)

            def normalise(i, w):
                one, n = slice(w % 4, w % 4 + 1), width(w)
                dve.wait_ge(rden_ok, i * U + w + 1)
                dve.tensor_scalar(Pr[w % 4][:, 0:n], Pr[w % 4][:, 0:n], rden[:, one], None, ALU.mult).then_inc(p_norm, 1)

            def turned(i, w):
                hw, q = w // QT, QT - 1 - w % QT
                dve.wait_ge(pt_hi, i * U + w + 1)
                to = (slice(None), slice(0, q + 1), bass.ts(q, P))
                dve.tensor_tensor(PT_l[hw % 2][to], T_bank[w % 2][:, 0:P * (q + 1)].rearrange("p (k n) -> p k n", n=P),
                                  PT_h[hw % 2][to].bitcast(F32), ALU.subtract).then_inc(pt_lo, 1)

            def slot(i, b, s):
                mask_scores(i, s + LEAD)
                if s + SPLIT >= 0 and (s + SPLIT) % QT == 0:
                    hw = (s + SPLIT) // QT
                    dve.wait_ge(o_hi, i * R + hw + 1)
                    dve.tensor_tensor(O_l[:, hw % R], O_bank[:], O_h[:, hw % R].bitcast(F32), ALU.subtract).then_inc(o_lo, 1)
                if s + LEAD - 1 >= 0:
                    invert(i, s + LEAD - 1)
                if s + TURN >= 0:
                    turned(i, s + TURN)
                if s + LEAD - 1 >= 0:
                    normalise(i, s + LEAD - 1)
                for e, far, what, h in events(s):
                    lower((i + far) * NE + BEFORE + e + 1, what, h)
                for j in ADD.get(s, ()):
                    x = X1[:, bass.ds(b * QT + j, 1)].rearrange("p o d -> p (o d)")
                    dve.wait_ge(wo_done, i * QT + j + 1)
                    dve.tensor_tensor(x, Y_bank[j % 2][:], x, ALU.add).then_inc(added, 1)

            dve.wait_ge(const_ready, 32)
            lower(1, "q", 0)
            lower(2, "k", 0)
            for s in range(-LEAD, 0):
                slot(0, 0, s)
            with dve.Fori(0, BATCH) as b:
                with dve.Fori(0, HKV) as g:
                    for s in range(U):
                        slot(b * HKV + g, b, s)


EXPERTS, EXPERT_WIDTH = 8, 256


class Routing:

    def __init__(self, nc, ctx):
        m = Stage(nc, ctx, "rt")
        self.logits = m.sb("logits", [P, TILES, EXPERTS])
        self.rbias = m.sb("rbias", [P, EXPERTS])
        self.before = m.sb("before", [P, EXPERTS, EXPERTS])
        self.comb = m.sb("comb", [P, EXPERTS, TILES])


class ExpertWeights:

    def __init__(self, nc, ctx):
        m = Stage(nc, ctx, "ew")
        IT = EXPERT_WIDTH // P
        self.Win = m.sb("Win", [P, DT, 2 * EXPERT_WIDTH])
        self.Wdin = m.sb("Wdin", [P, IT, D])
        self.W_h = [m.sb(f"W_h{i}", [P, DT, 2 * EXPERT_WIDTH], F32R) for i in range(2)]
        self.W_l = [m.sb(f"W_l{i}", [P, DT, 2 * EXPERT_WIDTH], F32R) for i in range(2)]
        self.Wd_h = [m.sb(f"Wd_h{i}", [P, IT, D], F32R) for i in range(2)]
        self.Wd_l = [m.sb(f"Wd_l{i}", [P, IT, D], F32R) for i in range(2)]
        self.w_in, self.wd_in = [m.sem(f"w_in{i}") for i in range(2)], m.sem("wd_in")
        self.w_hi, self.w_lo = m.sem("w_hi"), m.sem("w_lo")

    def load(self, sp, e, wg_dram, wu_dram, wd_dram):
        sp.wait_ge(self.w_lo, e * 2)
        for i, w in enumerate((wg_dram, wu_dram)):
            sp.dma_start(self.Win[:, :, bass.ts(i, EXPERT_WIDTH)],
                         w[bass.ds(e % EXPERTS, 1)].rearrange("o (t p) i -> p (o t) i", p=P)).then_inc(self.w_in[i], 16)
        sp.dma_start(self.Wdin[:], wd_dram[bass.ds(e % EXPERTS, 1)].rearrange("o (t p) n -> p (o t) n", p=P)).then_inc(self.wd_in, 16)

    def upper(self, act, e, x):
        act.wait_ge(self.w_in[0], e * 16 + 16)
        act.wait_ge(self.w_in[1], e * 16 + 16)
        act.copy(self.W_h[x][:], self.Win[:]).then_inc(self.w_hi, 1)
        act.wait_ge(self.wd_in, e * 16 + 16)
        act.copy(self.Wd_h[x][:], self.Wdin[:]).then_inc(self.w_hi, 1)

    def lower(self, pool, e, x):
        pool.wait_ge(self.w_hi, e * 2 + 1)
        pool.tensor_tensor(self.W_l[x][:], self.Win[:], self.W_h[x][:].bitcast(F32), ALU.subtract).then_inc(self.w_lo, 1)
        pool.wait_ge(self.w_hi, e * 2 + 2)
        pool.tensor_tensor(self.Wd_l[x][:], self.Wdin[:], self.Wd_h[x][:].bitcast(F32), ALU.subtract).then_inc(self.w_lo, 1)


def route(nc, H, const, weights, routing, h_dram, T_h, T_l, wg_dram, wu_dram, wd_dram, ln2_dram, router_dram, rbias_dram, before_dram):
    E = EXPERTS
    RMS_EPS = 1e-6
    ident, _, const_ready, waited = const

    SQUARE, NORM, TURN = QT + 3, QT + 2, QT + 1
    assert DT == QT

    with ExitStack() as ctx:
        m = Stage(nc, ctx, "ro")
        ln2 = m.sb("ln2", [P, D])
        Wr = m.sb("Wr", [P, DT, E])
        Wr_h, Wr_l = m.sb("Wr_h", [P, DT, E], F32R), m.sb("Wr_l", [P, DT, E], F32R)
        LT = m.sb("LT", [E, TILES * P])
        rbias, before, logits = routing.rbias, routing.before, routing.logits
        h_in = [m.sb(f"h_in{j}", [P, D]) for j in range(QT)]
        XN = [m.sb(f"XN{i}", [P, D]) for i in range(2)]
        unused = m.sb("unused", [P, D])
        eps = m.sb("eps", [P, 1])
        ssx, std, rstd = m.sb("ssx", [P, 1]), m.sb("std", [P, 2]), m.sb("rstd", [P, 1])
        X_bank = [m.bank(f"X_bank{i}") for i in range(2)]
        LT_bank, L_bank = m.bank("LT_bank"), m.bank("L_bank")

        tabs_in, prepared = m.sem("tabs_in"), m.sem("prepared")
        h_loaded = [m.sem(f"h_loaded{j}") for j in range(QT)]
        squared, std_ok, inverted, nrm, restored = (m.sem(x) for x in ("squared", "std_ok", "inverted", "nrm", "restored"))
        xt_done, xt_hi, xt_lo = m.sem("xt_done"), m.sem("xt_hi"), m.sem("xt_lo")
        wr_hi, lt_done, lt_out, l_done = m.sem("wr_hi"), m.sem("lt_done"), m.sem("lt_out"), m.sem("l_done")
        block = ctx.enter_context(nc.Block())

        def positive(n):
            return max(n, 0) if isinstance(n, int) else n

        def slots(fori, slot):
            for s in range(-SQUARE, 0):
                slot(0, s, TILES)
            with fori(0, BATCH - 2) as b:
                for s in range(QT):
                    slot(b, s, TILES)
            for b in (BATCH - 2, BATCH - 1):
                for s in range(QT):
                    slot(b, s, (BATCH - b) * QT)

        def h_tile(b, n):
            return H[:, bass.ds(b * QT + n, 1)].rearrange("p o d -> p (o d)")

        @block.sync
        def _(sp):
            sp.dma_start(ln2[:], ln2_dram.partition_broadcast(P)).then_inc(tabs_in, 16)
            sp.dma_start(Wr[:], router_dram.rearrange("(t p) e -> p t e", p=P)).then_inc(tabs_in, 16)
            sp.dma_start(rbias[:], rbias_dram.partition_broadcast(P)).then_inc(tabs_in, 16)
            sp.dma_start(before[:], before_dram.partition_broadcast(P)).then_inc(tabs_in, 16)
            weights.load(sp, 0, wg_dram, wu_dram, wd_dram)
            with sp.Fori(0, BATCH) as b:
                for j in range(QT):
                    sp.wait_ge(restored, b * QT)
                    sp.dma_start(h_in[j][:], h_dram[:, bass.ds(b * QT + j, 1)].rearrange("p o d -> p (o d)")).then_inc(h_loaded[j], 16)
            for j in range(QT):
                sp.wait_ge(h_loaded[j], 16 * BATCH)

        @block.gpsimd
        def _(pool):
            def restore(b, j):
                pool.wait_ge(h_loaded[j], b * 16 + 16)
                pool.wait_ge(nrm, b * QT + j + 1)
                pool.sem_inc(waited, 1)
                pool.tensor_tensor(h_tile(b, j), h_tile(b, j), h_in[j][:], ALU.add).then_inc(restored, 1)

            with pool.Fori(0, BATCH - 1) as b:
                for j in range(QT):
                    restore(b, j)
            weights.lower(pool, 0, 0)

        @block.tensor
        def _(pe):
            pe.wait_ge(const_ready, 32)

            def slot(b, s, end):
                if 0 <= s + TURN < end:
                    n = s + TURN
                    pe.wait_ge(nrm, b * QT + n + 1)
                    pe.wait_ge(xt_lo, positive(b * QT + n - 1))
                    for t in range(DT):
                        mm = pe.transpose(X_bank[n % 2][:, bass.ts(t, P)], XN[n % 2][:, bass.ts(t, P)], ident[:])
                    mm.then_inc(xt_done, 1)
                if s == -1:
                    pe.wait_ge(prepared, 2)
                if s >= 0:
                    if s == 0:
                        pe.wait_ge(xt_lo, b * QT + QT)
                        pe.wait_ge(lt_out, b)
                    w = bass.ds(b * SEQ, SEQ)
                    mm = product(pe, LT_bank[0:E, :], (Wr_h[:, s], Wr_l[:, s]), (T_h[:, s, w], T_l[:, s, w]), s == 0, s == DT - 1)
                    if s == DT - 1:
                        mm.then_inc(lt_done, 1)

            slots(pe.Fori, slot)
            pe.wait_ge(lt_out, BATCH)
            for t in range(TILES):
                mm = pe.transpose(L_bank[:, bass.ts(t, E)], LT[:, bass.ts(t, P)], ident[0:E, 0:E])
            mm.then_inc(l_done, 1)

        @block.scalar
        def _(act):
            act.wait_ge(prepared, 1)

            def squares(b, n):
                N_ = b * QT + n
                act.wait_ge(std_ok, N_)
                act.sem_inc(waited, 1)
                act.activation(unused[:], h_tile(b, n), ACT.Square, accum_out=ssx[:]).then_inc(squared, 1)
                act.wait_ge(squared, N_ + 1)
                act.wait_ge(inverted, positive(N_ - 1))
                act.activation(std[:, n % 2:n % 2 + 1], ssx[:], ACT.Sqrt, bias=eps[:, 0:1], scale=1.0 / D).then_inc(std_ok, 1)

            def upper(b, n):
                N_ = b * QT + n
                act.wait_ge(xt_done, N_ + 1)
                act.copy(T_h[:, :, bass.ds(N_ * P, P)], X_bank[n % 2][:].rearrange("p (t n) -> p t n", n=P)).then_inc(xt_hi, 1)

            def slot(b, s, end):
                if 0 <= s + TURN < end:
                    upper(b, s + TURN)
                if s + SQUARE < end:
                    squares(b, s + SQUARE)
                if s == -1:
                    act.wait_ge(tabs_in, 64)
                    act.copy(Wr_h[:], Wr[:]).then_inc(wr_hi, 1)
                if s == 0 and end == 2 * QT:
                    weights.upper(act, 0, 0)
                if s == QT - 1:
                    act.wait_ge(lt_done, b + 1)
                    act.copy(LT[:, bass.ds(b * SEQ, SEQ)], LT_bank[0:E, :]).then_inc(lt_out, 1)

            slots(act.Fori, slot)
            act.wait_ge(l_done, 1)
            act.copy(logits[:], L_bank[:, 0:TILES * E].rearrange("p (t e) -> p t e", e=E))

        @block.vector
        def _(dve):
            dve.memset(eps[:], RMS_EPS).then_inc(prepared, 1)
            dve.wait_ge(tabs_in, 64)

            def normalise(b, n):
                N_ = b * QT + n
                dve.wait_ge(std_ok, N_ + 1)
                dve.wait_ge(nrm, positive(N_))
                dve.reciprocal(rstd[:], std[:, n % 2:n % 2 + 1]).then_inc(inverted, 1)
                dve.wait_ge(xt_done, positive(N_ - 1))
                dve.wait_ge(inverted, N_ + 1)
                dve.scalar_tensor_tensor(out=XN[n % 2][:], in0=h_tile(b, n), scalar=rstd[:, 0:1], in1=ln2[:],
                                         op0=ALU.mult, op1=ALU.mult).then_inc(nrm, 1)

            def lower(b, n):
                w = bass.ds((b * QT + n) * P, P)
                dve.wait_ge(xt_hi, b * QT + n + 1)
                dve.tensor_tensor(T_l[:, :, w], X_bank[n % 2][:].rearrange("p (t n) -> p t n", n=P), T_h[:, :, w].bitcast(F32),
                                  ALU.subtract).then_inc(xt_lo, 1)

            def slot(b, s, end):
                if s == -1:
                    dve.wait_ge(wr_hi, 1)
                    dve.tensor_tensor(Wr_l[:], Wr[:], Wr_h[:].bitcast(F32), ALU.subtract).then_inc(prepared, 1)
                if s + NORM >= 0 and s + NORM < end:
                    normalise(b, s + NORM)
                if 0 <= s + TURN < end:
                    lower(b, s + TURN)

            slots(dve.Fori, slot)
            for j in range(QT):
                t = (BATCH - 1) * QT + j
                dve.wait_ge(h_loaded[j], 16 * BATCH)
                dve.tensor_tensor(H[:, t], H[:, t], h_in[j][:], ALU.add)


def experts(nc, H, weights, routing, T_h, T_l, out, wg_dram, wu_dram, wd_dram):
    E, I = EXPERTS, EXPERT_WIDTH
    TOPK = 2
    IT = I // P
    CHUNKS = TILES * P // 512
    CT = TILES // CHUNKS
    PAIR = 2
    U = PAIR * CHUNKS

    with ExitStack() as ctx:
        m = Stage(nc, ctx, "ex")
        rbias, before, logits, comb = routing.rbias, routing.before, routing.logits, routing.comb
        grow, sig, score = (m.sb(x, [P, TILES, E]) for x in ("grow", "sig", "score"))
        above, equal = m.sb("above", [P, TILES, E, E]), m.sb("equal", [P, TILES, E, E])
        rank, chosen, total = m.sb("rank", [P, TILES, E]), m.sb("chosen", [P, TILES, E]), m.sb("total", [P, TILES])
        W_h, W_l, Wd_h, Wd_l, w_lo = weights.W_h, weights.W_l, weights.Wd_h, weights.Wd_l, weights.w_lo
        gate = [m.sb(f"gate{i}", [P, 512]) for i in range(IT)]
        hidden = [m.sb(f"hidden{i}", [P, 512]) for i in range(IT)]
        A_h = [m.sb(f"A_h{i}", [P, IT, 512], F32R) for i in range(2)]
        A_l = [m.sb(f"A_l{i}", [P, IT, 512], F32R) for i in range(2)]
        G_bank = [m.bank(f"G_bank{i}") for i in range(IT)]
        U_bank = [m.bank(f"U_bank{i}") for i in range(IT)]
        Y_bank = [m.bank(f"Y_bank{i}") for i in range(4)]

        g_done, u_done, gated, acted, a_hi, a_lo = (m.sem(x) for x in ("g_done", "u_done", "gated", "acted", "a_hi", "a_lo"))
        y_done, added, stored = m.sem("y_done"), m.sem("added"), m.sem("stored")
        grown, sel = m.sem("grown"), m.sem("sel")
        block = ctx.enter_context(nc.Block())
        NY = U * CT
        NEXT = {1: 1, CHUNKS + 1: 2}

        def older(n):
            return max(n - 1, 0)

        @block.sync
        def _(sp):
            with sp.Fori(1, E + 1) as e:
                weights.load(sp, e, wg_dram, wu_dram, wd_dram)
            for loaded in (*weights.w_in, weights.wd_in):
                sp.wait_ge(loaded, 16 * (E + 1))
            for c in range(CHUNKS):
                sp.wait_ge(added, (E - 1) * TILES + CT * (c + 1))
                sp.dma_start(out[bass.ts(c, 512)].rearrange("(t p) d -> p t d", p=P), H[:, bass.ts(c, CT)]).then_inc(stored, 16)
            sp.wait_ge(stored, 16 * CHUNKS)

        @block.gpsimd
        def _(pool):
            def lower(u, n):
                for i in range(IT):
                    pool.wait_ge(a_hi, n * IT + i + 1)
                    pool.tensor_tensor(A_l[u % 2][:, i], hidden[i][:], A_h[u % 2][:, i].bitcast(F32), ALU.subtract).then_inc(a_lo, 1)

            with pool.Fori(0, E // PAIR) as k:
                for u in range(U):
                    lower(u, k * U + u)
                    if u in NEXT:
                        weights.lower(pool, k * PAIR + NEXT[u], NEXT[u] % PAIR)

        @block.scalar
        def _(act):
            act.activation(grow[:], logits[:], ACT.Exp, scale=-1.0).then_inc(grown, 1)
            with act.Fori(0, E // PAIR) as k:
                for u in range(U):
                    for i in range(IT):
                        act.wait_ge(acted, k * (U * IT) + older(u * IT + i))
                        act.wait_ge(g_done, k * (U * IT) + u * IT + i + 1)
                        act.activation(gate[i][:], G_bank[i][:], ACT.Silu).then_inc(gated, 1)
                    act.wait_ge(y_done, k * NY + CT * max(u - 1, 0))
                    for i in range(IT):
                        act.wait_ge(acted, k * (U * IT) + u * IT + i + 1)
                        act.copy(A_h[u % 2][:, i], hidden[i][:]).then_inc(a_hi, 1)
                    if u in NEXT:
                        act.wait_ge(y_done, k * NY + (CT * CHUNKS if u > CHUNKS else 0))
                        weights.upper(act, k * PAIR + NEXT[u], NEXT[u] % PAIR)

        @block.vector
        def _(dve):
            def accumulate(k, u):
                x, c = u // CHUNKS, u % CHUNKS
                for j in range(CT):
                    t = c * CT + j
                    w = comb[:, bass.ds(k * PAIR + x, 1), t:t + 1].rearrange("p o t -> p (o t)")
                    dve.wait_ge(y_done, k * NY + u * CT + j + 1)
                    dve.scalar_tensor_tensor(out=H[:, t], in0=Y_bank[j][:], scalar=w, in1=H[:, t], op0=ALU.mult, op1=ALU.add).then_inc(added, 1)

            def select():
                by_e = lambda x: x[:].unsqueeze(3).to_broadcast([P, TILES, E, E])
                by_f = lambda x: x[:].unsqueeze(2).to_broadcast([P, TILES, E, E])
                dve.wait_ge(grown, 1)
                dve.tensor_scalar(grow[:], grow[:], 1.0, None, ALU.add).then_inc(sel, 1)
                dve.wait_ge(sel, 1)
                dve.reciprocal(sig[:], grow[:]).then_inc(sel, 1)
                dve.wait_ge(sel, 2)
                dve.tensor_tensor(score[:], sig[:], rbias[:].unsqueeze(1).to_broadcast([P, TILES, E]), ALU.add).then_inc(sel, 1)
                dve.wait_ge(sel, 3)
                dve.tensor_tensor(above[:], by_f(score), by_e(score), ALU.is_gt).then_inc(sel, 1)
                dve.tensor_tensor(equal[:], by_f(score), by_e(score), ALU.is_equal).then_inc(sel, 1)
                dve.wait_ge(sel, 5)
                eq = equal[:].rearrange("p t e f -> p t (e f)")
                first = before[:].rearrange("p e f -> p (e f)").unsqueeze(1).to_broadcast([P, TILES, E * E])
                dve.tensor_tensor(eq, eq, first, ALU.mult).then_inc(sel, 1)
                dve.wait_ge(sel, 6)
                dve.tensor_tensor(above[:], above[:], equal[:], ALU.add).then_inc(sel, 1)
                dve.wait_ge(sel, 7)
                dve.reduce_sum(rank[:], above[:], AX_X).then_inc(sel, 1)
                dve.wait_ge(sel, 8)
                dve.scalar_tensor_tensor(out=chosen[:], in0=rank[:], scalar=TOPK - 0.5, in1=sig[:], op0=ALU.is_lt, op1=ALU.mult).then_inc(sel, 1)
                dve.wait_ge(sel, 9)
                dve.reduce_sum(total[:], chosen[:], AX_X).then_inc(sel, 1)
                dve.wait_ge(sel, 10)
                dve.reciprocal(total[:], total[:]).then_inc(sel, 1)
                dve.wait_ge(sel, 11)
                dve.tensor_tensor(comb[:].rearrange("p e t -> p t e"), chosen[:], total[:].unsqueeze(2).to_broadcast([P, TILES, E]), ALU.mult)\
                   .then_inc(sel, 1)

            select()
            dve.wait_ge(sel, 12)
            with dve.Fori(0, E // PAIR) as k:
                for u in range(U + 1):
                    if u < U:
                        for i in range(IT):
                            dve.wait_ge(a_lo, k * (U * IT) + older(u * IT + i))
                            dve.wait_ge(u_done, k * (U * IT) + u * IT + i + 1)
                            dve.wait_ge(gated, k * (U * IT) + u * IT + i + 1)
                            dve.tensor_tensor(hidden[i][:], U_bank[i][:], gate[i][:], ALU.mult).then_inc(acted, 1)
                    if u >= 1:
                        accumulate(k, u - 1)

        @block.tensor
        def _(pe):
            def gate_up(k, u):
                x, c = u // CHUNKS, u % CHUNKS
                w = bass.ts(c, 512)
                if c == 0:
                    pe.wait_ge(w_lo, k * (2 * PAIR) + 2 * x + 2)
                for i in range(IT):
                    for n, (bank, done, free) in enumerate(((G_bank, g_done, gated), (U_bank, u_done, acted))):
                        pe.wait_ge(free, k * (U * IT) + older(u * IT + i))
                        ic = slice(n * I + i * P, n * I + (i + 1) * P)
                        for t in range(DT):
                            mm = product(pe, bank[i][:], (W_h[x][:, t, ic], W_l[x][:, t, ic]), (T_h[:, t, w], T_l[:, t, w]),
                                         t == 0, t == DT - 1)
                        mm.then_inc(done, 1)

            def down(k, u):
                x = u // CHUNKS
                pe.wait_ge(a_lo, k * (U * IT) + u * IT + IT)
                for j in range(CT):
                    pe.wait_ge(added, k * NY + max(u * CT + j + 1 - CT, 0))
                    for i in range(IT):
                        mm = product(pe, Y_bank[j][:], (A_h[u % 2][:, i, bass.ts(j, P)], A_l[u % 2][:, i, bass.ts(j, P)]),
                                     (Wd_h[x][:, i], Wd_l[x][:, i]), i == 0, i == IT - 1)
                    mm.then_inc(y_done, 1)

            with pe.Fori(0, E // PAIR) as k:
                for u in range(U + 1):
                    if u < U:
                        gate_up(k, u)
                    if u >= 1:
                        down(k, u - 1)


def bass_lm_tower(nc, ids, tok_w, attn_w, attn_b, attn_wo, ln1, ln2, blk_w, blk_norm, blk_wo, router, rbias, wg, wu, wd,
                  pos, iota, ident_d, mask_d, cos32, sin32, cos64, sin64, before, out):
    h_dram = nc.dram_tensor("h_saved", [P, TILES, D], F32, kind="Internal").ap()
    q_dram = nc.dram_tensor("q_rows", [16, SEQ, 512], F32, kind="Internal").ap()
    k_dram = nc.dram_tensor("k_rows", [16, SEQ, 128], F32, kind="Internal").ap()
    v_dram = nc.dram_tensor("v_rows", [16, SEQ, 128], F32, kind="Internal").ap()
    with ExitStack() as ctx:
        H = ctx.enter_context(nc.sbuf_tensor("H", [P, TILES, D], F32))
        ident = ctx.enter_context(nc.sbuf_tensor("ident", [P, P], F32))
        mask = ctx.enter_context(nc.sbuf_tensor("mask", [P, SEQ], F32))
        const_ready = ctx.enter_context(nc.semaphore("const_ready"))
        waited = ctx.enter_context(nc.semaphore("waited"))
        with nc.Block() as block:
            @block.sync
            def _(sp):
                sp.dma_start(ident[:], ident_d).then_inc(const_ready, 16)
                sp.dma_start(mask[:], mask_d).then_inc(const_ready, 16)
        const = ident, mask, const_ready, waited
        ahead_ctx = ctx.enter_context(ExitStack())
        ahead = WeightsAhead(nc, ahead_ctx)
        token_stage(nc, H, const, ahead, tok_w, attn_w, ids, pos, iota)
        with (nc.sbuf_tensor("Q_jobs", [P, BATCH * 2, QT, 256], F32) as Q_jobs,
              nc.sbuf_tensor("K_jobs", [P, BATCH * 2, QT, 32], F32) as K_jobs,
              nc.sbuf_tensor("V_jobs", [P, BATCH * 2, QT, 32], F32) as V_jobs):
            attn_project(nc, H, const, ahead, Q_jobs, K_jobs, V_jobs, attn_b, cos32, sin32)
            attn_attend(nc, H, const, ahead, Q_jobs, K_jobs, V_jobs, attn_wo, blk_w)
        jobs = JobsAhead(nc, ahead_ctx, ahead)
        block_project(nc, H, const, ahead, jobs, h_dram, q_dram, k_dram, v_dram, blk_w, blk_wo, ln1, blk_norm, cos64, sin64)
        block_attend(nc, H, const, jobs, q_dram, k_dram, v_dram, blk_wo)
        ahead_ctx.close()
        with (nc.sbuf_tensor("T_h", [P, DT, TILES * P], F32R) as T_h, nc.sbuf_tensor("T_l", [P, DT, TILES * P], F32R) as T_l,
              ExitStack() as moe_ctx):
            weights, routing = ExpertWeights(nc, moe_ctx), Routing(nc, moe_ctx)
            route(nc, H, const, weights, routing, h_dram, T_h, T_l, wg, wu, wd, ln2, router, rbias, before)
            experts(nc, H, weights, routing, T_h, T_l, out, wg, wu, wd)


def tables():
    f = np.float32
    half = np.arange(0, D, 2, dtype=f)
    div = np.exp(-(np.log(f(10000.0)) / f(D)) * half).astype(f)
    ang = np.arange(SEQ, dtype=f)[:, None] * div
    pos = np.zeros((SEQ, D), f)
    pos[:, 0::2], pos[:, 1::2] = np.sin(ang), np.cos(ang)
    mask = np.zeros((P, SEQ), f)
    mask[:, SEQ - P:] = np.where(np.arange(P)[None, :] > np.arange(P)[:, None], f(MASKED), f(0))

    def angles(dim, theta):
        i = np.arange(dim // 2, dtype=f)
        if theta == 1e4:
            inv = f(theta) ** (-i / f(dim // 2))
        else:
            inv = f(1) / f(theta) ** (np.arange(0, dim, 2, dtype=f) / f(dim))
        a = np.arange(SEQ, dtype=f)[:, None] * inv.astype(f)[None]
        c, s = np.cos(a), np.sin(a)
        return np.concatenate([c, c], 1), np.concatenate([-s, s], 1)

    cos32, sin32 = angles(32, 1e4)
    cos64, sin64 = angles(64, 1e6)
    return {"cos32": cos32, "sin32": sin32, "cos64": cos64, "sin64": sin64, "pos": pos,
            "iota": np.tile(np.arange(D, dtype=f), (P, 1)), "ident": np.eye(P, dtype=f), "mask": mask,
            "before": (np.arange(EXPERTS)[None, :] < np.arange(EXPERTS)[:, None]).astype(f)}


def kernel(**inputs):
    import concourse.bacc as _bacc
    from concourse.bass_utils import run_bass_kernel_spmd as _run

    x = {k: np.asarray(v) for k, v in inputs.items()}
    c = tables()
    cat, flat = np.concatenate, np.ascontiguousarray
    arrays = {
        "ids": flat(x["x"].reshape(TILES, P).T),
        "tok_w": cat([x["L0_tok_Wq"], x["L0_tok_Wk"]], 2),
        "attn_w": flat(cat([x["L0_attn_wq"], x["L0_attn_wk"], x["L0_attn_wv"]], 0).T),
        "attn_b": cat([x["L0_attn_bq"], x["L0_attn_bk"], x["L0_attn_bv"]]),
        "attn_wo": flat(x["L0_attn_wo"].T),
        "ln1": x["L0_ffn_ln1_w"],
        "ln2": x["L0_ffn_ln2_w"],
        "blk_w": cat([x["L0_ffn_wq"], x["L0_ffn_wk"], x["L0_ffn_wv"]], 1),
        "blk_norm": cat([x["L0_ffn_qnorm_w"], x["L0_ffn_knorm_w"]]),
        "blk_wo": x["L0_ffn_wo"],
        "router": x["L0_ffn_router_w"],
        "rbias": x["L0_ffn_router_bias"],
        "wg": x["L0_ffn_wg"],
        "wu": x["L0_ffn_wu"],
        "wd": x["L0_ffn_wd"],
    }
    arrays |= {k: c[k] for k in ("pos", "iota", "ident", "mask", "cos32", "sin32", "cos64", "sin64", "before")}
    nc = _bacc.Bacc("TRN2", target_bir_lowering=False, num_devices=1)
    args = [nc.dram_tensor(f"in_{k}", a.shape, mybir.dt.from_np(a.dtype), kind="ExternalInput").ap() for k, a in arrays.items()]
    out = nc.dram_tensor("out", [TILES * P, D], F32, kind="ExternalOutput").ap()
    bass_lm_tower(nc, *args, out)
    r = _run(nc, [{f"in_{k}": a for k, a in arrays.items()}], core_ids=[0])
    return r.results[0]["out"].reshape(BATCH, SEQ, D)
```
